# Optimizing a Trainium2 kernel written in Bass

```python
import numpy as np
import jax
import jax.numpy as jnp

def _softmax(x, axis=-1):
    return jax.nn.softmax(x, axis=axis)

def _gelu(x):
    return jax.nn.gelu(x, approximate=True)

def _silu(x):
    return jax.nn.silu(x)

def _sigmoid(x):
    return jax.nn.sigmoid(x)

def _layernorm(x, axis=-1, eps=1e-05):
    m = jnp.mean(x, axis=axis, keepdims=True)
    v = jnp.var(x, axis=axis, keepdims=True)
    return (x - m) / jnp.sqrt(v + eps)

def _scatter_add(tgt, idx, src, axis=0):
    return tgt.at[idx].add(src)

def _segment_sum(src, seg, n):
    return jax.ops.segment_sum(src, seg, n)
kernel_name = 'mk_gnn_resnorm_d4_gnn_r64_2ee74b'

def setup_inputs(seed: int=0):
    np.random.seed(seed)
    _w = jnp.asarray

    def _rec_inputs():
        import jax
        import jax.numpy as jnp
        _gk = jax.random.key(seed)
        x = -0.0001006 + 1 * jax.random.normal(jax.random.fold_in(_gk, 1), (50000, 96), jnp.float32)
        src = jax.random.randint(jax.random.fold_in(_gk, 2), (25000,), 0, 50000, jnp.int32)
        dst = jnp.minimum((50000 * jax.random.uniform(jax.random.fold_in(_gk, 3), (25000,)) ** 2.0).astype(jnp.int32), 49999)
        _o = jnp.argsort(dst, stable=True)
        src = src[_o]
        dst = dst[_o]
        edge_attr_96 = 5.93493e-05 + 1.00006 * jax.random.normal(jax.random.fold_in(_gk, 12), (25000, 96), jnp.float32)
        edge_weight = jax.random.uniform(jax.random.fold_in(_gk, 14), (25000,), jnp.float32, 0.0, 0.999998)
        return (x, src, dst, edge_attr_96, edge_weight)
    x, src, dst, edge_attr_96, edge_weight = _rec_inputs()

    def _L0_gnn_setup():
        import jax, jax.numpy as jnp
        import numpy as np
        N_NODES = 50000
        N_EDGES = 12500
        IN_DIM = 96
        NUM_HEADS = 8
        HEAD_DIM = IN_DIM // NUM_HEADS
        key = jax.random.key(seed)
        ks = jax.random.split(key, 11)
        s = 1.0 / np.sqrt(IN_DIM)
        return {'x': jax.random.normal(ks[0], (N_NODES, IN_DIM), dtype=jnp.float32), 'edge_index': jax.random.randint(ks[1], (2, N_EDGES), 0, N_NODES, dtype=jnp.int64), 'edge_attr': jax.random.normal(ks[2], (N_EDGES, IN_DIM), dtype=jnp.float32), 'Wq': jax.random.normal(ks[3], (IN_DIM, IN_DIM), dtype=jnp.float32) * s, 'bq': jax.random.normal(ks[4], (IN_DIM,), dtype=jnp.float32) * s, 'Wk': jax.random.normal(ks[5], (IN_DIM, IN_DIM), dtype=jnp.float32) * s, 'bk': jax.random.normal(ks[6], (IN_DIM,), dtype=jnp.float32) * s, 'We': jax.random.normal(ks[7], (IN_DIM, IN_DIM), dtype=jnp.float32) * s, 'be': jax.random.normal(ks[8], (IN_DIM,), dtype=jnp.float32) * s, 'Wv': jax.random.normal(ks[9], (IN_DIM, IN_DIM), dtype=jnp.float32) * s, 'bv': jax.random.normal(ks[10], (IN_DIM,), dtype=jnp.float32) * s}
    _L0_gnn_all = _L0_gnn_setup()
    _L0_gnn_in = {k: v for k, v in _L0_gnn_all.items() if k in ('Wq', 'bq', 'Wk', 'bk', 'We', 'be', 'Wv', 'bv')}
    del _L0_gnn_all

    def _L1_gnn_setup():
        import jax, jax.numpy as jnp
        import numpy as np
        K = 16
        ALPHA = 0.1
        key = jax.random.key(seed)
        k1, k2 = jax.random.split(key)
        N, E, D = (50000, 12500, 96)
        x = jax.random.normal(k1, (N, D), dtype=jnp.float32)
        edge_index = jax.random.randint(k2, (2, E), 0, N, dtype=jnp.int64)
        return {'x': x, 'edge_index': edge_index}
    _L1_gnn_all = _L1_gnn_setup()
    _L1_gnn_in = {k: v for k, v in _L1_gnn_all.items() if k in ()}
    del _L1_gnn_all

    def _L2_gnn_setup():
        import jax, jax.numpy as jnp
        import numpy as np
        N_NODES = 50000
        N_EDGES = 12500
        D = 96

        def _gcn_conv(x, src, dst, ew, W, b):
            n = x.shape[0]
            loop = jnp.arange(n)
            src_a = jnp.concatenate([src, loop])
            dst_a = jnp.concatenate([dst, loop])
            w_a = jnp.concatenate([ew, jnp.ones((n,), ew.dtype)])
            deg = jax.ops.segment_sum(w_a, dst_a, num_segments=n)
            dis = jnp.where(deg > 0, jax.lax.rsqrt(deg), jnp.zeros_like(deg))
            norm = dis[src_a] * w_a * dis[dst_a]
            h = x @ W
            msg = h[src_a] * norm[:, None]
            out = jax.ops.segment_sum(msg, dst_a, num_segments=n)
            return out + b
        key = jax.random.key(seed)
        ks = jax.random.split(key, 10)
        x = jax.random.normal(ks[0], (N_NODES, D), dtype=jnp.float32)
        edge_index = jax.random.randint(ks[1], (2, N_EDGES), 0, N_NODES, dtype=jnp.int64)
        edge_weight = jax.random.uniform(ks[2], (N_EDGES,), dtype=jnp.float32)
        s = 1.0 / np.sqrt(D)
        W1 = jax.random.uniform(ks[3], (D, D), jnp.float32, -s, s)
        b1 = jnp.zeros((D,), jnp.float32)
        W2 = jax.random.uniform(ks[4], (D, D), jnp.float32, -s, s)
        b2 = jnp.zeros((D,), jnp.float32)
        W3 = jax.random.uniform(ks[5], (D, D), jnp.float32, -s, s)
        b3 = jnp.zeros((D,), jnp.float32)
        return {'x': x, 'edge_index': edge_index, 'edge_weight': edge_weight, 'W1': W1, 'b1': b1, 'W2': W2, 'b2': b2, 'W3': W3, 'b3': b3}
    _L2_gnn_all = _L2_gnn_setup()
    _L2_gnn_in = {k: v for k, v in _L2_gnn_all.items() if k in ('W1', 'b1', 'W2', 'b2', 'W3', 'b3')}
    del _L2_gnn_all

    def _L3_gnn_setup():
        import jax, jax.numpy as jnp
        import numpy as np
        N_NODES = 50000
        N_EDGES = 12500
        D_FEAT = 96
        D_OUT = 96
        key = jax.random.key(seed)
        ks = jax.random.split(key, 6)
        feat = jax.random.normal(ks[0], (N_NODES, D_FEAT), dtype=jnp.float32)
        affine = jax.random.uniform(ks[1], (N_EDGES,), dtype=jnp.float32)
        mlp_w = jax.random.normal(ks[2], (D_OUT, 2 * D_FEAT), dtype=jnp.float32) * (1.0 / np.sqrt(2 * D_FEAT))
        mlp_b = jax.random.normal(ks[3], (D_OUT,), dtype=jnp.float32) * 0.01
        src_idx = jax.random.randint(ks[4], (N_EDGES,), 0, N_NODES, dtype=jnp.int64)
        dst_idx = jax.random.randint(ks[5], (N_EDGES,), 0, N_NODES, dtype=jnp.int64)
        return {'feat': feat, 'affine': affine, 'mlp_w': mlp_w, 'mlp_b': mlp_b, 'src_idx': src_idx, 'dst_idx': dst_idx}
    _L3_gnn_all = _L3_gnn_setup()
    _L3_gnn_in = {k: v for k, v in _L3_gnn_all.items() if k in ('mlp_w', 'mlp_b')}
    del _L3_gnn_all
    return {'x': x, 'src': src, 'dst': dst, 'edge_attr_96': edge_attr_96, 'edge_weight': edge_weight, 'L0_gnn_Wq': _L0_gnn_in['Wq'], 'L0_gnn_bq': _L0_gnn_in['bq'], 'L0_gnn_Wk': _L0_gnn_in['Wk'], 'L0_gnn_bk': _L0_gnn_in['bk'], 'L0_gnn_We': _L0_gnn_in['We'], 'L0_gnn_be': _L0_gnn_in['be'], 'L0_gnn_Wv': _L0_gnn_in['Wv'], 'L0_gnn_bv': _L0_gnn_in['bv'], 'L2_gnn_W1': _L2_gnn_in['W1'], 'L2_gnn_b1': _L2_gnn_in['b1'], 'L2_gnn_W2': _L2_gnn_in['W2'], 'L2_gnn_b2': _L2_gnn_in['b2'], 'L2_gnn_W3': _L2_gnn_in['W3'], 'L2_gnn_b3': _L2_gnn_in['b3'], 'L3_gnn_mlp_w': _L3_gnn_in['mlp_w'], 'L3_gnn_mlp_b': _L3_gnn_in['mlp_b']}

def reference(x, src, dst, edge_attr_96, edge_weight, L0_gnn_Wq, L0_gnn_bq, L0_gnn_Wk, L0_gnn_bk, L0_gnn_We, L0_gnn_be, L0_gnn_Wv, L0_gnn_bv, L2_gnn_W1, L2_gnn_b1, L2_gnn_W2, L2_gnn_b2, L2_gnn_W3, L2_gnn_b3, L3_gnn_mlp_w, L3_gnn_mlp_b):
    import jax
    import jax.numpy as jnp

    def _L0_gnn_ref(x, edge_index, edge_attr, Wq, bq, Wk, bk, We, be, Wv, bv):
        import jax, jax.numpy as jnp
        import numpy as np
        N_NODES = 50000
        N_EDGES = 12500
        IN_DIM = 96
        NUM_HEADS = 8
        HEAD_DIM = IN_DIM // NUM_HEADS
        N = x.shape[0]
        H, D = (NUM_HEADS, HEAD_DIM)
        Q_h = (x @ Wq + bq).reshape(N, H, D)
        K_h = (x @ Wk + bk).reshape(N, H, D)
        V_h = (x @ Wv + bv).reshape(N, H, D)
        E = (edge_attr @ We + be).reshape(-1, H, D)
        src_idx = edge_index[0]
        dst_idx = edge_index[1]
        src = K_h[src_idx]
        dest = Q_h[dst_idx]
        score = src * dest / jnp.sqrt(jnp.asarray(D, x.dtype))
        score = score * E
        score = jnp.exp(jnp.clip(score.sum(-1, keepdims=True), -5.0, 5.0))
        msg = V_h[src_idx] * score
        wV = jax.ops.segment_sum(msg, dst_idx, num_segments=N)
        Z = jax.ops.segment_sum(score, dst_idx, num_segments=N)
        h_out = wV / (Z + 1e-06)
        return h_out.reshape(N, H * D)

    def _L1_gnn_ref(x, edge_index):
        import jax, jax.numpy as jnp
        import numpy as np
        K = 16
        ALPHA = 0.1
        N = x.shape[0]
        loop = jnp.arange(N, dtype=edge_index.dtype)
        row = jnp.concatenate([edge_index[0], loop])
        col = jnp.concatenate([edge_index[1], loop])
        deg = jax.ops.segment_sum(jnp.ones_like(col, dtype=x.dtype), col, num_segments=N)
        deg_inv_sqrt = jnp.where(deg > 0, jax.lax.rsqrt(jnp.maximum(deg, 1e-30)), 0.0)
        norm = (deg_inv_sqrt[row] * deg_inv_sqrt[col])[:, None]
        h = x
        for _ in range(K):
            h_neighbors = jax.ops.segment_sum(norm * h[row], col, num_segments=N)
            h = (1.0 - ALPHA) * h_neighbors + ALPHA * x
        return h

    def _L2_gnn_ref(x, edge_index, edge_weight, W1, b1, W2, b2, W3, b3):
        import jax, jax.numpy as jnp
        import numpy as np
        N_NODES = 50000
        N_EDGES = 12500
        D = 96

        def _gcn_conv(x, src, dst, ew, W, b):
            n = x.shape[0]
            loop = jnp.arange(n)
            src_a = jnp.concatenate([src, loop])
            dst_a = jnp.concatenate([dst, loop])
            w_a = jnp.concatenate([ew, jnp.ones((n,), ew.dtype)])
            deg = jax.ops.segment_sum(w_a, dst_a, num_segments=n)
            dis = jnp.where(deg > 0, jax.lax.rsqrt(deg), jnp.zeros_like(deg))
            norm = dis[src_a] * w_a * dis[dst_a]
            h = x @ W
            msg = h[src_a] * norm[:, None]
            out = jax.ops.segment_sum(msg, dst_a, num_segments=n)
            return out + b
        src, dst = (edge_index[0], edge_index[1])
        h = _gcn_conv(x, src, dst, edge_weight, W1, b1)
        h = jax.nn.relu(h)
        h = _gcn_conv(h, src, dst, edge_weight, W2, b2)
        h = jax.nn.relu(h)
        h = _gcn_conv(h, src, dst, edge_weight, W3, b3)
        return h

    def _L3_gnn_ref(feat, affine, mlp_w, mlp_b, src_idx, dst_idx):
        import jax, jax.numpy as jnp
        import numpy as np
        N_NODES = 50000
        N_EDGES = 12500
        D_FEAT = 96
        D_OUT = 96
        msgs = feat[src_idx] * affine[:, None]
        agg = jax.ops.segment_sum(msgs, dst_idx, num_segments=feat.shape[0])
        gcn_feat = jnp.concatenate([feat, agg], axis=-1)
        out = gcn_feat @ mlp_w.T + mlp_b
        return out
    edge_index = jnp.stack([src, dst])
    x = _layernorm(x + _L0_gnn_ref(x, edge_index, edge_attr_96, L0_gnn_Wq, L0_gnn_bq, L0_gnn_Wk, L0_gnn_bk, L0_gnn_We, L0_gnn_be, L0_gnn_Wv, L0_gnn_bv), axis=-1)
    x = _layernorm(x + _L1_gnn_ref(x, edge_index), axis=-1)
    x = _layernorm(x + _L2_gnn_ref(x, edge_index, edge_weight, L2_gnn_W1, L2_gnn_b1, L2_gnn_W2, L2_gnn_b2, L2_gnn_W3, L2_gnn_b3), axis=-1)
    x = _layernorm(x + _L3_gnn_ref(x, edge_weight, L3_gnn_mlp_w, L3_gnn_mlp_b, src, dst), axis=-1)
    return x

_drawn_inputs = setup_inputs


def setup_inputs(seed=0):
    import zlib

    import numpy as np

    out = dict(_drawn_inputs(seed))
    spreads = {'L2_gnn_b1': (0.0, 0.548), 'L2_gnn_b2': (0.0, 0.1), 'L2_gnn_b3': (0.0, 0.1)}
    factors = {'L0_gnn_bq': 8.0, 'L0_gnn_bk': 8.0, 'L0_gnn_be': 7.684, 'L3_gnn_mlp_b': 7.507}
    for name, (base, spread) in spreads.items():
        noise = np.random.default_rng([zlib.crc32(name.encode()), seed]).standard_normal(out[name].shape)
        drawn = base * np.exp(spread * noise) if base else spread * noise
        out[name] = jnp.asarray(drawn.astype(out[name].dtype))
    for name, factor in factors.items():
        out[name] = (out[name] * factor).astype(out[name].dtype)
    return out
```

```python
from contextlib import ExitStack, contextmanager

import concourse.bass as bass
from concourse import mybir

F32 = mybir.dt.float32
I32 = mybir.dt.int32
ALU = mybir.AluOpType
ACT = mybir.ActivationFunctionType
AX_X = mybir.AxisListType.X

P = 128
D = 96
N = 50000
E = 25000
HEADS = 8
DH = D // HEADS
STEPS = 16
ALPHA = 0.1
EPS = 1e-5

RE = P - 1
CH = 5
R = 2 * CH
T = -(-E // (RE * R)) * R
NB = T // R
NS = T * P
NQ = 392
NN = P * NQ
LNW = 7
JW = 4
SKIP = 1 << 20
MSG = D + HEADS + 2


class Count:

    def __init__(self, sem, turn, per):
        self.sem, self.turn, self.per, self.n = sem, turn, per, 0

    def up(self, instruction):
        if hasattr(instruction, "then_inc"):
            instruction.then_inc(self.sem, 1)
        else:
            instruction.sem_inc(self.sem, 1)
        self.n += 1
        return instruction

    def now(self):
        return self.turn * self.per + self.n


@contextmanager
def semaphores(nc):
    taken = []

    def sem(name):
        taken.append(nc.alloc_semaphore(name))
        return taken[-1]

    yield sem
    nc.clear_and_free_semaphores(taken)
    nc.all_engine_barrier()


def ds(start, size):
    return bass.ds(start, size)


def per_head(ap):
    return ap.rearrange("p c (h d) -> p c h d", h=HEADS)


def every(ap):
    return ap.rearrange("p c (h o) -> p c h o", o=1).broadcast_to([P, CH, HEADS, DH])


def cols(ap):
    return ap.rearrange("p a d -> p (a d)")


def row_moments(dve, done, tiles, stats, mv):
    for j, tile in enumerate(tiles):
        done.up(dve.bn_stats(stats[:, j, :], tile))
    dve.wait_ge(done.sem, done.now())
    done.up(dve)
    for j in range(len(tiles)):
        done.up(dve.bn_aggr(mv[:, j, :], stats[:, j, :]))
    dve.wait_ge(done.sem, done.now())


def build_graph_kernel(nc, scratch, x, src_p, dst_k, dst_next, dst_i, w_p, ea_t, wkv, wq, we, w1, w2, w3, wa, wb, out):
    tab1 = scratch("tab1", [2 * NS + NN, D], F32)
    tab2, tab3, tab4, tab5 = (scratch(f"tab{k}", [NS + NN, D], F32) for k in (2, 3, 4, 5))
    slotmap = scratch("slotmap", [NN, 1], I32)
    sums = scratch("sums", [P, (T + R) * P], F32)

    def slot_rows(tab, base=0):
        return tab[base:base + NS, :].rearrange("(p t) d -> p t d", p=P)

    def node_rows(tab):
        return tab[NS:NS + NN, :].rearrange("(p q) d -> p q d", p=P)

    x_rows = x.rearrange("(p q) d -> p q d", p=P)
    out_rows = out.rearrange("(p q) d -> p q d", p=P)

    with ExitStack() as whole:
        def keep(name, shape, dt=F32):
            return whole.enter_context(nc.sbuf_tensor(name, shape, dt))

        state = keep("state", [P, T, D])
        fixed = keep("fixed", [P, T, D])
        ident = keep("ident", [P, P])
        ptr_a = keep("ptr_a", [P, T], I32)
        ptr_b = keep("ptr_b", [P, T], I32)
        src_s = keep("src_s", [P, T], I32)
        dst_s = keep("dst_s", [P, T], I32)
        scat = keep("scat", [P, T], I32)
        w_s = keep("w_s", [P, T])
        cnt = keep("cnt", [P, T])
        wsum = keep("wsum", [P, T])
        canon = keep("canon", [P, T])
        step_a = keep("step_a", [P, T])
        dis_w = keep("dis_w", [P, T])
        dis_c = keep("dis_c", [P, T])

        with ExitStack() as c:
            sem = c.enter_context(semaphores(nc))
            key_k = c.enter_context(nc.sbuf_tensor("key_k", [P, T + R], I32))
            key_f = c.enter_context(nc.sbuf_tensor("key_f", [P, T + R], F32))
            nxt = c.enter_context(nc.sbuf_tensor("nxt", [P, T], I32))
            nxt_f = c.enter_context(nc.sbuf_tensor("nxt_f", [P, T], F32))
            same = c.enter_context(nc.sbuf_tensor("same", [P, T], F32))
            slot_id = c.enter_context(nc.sbuf_tensor("slot_id", [P, T], I32))
            node_id = c.enter_context(nc.sbuf_tensor("node_id", [P, NQ], I32))
            loaded, made, map_set = sem("loaded"), sem("made"), sem("map_set")
            id_set = sem("id_set")
            vec = sem("index_steps")
            with nc.Block() as block:
                @block.sync
                def _(sp):
                    for to, frm in ((key_k, dst_k), (nxt, dst_next), (src_s, src_p), (w_s, w_p)):
                        sp.dma_start(to[:], frm).then_inc(loaded, 16)
                    sp.wait_ge(made, 2)
                    sp.dma_start(slotmap.rearrange("(p q) o -> p (q o)", p=P), node_id[:]).then_inc(map_set, 16)
                    sp.wait_ge(map_set, 16)

                @block.gpsimd
                def _(pool):
                    pool.iota(slot_id[:], [[1, T]], base=0, channel_multiplier=T).then_inc(made, 1)
                    pool.iota(node_id[:], [[1, NQ]], base=NS, channel_multiplier=NQ).then_inc(made, 1)
                    pool.memset(ident[:], 0.0).then_inc(id_set, 1)
                    pool.wait_ge(id_set, 1)
                    pool.affine_select(out=ident[:], in_=ident[:], compare_op=ALU.not_equal, fill=1.0, base=0,
                                       pattern=[[-1, P]], channel_multiplier=1).then_inc(id_set, 1)

                @block.vector
                def _(dve):
                    done = Count(vec, 0, 0)
                    dve.wait_ge(loaded, 64)
                    done.up(nc.vector.tensor_copy(key_f[:], key_k[:]))
                    done.up(nc.vector.tensor_copy(nxt_f[:], nxt[:]))
                    dve.wait_ge(vec, done.now())
                    done.up(nc.vector.tensor_tensor(same[:], key_f[:, 0:T], nxt_f[:], ALU.is_equal))
                    done.up(nc.vector.tensor_scalar(dst_s[:], key_f[:, 0:T], float(N - 1), 0.0, ALU.min, ALU.max))
                    dve.wait_ge(vec, done.now())
                    done.up(nc.vector.tensor_scalar(canon[:], same[:], -1.0, 1.0, ALU.mult, ALU.add))
                    done.up(nc.vector.scalar_tensor_tensor(out=scat[:], in0=same[:], scalar=float(SKIP),
                                                           in1=key_f[:, 0:T], op0=ALU.mult, op1=ALU.add))

            keys = c.enter_context(nc.sbuf_tensor("keys", [P, 2, CH * P], I32))
            s_new = c.enter_context(nc.sbuf_tensor("s_new", [P, 2, CH * P], F32))
            xin = c.enter_context(nc.sbuf_tensor("xin", [P, 2, LNW, D], F32))
            xout = c.enter_context(nc.sbuf_tensor("xout", [P, 2, LNW, D], F32))
            stats = c.enter_context(nc.sbuf_tensor("stats", [P, LNW, 6], F32))
            mv = c.enter_context(nc.sbuf_tensor("mv", [P, 2, LNW, 2], F32))
            var = c.enter_context(nc.sbuf_tensor("var", [P, 2, LNW], F32))
            rstd = c.enter_context(nc.sbuf_tensor("rstd", [P, 2, LNW], F32))
            idx = c.enter_context(nc.sbuf_tensor("idx", [P, 2, CH], I32))
            val = c.enter_context(nc.sbuf_tensor("val", [P, 2, CH], I32))
            keys_in = [sem(f"keys_in{h}") for h in range(2)]
            s_out = [sem(f"s_out{h}") for h in range(2)]
            s_made = sem("s_made")
            x_in = [sem(f"x_in{h}") for h in range(2)]
            x_out = [sem(f"x_out{h}") for h in range(2)]
            ln_done, ln_steps, var_ready, rstd_ready = sem("ln_done"), sem("ln_steps"), sem("var_ready"), sem("rstd_ready")
            staged, go = sem("staged"), sem("go")
            map_done = [sem(f"map_done{h}") for h in range(2)]
            ptr_in = [sem(f"ptr_in{h}") for h in range(2)]
            ptr_kept, ptr_ready = sem("ptr_kept"), sem("ptr_ready")
            NCH = (T + R) // CH
            NJ = NQ // LNW
            with nc.Block() as block:
                @block.sync
                def _(sp):
                    def load_keys(c_, h):
                        part = dst_i[ds(c_ * (CH * P), CH * P)].rearrange("(o n) -> o n", o=1)
                        sp.dma_start(keys[:, h, :], part.broadcast_to([P, CH * P])).then_inc(keys_in[h], 16)

                    for h in range(2):
                        load_keys(h, h)
                        sp.dma_start(xin[:, h], x_rows[:, h * LNW:(h + 1) * LNW, :]).then_inc(x_in[h], 16)
                    with sp.Fori(0, NCH // 2 - 1) as b:
                        for h in range(2):
                            sp.wait_ge(s_made, 2 * b + h + 1)
                            load_keys(2 * b + 2 + h, h)
                            sp.dma_start(sums[:, ds((2 * b + h) * (CH * P), CH * P)], s_new[:, h, :]).then_inc(s_out[h], 16)
                    for h in range(2):
                        sp.wait_ge(s_made, NCH - 1 + h)
                        sp.dma_start(sums[:, (NCH - 2 + h) * CH * P:(NCH - 1 + h) * CH * P], s_new[:, h, :]).then_inc(s_out[h], 16)
                    with sp.Fori(0, NJ // 2 - 1) as b:
                        for h in range(2):
                            sp.wait_ge(ln_done, 2 * b + h + 1)
                            sp.dma_start(xin[:, h], x_rows[:, ds((2 * b + 2 + h) * LNW, LNW), :]).then_inc(x_in[h], 16)
                            sp.dma_start(node_rows(tab1)[:, ds((2 * b + h) * LNW, LNW), :], xout[:, h]).then_inc(x_out[h], 16)
                    for h in range(2):
                        sp.wait_ge(ln_done, NJ - 1 + h)
                        sp.dma_start(node_rows(tab1)[:, (NJ - 2 + h) * LNW:(NJ - 1 + h) * LNW, :], xout[:, h]).then_inc(x_out[h], 16)
                    for h in range(2):
                        sp.wait_ge(s_out[h], 16 * (NCH // 2))
                        sp.wait_ge(x_out[h], 16 * (NJ // 2))

                @block.scalar
                def _(act):
                    with act.Fori(0, NJ // 2) as b:
                        for h in range(2):
                            act.wait_ge(var_ready, 2 * b + h + 1)
                            nc.scalar.activation(rstd[:, h, :], var[:, h, :], ACT.Sqrt).then_inc(rstd_ready, 1)

                @block.vector
                def _(dve):
                    with dve.Fori(0, NCH // 2) as b:
                        for h in range(2):
                            dve.wait_ge(keys_in[h], b * 16 + 16)
                            dve.wait_ge(s_out[h], b * 16)
                            for j in range(CH):
                                k = nc.vector.tensor_scalar(s_new[:, h, j * P:(j + 1) * P], keys[:, h, j * P:(j + 1) * P],
                                                            key_f[:, ds(b * R + h * CH + j, 1)], None, ALU.is_equal)
                            k.then_inc(s_made, 1)
                    with dve.Fori(0, NJ // 2) as b:
                        done = Count(ln_steps, b, 2 * (2 * LNW + 2))
                        for h in range(2):
                            dve.wait_ge(x_in[h], b * 16 + 16)
                            row_moments(dve, done, [xin[:, h, j, :] for j in range(LNW)], stats, mv[:, h])
                            done.up(nc.vector.tensor_scalar(var[:, h, :], mv[:, h, :, 1], EPS, None, ALU.add))
                            dve.wait_ge(ln_steps, done.now())
                            nc.vector.reciprocal(var[:, h, :], var[:, h, :]).then_inc(var_ready, 1)
                        for h in range(2):
                            dve.wait_ge(x_out[h], b * 16)
                            dve.wait_ge(rstd_ready, 2 * b + h + 1)
                            for j in range(LNW):
                                k = nc.vector.tensor_scalar(xout[:, h, j, :], xin[:, h, j, :], mv[:, h, j, 0:1], rstd[:, h, j:j + 1],
                                                            ALU.subtract, ALU.mult)
                            k.then_inc(ln_done, 1)
                    dve.wait_ge(ptr_kept, 2 * NB)
                    nc.vector.tensor_copy(nxt_f[:], ptr_a[:]).then_inc(ptr_ready, 1)
                    dve.wait_ge(ptr_ready, 1)
                    nc.vector.tensor_scalar(same[:], nxt_f[:], float(NS), float(NS + NN), ALU.is_lt, ALU.mult).then_inc(ptr_ready, 1)
                    dve.wait_ge(ptr_ready, 2)
                    nc.vector.tensor_tensor(ptr_b[:], nxt_f[:], same[:], ALU.add).then_inc(ptr_ready, 1)

                @block.gpsimd
                def _(pool):
                    with pool.Fori(0, NB) as b:
                        for h in range(2):
                            pool.wait_ge(map_done[h], b * (16 * CH))
                            nc.gpsimd.tensor_copy(idx[:, h, :], scat[:, ds(b * R + h * CH, CH)]).then_inc(staged, 1)
                            nc.gpsimd.tensor_copy(val[:, h, :], slot_id[:, ds(b * R + h * CH, CH)]).then_inc(staged, 1)
                            pool.wait_ge(staged, b * 4 + 2 * h + 2)
                            pool.sem_inc(go, 1)
                            for j in range(CH):
                                nc.gpsimd.indirect_dma_start(slotmap, bass.IndirectOffsetOnAxis(ap=idx[:, h, j:j + 1], axis=0),
                                                             val[:, h, j:j + 1], None, bounds_check=N - 1,
                                                             oob_is_err=False).then_inc(map_done[h], 16)
                    for h in range(2):
                        pool.wait_ge(map_done[h], 16 * CH * NB)
                    with pool.Fori(0, NB) as b:
                        for h in range(2):
                            nc.gpsimd.tensor_copy(idx[:, h, :], src_s[:, ds(b * R + h * CH, CH)]).then_inc(staged, 1)
                            pool.wait_ge(staged, b * 2 + (4 * NB + h + 1))
                            pool.sem_inc(go, 1)
                            for j in range(CH):
                                nc.gpsimd.indirect_dma_start(val[:, h, j:j + 1], None, slotmap,
                                                             bass.IndirectOffsetOnAxis(ap=idx[:, h, j:j + 1], axis=0)).then_inc(ptr_in[h], 16)
                        for h in range(2):
                            pool.wait_ge(ptr_in[h], b * (16 * CH) + 16 * CH)
                            nc.gpsimd.tensor_copy(ptr_a[:, ds(b * R + h * CH, CH)], val[:, h, :]).then_inc(ptr_kept, 1)
                        pool.wait_ge(ptr_kept, b * 2 + 2)

        edge_attention(nc, state, fixed, ident, src_s, dst_s, w_s, cnt, wsum, x, ea_t, wkv, wq, we, sums, slot_rows(tab1))
        degrees(nc, cnt, wsum, step_a, dis_w)
        appnp(nc, state, fixed, ident, ptr_a, ptr_b, step_a, sums, tab1, slot_rows)
        isolated_nodes(nc, ident, w1, w2, w3, wa, (tab1, tab2, tab3, tab4, tab5), node_rows, out_rows)
        second_norm(nc, state, fixed, cnt, dis_w, dis_c, canon, slot_rows(tab2))
        layers = ((w1, tab2, tab3), (w2, tab3, tab4), (w3, tab4, tab5))
        for n, (w, tab, nxt_tab) in enumerate(layers):
            convolution(nc, n + 2, state, fixed, ident, ptr_a, w_s, dis_w, dis_c, scat, w, None, tab, sums,
                        slot_rows(nxt_tab), out)
        convolution(nc, 5, state, fixed, ident, ptr_a, w_s, dis_w, dis_c, scat, wb, wa, tab5, sums, None, out)


def edge_attention(nc, state, fixed, ident, src_s, dst_s, w_s, cnt, wsum, x, ea_t, wkv, wq, we, sums, tab_slots):
    with ExitStack() as c:
        sem = c.enter_context(semaphores(nc))
        def sb(name, shape, dt=F32):
            return c.enter_context(nc.sbuf_tensor(name, shape, dt))

        wkv_s, wq_s, we_s = sb("wkv_s", [D + 1, 2 * D]), sb("wq_s", [D + 1, D]), sb("we_s", [D + 1, D])
        idx = sb("idx_l0", [P, 2, 2, CH], I32)
        xs = sb("xs", [P, R, D])
        xd = sb("xd", [P, R, D])
        ea = sb("ea", [D + 1, 2, CH * P])
        s_in = sb("s_l0", [P, 2, CH * P])
        xt = sb("xt", [D + 1, 2, 2 * P])
        kvqe = sb("kvqe", [P, CH, 4 * D])
        prod = sb("prod", [P, CH, D])
        score = sb("score", [P, CH, HEADS])
        msg = sb("msg", [P, 2, CH, MSG])
        agg = sb("agg", [P, CH, MSG])
        zinv = sb("zinv", [P, CH, HEADS])
        deg = sb("deg", [P, CH])
        var = sb("var_l0", [P, CH])
        stats = sb("stats_l0", [P, CH, 6])
        mv = sb("mv_l0", [P, CH, 2])
        rstd = sb("rstd_l0", [P, CH])
        ps_t = [c.enter_context(nc.psum_tensor(f"ps_t{k}", [P, 512], F32)) for k in range(2)]
        ps_p = [c.enter_context(nc.psum_tensor(f"ps_p{k}", [P, 512], F32)) for k in range(2)]
        ps_s = [c.enter_context(nc.psum_tensor(f"ps_s{k}", [P, 512], F32)) for k in range(2)]
        ps_c = [c.enter_context(nc.psum_tensor(f"ps_c{k}", [P, 512], F32)) for k in range(2)]

        const_in = sem("const_in")
        rows_in = [sem(f"l0_rows_in{i}") for i in range(R)]
        ea_in = [sem(f"l0_ea_in{h}") for h in range(2)]
        sm_in = [sem(f"l0_s_in{h}") for h in range(2)]
        staged, go = sem("l0_staged"), sem("l0_go")
        turned, turned_kept = sem("l0_turned"), sem("l0_turned_kept")
        projected, projected_kept = sem("l0_projected"), sem("l0_projected_kept")
        scored, exped, msg_ready = sem("l0_scored"), sem("l0_exped"), sem("l0_msg_ready")
        carry_out, carry_kept = sem("l0_carry_out"), sem("l0_carry_kept")
        summed, sum_kept = sem("l0_summed"), sem("l0_sum_kept")
        posted, written = sem("l0_posted"), sem("l0_written")
        steps, var_ready, rstd_ready = sem("l0_steps"), sem("l0_var_ready"), sem("l0_rstd_ready")
        NCH = 2 * NB

        with nc.Block() as block:
            @block.sync
            def _(sp):
                for to, frm in ((wkv_s, wkv), (wq_s, wq), (we_s, we)):
                    sp.dma_start(to[:], frm).then_inc(const_in, 16)
                sp.wait_ge(const_in, 48)

            @block.vector
            def _(dve):
                nc.vector.memset(xt[D:D + 1, :, :], 1.0)
                nc.vector.memset(ea[D:D + 1, :, :], 1.0)
                nc.vector.memset(ps_c[1][0:1, :], 0.0)

        with nc.Block() as block:
            @block.sync
            def _(sp):
                def load(cc, h):
                    sp.dma_start(ea[0:D, h, :], ea_t[:, ds(cc * (CH * P), CH * P)]).then_inc(ea_in[h], 16)
                    sp.dma_start(s_in[:, h, :], sums[:, ds(cc * (CH * P), CH * P)]).then_inc(sm_in[h], 16)

                for h in range(2):
                    load(h, h)

                def turn(b, last):
                    for h in range(2):
                        if not last:
                            sp.wait_ge(summed, b * R + (h + 1) * CH)
                            load(2 * b + 2 + h, h)
                        sp.wait_ge(posted, 2 * b + h + 1)
                        sp.dma_start(tab_slots[:, ds(b * R + h * CH, CH), :], state[:, ds(b * R + h * CH, CH), :]).then_inc(written, 16)

                with sp.Fori(0, NB - 1) as b:
                    turn(b, False)
                turn(NB - 1, True)
                sp.wait_ge(written, 16 * NCH)

            @block.gpsimd
            def _(pool):
                def turn(b, first):
                    for h in range(2):
                        if not first:
                            pool.wait_ge(posted, 2 * b + (h - 1))
                        for k, of in enumerate((src_s, dst_s)):
                            nc.gpsimd.tensor_copy(idx[:, h, k, :], of[:, ds(b * R + h * CH, CH)]).then_inc(staged, 1)
                        pool.wait_ge(staged, b * 4 + 2 * h + 2)
                        pool.sem_inc(go, 1)
                        for j in range(CH):
                            for k, to in enumerate((xs, xd)):
                                nc.gpsimd.indirect_dma_start(to[:, h * CH + j, :], None, x,
                                                             bass.IndirectOffsetOnAxis(ap=idx[:, h, k, j:j + 1], axis=0)).then_inc(rows_in[h * CH + j], 16)

                turn(0, True)
                with pool.Fori(1, NB) as b:
                    turn(b, False)

            def turn_rows(pe, b, i):
                pe.wait_ge(rows_in[i], b * 32 + 32)
                nc.tensor.transpose(ps_t[i % 2][0:D, 0:P], xs[:, i, :], ident[:])
                nc.tensor.transpose(ps_t[i % 2][0:D, P:2 * P], xd[:, i, :], ident[:]).then_inc(turned, 1)

            def project(pe, b, i):
                h, j, n = i // CH, i % CH, b * R + i
                pe.wait_ge(turned_kept, n + 1)
                if j == 0:
                    pe.wait_ge(ea_in[h], b * 16 + 16)
                if not isinstance(n, int) or n > 1:
                    pe.wait_ge(projected_kept, n - 1)
                to = ps_p[i % 2]
                nc.tensor.matmul(to[:, 0:2 * D], xt[:, i % 2, 0:P], wkv_s[:], start=True, stop=True)
                nc.tensor.matmul(to[:, 2 * D:3 * D], xt[:, i % 2, P:2 * P], wq_s[:], start=True, stop=True)
                nc.tensor.matmul(to[:, 3 * D:4 * D], ea[:, h, j * P:(j + 1) * P], we_s[:], start=True, stop=True).then_inc(projected, 1)

            def sum_up(pe, b, i):
                h, j, n = i // CH, i % CH, b * R + i
                if j == 0:
                    pe.wait_ge(sm_in[h], b * 16 + 16)
                pe.wait_ge(carry_kept, n + 1)
                s = s_in[:, h, j * P:(j + 1) * P]
                nc.tensor.matmul(ps_c[i % 2][0:1, 0:MSG], s[:, 0:1], msg[:, h, j, :], start=True, stop=True).then_inc(carry_out, 1)
                pe.wait_ge(sum_kept, n - 1 if i else n)
                nc.tensor.matmul(ps_s[i % 2][:, 0:MSG], s, msg[:, h, j, :], start=True, stop=True).then_inc(summed, 1)

            @block.tensor
            def _(pe):
                def turn(b, last):
                    for h in range(2):
                        for j in range(CH):
                            ahead = (b, CH + j) if h == 0 else None if last else (b + 1, j)
                            if ahead:
                                turn_rows(pe, *ahead)
                            sum_up(pe, b, h * CH + j)
                            if ahead:
                                project(pe, *ahead)

                for j in range(CH):
                    turn_rows(pe, 0, j)
                    project(pe, 0, j)
                with pe.Fori(0, NB - 1) as b:
                    turn(b, False)
                turn(NB - 1, True)

            @block.scalar
            def _(act):
                def keep_turned(b, i):
                    n = b * R + i
                    act.wait_ge(turned, n + 1)
                    nc.scalar.copy(xt[0:D, i % 2, :], ps_t[i % 2][0:D, 0:2 * P]).then_inc(turned_kept, 1)

                def keep_projection(b, i):
                    n = b * R + i
                    act.wait_ge(projected, n + 1)
                    if i % CH == 0:
                        act.wait_ge(msg_ready, b * 2 + i // CH)
                    nc.scalar.copy(kvqe[:, i % CH, :], ps_p[i % 2][:, 0:4 * D]).then_inc(projected_kept, 1)

                def exponent(b, h):
                    act.wait_ge(scored, b * 2 + h + 1)
                    nc.scalar.activation(score[:], score[:], ACT.Exp, scale=float(DH) ** -0.5).then_inc(exped, 1)

                def keep_sums(b, i):
                    h, j, n = i // CH, i % CH, b * R + i
                    if j == 0:
                        act.wait_ge(msg_ready, b * 2 + h + 1)
                    act.wait_ge(carry_out, n)
                    nc.scalar.copy(msg[0:1, h, j, :], ps_c[(i - 1) % 2][0:1, 0:MSG]).then_inc(carry_kept, 1)
                    if j == 0:
                        act.wait_ge(posted, b * 2 + h)
                    act.wait_ge(summed, n + 1)
                    nc.scalar.copy(agg[:, j, :], ps_s[i % 2][:, 0:MSG]).then_inc(sum_kept, 1)

                def root(b, h):
                    act.wait_ge(var_ready, b * 2 + h + 1)
                    nc.scalar.activation(rstd[:], var[:], ACT.Sqrt).then_inc(rstd_ready, 1)

                def turn(b, last):
                    for h in range(2):
                        for j in range(CH):
                            ahead = (b, CH + j) if h == 0 else None if last else (b + 1, j)
                            if ahead:
                                keep_turned(*ahead)
                            keep_sums(b, h * CH + j)
                            if ahead:
                                keep_projection(*ahead)
                        if ahead:
                            exponent(*((b, 1) if h == 0 else (b + 1, 0)))
                        root(b, h)

                for j in range(CH):
                    keep_turned(0, j)
                    keep_projection(0, j)
                exponent(0, 0)
                with act.Fori(0, NB - 1) as b:
                    turn(b, False)
                turn(NB - 1, True)

            @block.vector
            def _(dve):
                def scores(b, h, done):
                    dve.wait_ge(projected_kept, b * R + (h + 1) * CH)
                    done.up(nc.vector.tensor_tensor(prod[:], kvqe[:, :, 0:D], kvqe[:, :, 2 * D:3 * D], ALU.mult))
                    dve.wait_ge(steps, done.now())
                    done.up(nc.vector.tensor_tensor(prod[:], prod[:], kvqe[:, :, 3 * D:4 * D], ALU.mult))
                    dve.wait_ge(steps, done.now())
                    nc.vector.tensor_reduce(out=cols(score[:]), in_=prod[:].rearrange("p c (h d) -> p (c h) d", h=HEADS),
                                            axis=AX_X, op=ALU.add).then_inc(scored, 1)

                def messages(b, h, done):
                    dve.wait_ge(exped, b * 2 + h + 1)
                    done.up(nc.vector.tensor_scalar(msg[:, h, :, D:D + HEADS], score[:], E_LOW, E_HIGH, ALU.max, ALU.min))
                    done.up(nc.vector.memset(msg[:, h, :, D + HEADS:D + HEADS + 1], 1.0))
                    done.up(nc.vector.tensor_copy(msg[:, h, :, D + HEADS + 1], w_s[:, ds(b * R + h * CH, CH)]))
                    dve.wait_ge(steps, done.now())
                    nc.vector.tensor_tensor(per_head(msg[:, h, :, 0:D]), per_head(kvqe[:, :, D:2 * D]),
                                            every(msg[:, h, :, D:D + HEADS]), ALU.mult).then_inc(msg_ready, 1)

                def attend(b, h, done):
                    t = ds(b * R + h * CH, CH)
                    y = xd[:, h * CH:(h + 1) * CH, :]
                    dve.wait_ge(sum_kept, b * R + (h + 1) * CH)
                    done.up(nc.vector.tensor_scalar(zinv[:], agg[:, :, D:D + HEADS], 1e-6, None, ALU.add))
                    done.up(nc.vector.tensor_copy(cnt[:, t], agg[:, :, D + HEADS]))
                    done.up(nc.vector.tensor_copy(wsum[:, t], agg[:, :, D + HEADS + 1]))
                    done.up(nc.vector.tensor_scalar(deg[:], agg[:, :, D + HEADS], 1.0, None, ALU.add))
                    dve.wait_ge(steps, done.now())
                    done.up(nc.vector.reciprocal(zinv[:], zinv[:]))
                    dve.wait_ge(steps, done.now())
                    done.up(nc.vector.tensor_tensor(per_head(prod[:]), per_head(agg[:, :, 0:D]), every(zinv[:]), ALU.mult))
                    dve.wait_ge(steps, done.now())
                    done.up(nc.vector.tensor_tensor(y, y, prod[:], ALU.add))
                    dve.wait_ge(steps, done.now())
                    row_moments(dve, done, [xd[:, h * CH + j, :] for j in range(CH)], stats, mv)
                    done.up(nc.vector.scalar_tensor_tensor(out=var[:], in0=mv[:, :, 1], scalar=EPS, in1=deg[:], op0=ALU.add, op1=ALU.mult))
                    dve.wait_ge(steps, done.now())
                    nc.vector.reciprocal(var[:], var[:]).then_inc(var_ready, 1)

                def new_state(b, h):
                    t = ds(b * R + h * CH, CH)
                    dve.wait_ge(rstd_ready, 2 * b + h + 1)
                    for j in range(CH):
                        k = nc.vector.tensor_scalar(state[:, ds(b * R + h * CH + j, 1), :], xd[:, h * CH + j:h * CH + j + 1, :],
                                                    mv[:, j, 0:1], rstd[:, j:j + 1], ALU.subtract, ALU.mult)
                    k.then_inc(posted, 1)
                    dve.wait_ge(posted, 2 * b + h + 1)
                    nc.vector.tensor_scalar(fixed[:, t, :], state[:, t, :], ALPHA, None, ALU.mult)

                per_turn = 2 * (5 + 9 + 2 * CH)
                before = Count(steps, 0, 0)

                def turn(b, last):
                    done = Count(steps, b, per_turn)
                    done.n = before.n
                    for h in range(2):
                        ahead = (b, 1) if h == 0 else None if last else (b + 1, 0)
                        if ahead:
                            scores(*ahead, done)
                        attend(b, h, done)
                        if ahead:
                            messages(*ahead, done)
                        new_state(b, h)
                    return done

                scores(0, 0, before)
                messages(0, 0, before)
                with dve.Fori(0, NB - 1) as b:
                    assert turn(b, False).n == before.n + per_turn
                turn(NB - 1, True)


E_LOW, E_HIGH = 0.006737946999085467, 148.4131591025766


def degrees(nc, cnt, wsum, step_a, dis_w):
    with semaphores(nc) as sem, nc.Block() as block:
        steps, inverse = sem("deg_steps"), sem("deg_inverse")

        @block.scalar
        def _(act):
            act.wait_ge(inverse, 1)
            nc.scalar.activation(dis_w[:], wsum[:], ACT.Sqrt)

        @block.vector
        def _(dve):
            nc.vector.tensor_scalar(cnt[:], cnt[:], 1.0, None, ALU.add).then_inc(steps, 1)
            nc.vector.tensor_scalar(wsum[:], wsum[:], 1.0, None, ALU.add).then_inc(steps, 1)
            dve.wait_ge(steps, 2)
            nc.vector.reciprocal(step_a[:], cnt[:]).then_inc(steps, 1)
            nc.vector.reciprocal(wsum[:], wsum[:]).then_inc(inverse, 1)
            dve.wait_ge(steps, 3)
            nc.vector.tensor_scalar(step_a[:], step_a[:], 1.0 - ALPHA, None, ALU.mult).then_inc(steps, 1)


def appnp(nc, state, fixed, ident, ptr_a, ptr_b, step_a, sums, tab1, slot_rows):
    PSUMS = 5
    with ExitStack() as c:
        sem = c.enter_context(semaphores(nc))
        g = c.enter_context(nc.sbuf_tensor("l1_g", [P, R, D], F32))
        s_in = c.enter_context(nc.sbuf_tensor("l1_s", [P, 2, CH * P], F32))
        idx = c.enter_context(nc.sbuf_tensor("l1_idx", [P, 2, CH], I32))
        ps = [c.enter_context(nc.psum_tensor(f"l1_ps{k}", [P, 512], F32)) for k in range(PSUMS)]
        pc = [c.enter_context(nc.psum_tensor(f"l1_pc{k}", [P, 512], F32)) for k in range(2)]
        rows_in = [sem(f"l1_rows_in{i}") for i in range(R)]
        s_landed = [sem(f"l1_s_in{h}") for h in range(2)]
        staged, go, zeroed = sem("l1_staged"), sem("l1_go"), sem("l1_zeroed")
        carry_out, carry_kept, summed = sem("l1_carry_out"), sem("l1_carry_kept"), sem("l1_summed")
        freed = sem("l1_freed")
        written = sem("l1_written")

        with nc.Block() as block:
            @block.vector
            def _(dve):
                nc.vector.memset(pc[1][0:1, :], 0.0).then_inc(zeroed, 1)
                dve.sem_inc(freed, R)

        with nc.Block() as block:
            @block.sync
            def _(sp):
                def load_s(cc, h):
                    sp.dma_start(s_in[:, h, :], sums[:, ds(cc * (CH * P), CH * P)]).then_inc(s_landed[h], 16)

                for h in range(2):
                    load_s(h, h)
                with sp.Fori(0, STEPS // 2) as pair:
                    for odd in range(2):
                        with sp.Fori(0, NB) as b:
                            n0 = pair * (2 * T) + b * R + odd * T
                            to = slot_rows(tab1, 0 if odd else NS + NN)
                            for h in range(2):
                                sp.wait_ge(summed, n0 + CH * (h + 1))
                                load_s(2 * b + 2 + h, h)
                                sp.wait_ge(freed, n0 + (R + CH * (h + 1)))
                                sp.dma_start(to[:, ds(b * R + CH * h, CH), :], state[:, ds(b * R + CH * h, CH), :]).then_inc(written, 16)
                sp.wait_ge(written, 16 * 2 * NB * STEPS)
                for h in range(2):
                    sp.wait_ge(s_landed[h], 16 * (NB * STEPS + 1))

            @block.gpsimd
            def _(pool):
                with pool.Fori(0, STEPS // 2) as pair:
                    for odd in range(2):
                        pool.wait_ge(written, pair * (64 * NB) + odd * (32 * NB))
                        pool.sem_inc(go, 1)
                        with pool.Fori(0, NB) as b:
                            n0 = pair * (2 * T) + b * R + odd * T
                            for h in range(2):
                                pool.wait_ge(freed, n0 + CH * (h + 1))
                                nc.gpsimd.tensor_copy(idx[:, h, :], (ptr_b if odd else ptr_a)[:, ds(b * R + h * CH, CH)]).then_inc(staged, 1)
                                pool.wait_ge(staged, pair * (4 * NB) + b * 2 + (odd * 2 * NB + h + 1))
                                pool.sem_inc(go, 1)
                                for j in range(CH):
                                    nc.gpsimd.indirect_dma_start(g[:, h * CH + j, :], None, tab1 if odd else tab1[0:NS + NN, :],
                                                                 bass.IndirectOffsetOnAxis(ap=idx[:, h, j:j + 1], axis=0)).then_inc(rows_in[h * CH + j], 16)

            @block.scalar
            def _(act):
                with act.Fori(0, STEPS) as r:
                    with act.Fori(0, NB) as b:
                        for i in range(R):
                            act.wait_ge(rows_in[i], r * (16 * NB) + b * 16 + 16)
                            act.wait_ge(carry_out, r * T + b * R + i)
                            nc.scalar.copy(g[0:1, i, :], pc[(i - 1) % 2][0:1, 0:D]).then_inc(carry_kept, 1)

            @block.tensor
            def _(pe):
                with pe.Fori(0, STEPS) as r:
                    with pe.Fori(0, NB) as b:
                        for i in range(R):
                            h, j = i // CH, i % CH
                            if j == 0:
                                pe.wait_ge(s_landed[h], r * (16 * NB) + b * 16 + 16)
                            pe.wait_ge(freed, r * T + b * R + (i + 1 + R - PSUMS))
                            to = ps[i % PSUMS][:, 0:D]
                            s = s_in[:, h, j * P:(j + 1) * P]
                            nc.tensor.matmul(to, ident[:], cols(state[:, ds(b * R + i, 1), :]), start=True, stop=False)
                            pe.wait_ge(carry_kept, r * T + b * R + i + 1)
                            nc.tensor.matmul(pc[i % 2][0:1, 0:D], s[:, 0:1], g[:, i, :], start=True, stop=True).then_inc(carry_out, 1)
                            nc.tensor.matmul(to, s, g[:, i, :], start=False, stop=True).then_inc(summed, 1)

            @block.vector
            def _(dve):
                with dve.Fori(0, STEPS) as r:
                    with dve.Fori(0, NB) as b:
                        for i in range(R):
                            t = ds(b * R + i, 1)
                            dve.wait_ge(summed, r * T + b * R + i + 1)
                            nc.vector.scalar_tensor_tensor(out=state[:, t, :], in0=ps[i % PSUMS][:, 0:D].rearrange("p (a d) -> p a d", a=1),
                                                           scalar=step_a[:, t], in1=fixed[:, t, :], op0=ALU.mult, op1=ALU.add).then_inc(freed, 1)


def isolated_nodes(nc, ident, w1, w2, w3, wa, tabs, node_rows, out_rows):
    NJ = NQ // JW
    W = JW * P
    tab1, tab2, tab3, tab4, tab5 = tabs
    with ExitStack() as c:
        sem = c.enter_context(semaphores(nc))
        def sb(name, shape):
            return c.enter_context(nc.sbuf_tensor("n_" + name, shape, F32))

        w1_s, w2_s, w3_s, wa_s = (sb(k, [D + 1, D]) for k in ("w1", "w2", "w3", "wa"))
        x1 = sb("x1", [P, 2, JW, D])
        x2 = sb("x2", [P, 2, JW, D])
        h1 = sb("h1", [P, 2, JW, D])
        h2 = sb("h2", [P, 2, JW, D])
        y = sb("y", [P, 2, JW, D])
        x3 = sb("x3", [P, 2, JW, D])
        res = sb("res", [P, 2, JW, D])
        xt = sb("xt", [D + 1, 2, W])
        h1t = sb("h1t", [D + 1, 2, W])
        h2t = sb("h2t", [D + 1, 2, W])
        stats = sb("stats", [P, 2, JW, 6])
        mv = sb("mv", [P, 2, JW, 2])
        var = sb("var", [P, 2, JW])
        rstd = sb("rstd", [P, 2, JW])
        ps_a = [c.enter_context(nc.psum_tensor(f"n_ps_a{k}", [P, 512], F32)) for k in range(2)]
        ps_b = [c.enter_context(nc.psum_tensor(f"n_ps_b{k}", [P, 512], F32)) for k in range(2)]
        ps_c = [c.enter_context(nc.psum_tensor(f"n_ps_c{k}", [P, 512], F32)) for k in range(2)]

        def s(name):
            return sem("n_" + name)

        const_in = s("const_in")
        x1_in = [s(f"x1_in{k}") for k in range(2)]
        outs = {k: [s(f"{k}_out{j}") for j in range(2)] for k in ("x2", "h1", "h2", "x3", "res")}
        steps, var_ready, rstd_ready = s("steps"), s("var_ready"), s("rstd_ready")
        x2_ready, h1_ready, h2_ready, y_ready, x3_ready, res_ready = (s(k) for k in ("x2_ready", "h1_ready", "h2_ready", "y_ready", "x3_ready", "res_ready"))
        turned, turned_kept = s("turned"), s("turned_kept")
        wide, wide_kept, narrow, turns = s("wide"), s("wide_kept"), s("narrow"), s("turns")

        with nc.Block() as block:
            @block.sync
            def _(sp):
                for to, frm in ((w1_s, w1), (w2_s, w2), (w3_s, w3), (wa_s, wa)):
                    sp.dma_start(to[:], frm).then_inc(const_in, 16)
                sp.wait_ge(const_in, 64)

            @block.vector
            def _(dve):
                for a in (xt, h1t, h2t):
                    nc.vector.memset(a[D:D + 1, :, :], 1.0)

        with nc.Block() as block:
            @block.sync
            def _(sp):
                def load(J, k):
                    sp.dma_start(x1[:, k], node_rows(tab1)[:, ds(J * JW, JW), :]).then_inc(x1_in[k], 16)

                def store(J, k, name, ready, frm, to):
                    sp.wait_ge(ready, J + 1)
                    sp.sem_inc(turns, 1)
                    sp.dma_start(to[:, ds(J * JW, JW), :], frm[:, k]).then_inc(outs[name][k], 16)

                def turn(b, last):
                    for k in range(2):
                        store(2 * b + k, k, "x2", x2_ready, x2, node_rows(tab2))
                        if not last:
                            load(2 * b + 2 + k, k)
                    for name, ready, frm, to in (("h1", h1_ready, h1, node_rows(tab3)), ("h2", h2_ready, h2, node_rows(tab4)),
                                                 ("x3", x3_ready, x3, node_rows(tab5)), ("res", res_ready, res, out_rows)):
                        for k in range(2):
                            store(2 * b + k, k, name, ready, frm, to)

                for k in range(2):
                    load(k, k)
                with sp.Fori(0, NJ // 2 - 1) as b:
                    turn(b, False)
                turn(NJ // 2 - 1, True)
                for k in range(2):
                    for name in outs:
                        sp.wait_ge(outs[name][k], 16 * (NJ // 2))

            @block.tensor
            def _(pe):
                def transpose(J, k, ready, frm, stage):
                    pe.wait_ge(ready, J + 1)
                    for j in range(JW):
                        m = nc.tensor.transpose(ps_a[k][0:D, j * P:(j + 1) * P], frm[:, k, j, :], ident[:])
                    m.then_inc(turned, 1)

                def linear(b, k, kept, count, frm, w, wide_too):
                    pe.wait_ge(kept, count)
                    if wide_too:
                        nc.tensor.matmul(ps_b[k][0:D, 0:W], w[:], frm[:, k, :], start=True, stop=True).then_inc(wide, 1)
                    for j in range(JW):
                        m = nc.tensor.matmul(ps_c[k][:, j * D:(j + 1) * D], frm[:, k, j * P:(j + 1) * P], w[:], start=True, stop=True)
                    m.then_inc(narrow, 1)

                with pe.Fori(0, NJ // 2) as b:
                    for k in range(2):
                        transpose(2 * b + k, k, x2_ready, x2, 0)
                    for k in range(2):
                        linear(b, k, turned_kept, b * 4 + k + 1, xt, w1_s, True)
                    for k in range(2):
                        pe.wait_ge(h1_ready, 2 * b + k + 1)
                        linear(b, k, wide_kept, b * 4 + k + 1, h1t, w2_s, True)
                    for k in range(2):
                        pe.wait_ge(h2_ready, 2 * b + k + 1)
                        linear(b, k, wide_kept, b * 4 + k + 3, h2t, w3_s, False)
                    for k in range(2):
                        transpose(2 * b + k, k, x3_ready, x3, 1)
                    for k in range(2):
                        linear(b, k, turned_kept, b * 4 + k + 3, xt, wa_s, False)

            @block.scalar
            def _(act):
                def root(b, k, stage):
                    act.wait_ge(var_ready, b * 6 + (stage * 2 + k + 1))
                    nc.scalar.activation(rstd[:, k, :], var[:, k, :], ACT.Sqrt).then_inc(rstd_ready, 1)

                def keep_turned(b, k, stage):
                    act.wait_ge(turned, b * 4 + (stage * 2 + k + 1))
                    nc.scalar.copy(xt[0:D, k, :], ps_a[k][0:D, 0:W]).then_inc(turned_kept, 1)

                def keep_wide(b, k, stage, to):
                    act.wait_ge(wide, b * 4 + (stage * 2 + k + 1))
                    nc.scalar.activation(to[0:D, k, :], ps_b[k][0:D, 0:W], ACT.Relu).then_inc(wide_kept, 1)

                with act.Fori(0, NJ // 2) as b:
                    for k in range(2):
                        root(b, k, 0)
                    for k in range(2):
                        keep_turned(b, k, 0)
                    for k in range(2):
                        keep_wide(b, k, 0, h1t)
                    for k in range(2):
                        keep_wide(b, k, 1, h2t)
                    for k in range(2):
                        root(b, k, 1)
                    for k in range(2):
                        keep_turned(b, k, 1)
                    for k in range(2):
                        root(b, k, 2)

            @block.vector
            def _(dve):
                def moments(k, done, of, eps):
                    row_moments(dve, done, [of[:, k, j, :] for j in range(JW)], stats[:, k], mv[:, k])
                    done.up(nc.vector.tensor_scalar(var[:, k, :], mv[:, k, :, 1], eps, None, ALU.add))
                    dve.wait_ge(steps, done.now())
                    nc.vector.reciprocal(var[:, k, :], var[:, k, :]).then_inc(var_ready, 1)

                def normed(b, k, stage, frm, to, name, ready):
                    dve.wait_ge(outs[name][k], b * 16)
                    dve.wait_ge(rstd_ready, b * 6 + (stage * 2 + k + 1))
                    for j in range(JW):
                        m = nc.vector.tensor_scalar(to[:, k, j, :], frm[:, k, j, :], mv[:, k, j, 0:1], rstd[:, k, j:j + 1],
                                                    ALU.subtract, ALU.mult)
                    m.then_inc(ready, 1)

                def rectified(b, k, stage, to, name, ready):
                    dve.wait_ge(outs[name][k], b * 16)
                    dve.wait_ge(narrow, b * 8 + (stage * 2 + k + 1))
                    nc.vector.tensor_scalar(cols(to[:, k]), ps_c[k][:, 0:JW * D], 0.0, None, ALU.max).then_inc(ready, 1)

                def residual(b, k, stage, x_, done):
                    dve.wait_ge(narrow, b * 8 + (stage * 2 + k + 1))
                    done.up(nc.vector.tensor_tensor(cols(y[:, k]), cols(x_[:, k]), ps_c[k][:, 0:JW * D], ALU.add))
                    dve.wait_ge(steps, done.now())
                    moments(k, done, y, EPS)

                per_turn = 2 * (3 * (2 * JW + 2) + 2)
                with dve.Fori(0, NJ // 2) as b:
                    done = Count(steps, b, per_turn)
                    for k in range(2):
                        dve.wait_ge(x1_in[k], b * 16 + 16)
                        moments(k, done, x1, EPS / 4)
                    for k in range(2):
                        normed(b, k, 0, x1, x2, "x2", x2_ready)
                    for k in range(2):
                        rectified(b, k, 0, h1, "h1", h1_ready)
                    for k in range(2):
                        rectified(b, k, 1, h2, "h2", h2_ready)
                    for k in range(2):
                        residual(b, k, 2, x2, done)
                    for k in range(2):
                        normed(b, k, 1, y, x3, "x3", x3_ready)
                    for k in range(2):
                        residual(b, k, 3, x3, done)
                    for k in range(2):
                        normed(b, k, 2, y, res, "res", res_ready)
                    assert done.n == per_turn, done.n


def second_norm(nc, state, fixed, cnt, dis_w, dis_c, canon, tab_slots):
    with ExitStack() as c:
        sem = c.enter_context(semaphores(nc))
        y = c.enter_context(nc.sbuf_tensor("m_y", [P, 2, CH, D], F32))
        stats = c.enter_context(nc.sbuf_tensor("m_stats", [P, 2, CH, 6], F32))
        mv = c.enter_context(nc.sbuf_tensor("m_mv", [P, 2, CH, 2], F32))
        var = c.enter_context(nc.sbuf_tensor("m_var", [P, 2, CH], F32))
        rstd = c.enter_context(nc.sbuf_tensor("m_rstd", [P, 2, CH], F32))
        steps, var_ready, rstd_ready, normed = sem("m_steps"), sem("m_var_ready"), sem("m_rstd_ready"), sem("m_normed")
        masked, scaled, written = sem("m_masked"), sem("m_scaled"), sem("m_written")
        with nc.Block() as block:
            @block.sync
            def _(sp):
                with sp.Fori(0, NB) as b:
                    for h in range(2):
                        t = ds(b * R + h * CH, CH)
                        sp.wait_ge(scaled, 2 * b + h + 1)
                        sp.dma_start(tab_slots[:, t, :], state[:, t, :]).then_inc(written, 16)
                sp.wait_ge(written, 32 * NB)

            @block.scalar
            def _(act):
                act.wait_ge(masked, 1)
                with act.Fori(0, NB) as b:
                    for h in range(2):
                        act.wait_ge(var_ready, 2 * b + h + 1)
                        nc.scalar.activation(rstd[:, h, :], var[:, h, :], ACT.Sqrt).then_inc(rstd_ready, 1)
                    for h in range(2):
                        act.wait_ge(normed, 2 * b + h + 1)
                        for j in range(CH):
                            t = ds(b * R + h * CH + j, 1)
                            k = nc.scalar.activation(state[:, t, :], fixed[:, t, :], ACT.Copy, scale=dis_c[:, t])
                        k.then_inc(scaled, 1)

            @block.vector
            def _(dve):
                nc.vector.tensor_tensor(dis_c[:], dis_w[:], canon[:], ALU.mult).then_inc(masked, 1)
                per_turn = 2 * (1 + 2 * CH + 1 + 3)
                with dve.Fori(0, NB) as b:
                    done = Count(steps, b, per_turn)
                    for h in range(2):
                        t = ds(b * R + h * CH, CH)
                        dve.wait_ge(normed, 2 * b)
                        done.up(nc.vector.scalar_tensor_tensor(out=cols(y[:, h]), in0=cols(fixed[:, t, :]), scalar=1.0 / ALPHA, in1=cols(state[:, t, :]),
                                                               op0=ALU.mult, op1=ALU.add))
                        dve.wait_ge(steps, done.now())
                        row_moments(dve, done, [y[:, h, j, :] for j in range(CH)], stats[:, h], mv[:, h])
                        done.up(nc.vector.tensor_tensor(var[:, h, :], mv[:, h, :, 1], cnt[:, t], ALU.mult))
                        dve.wait_ge(steps, done.now())
                        done.up(nc.vector.tensor_scalar(var[:, h, :], var[:, h, :], EPS, None, ALU.add))
                        dve.wait_ge(steps, done.now())
                        done.up(nc.vector.reciprocal(var[:, h, :], var[:, h, :]))
                        dve.wait_ge(steps, done.now())
                        nc.vector.tensor_tensor(var[:, h, :], var[:, h, :], cnt[:, t], ALU.mult).then_inc(var_ready, 1)
                    for h in range(2):
                        dve.wait_ge(rstd_ready, 2 * b + h + 1)
                        for j in range(CH):
                            k = nc.vector.tensor_scalar(fixed[:, ds(b * R + h * CH + j, 1), :], y[:, h, j:j + 1, :], mv[:, h, j, 0:1],
                                                        rstd[:, h, j:j + 1], ALU.subtract, ALU.mult)
                        k.then_inc(normed, 1)
                    assert done.n == per_turn, done.n


def convolution(nc, layer, state, fixed, ident, ptr_a, w_s, dis_w, dis_c, scat, w, wa, tab, sums, tab_next, out):
    inner, final = layer < 4, layer == 5
    with ExitStack() as c:
        sem = c.enter_context(semaphores(nc))
        def sb(name, shape, dt=F32):
            return c.enter_context(nc.sbuf_tensor(f"c{layer}_{name}", shape, dt))

        def s(name):
            return sem(f"c{layer}_{name}")

        w_in = sb("w", [D, D])
        bias = sb("bias", [P, D])
        wa_in = sb("wa", [D + 1, D])
        g = sb("g", [P, R, D])
        gw = sb("gw", [P, R, D])
        s_in = sb("s", [P, 2, CH * P])
        idx = sb("idx", [P, 2, CH], I32)
        scat_idx = sb("scat_idx", [P, 2, CH], I32)
        at = sb("at", [D, 2, P])
        own = sb("own", [P, 2, D])
        own_t = sb("own_t", [D + 1, 2, P])
        y = sb("y", [P, CH, D])
        tmp = sb("tmp", [P, 2, D])
        res = sb("res", [P, 2, CH, D])
        stats, mv = sb("stats", [P, CH, 6]), sb("mv", [P, CH, 2])
        var, rstd = sb("var", [P, CH]), sb("rstd", [P, CH])
        ps_t = [c.enter_context(nc.psum_tensor(f"c{layer}_ps_t{k}", [P, 512], F32)) for k in range(2)]
        ps_w = [c.enter_context(nc.psum_tensor(f"c{layer}_ps_w{k}", [P, 512], F32)) for k in range(2)]
        pc = [c.enter_context(nc.psum_tensor(f"c{layer}_pc{k}", [P, 512], F32)) for k in range(2)]
        ps_o = [c.enter_context(nc.psum_tensor(f"c{layer}_ps_o{k}", [P, 512], F32)) for k in range(2)]
        const_in = s("const_in")
        rows_in = [s(f"rows_in{i}") for i in range(R)]
        s_landed = [s(f"s_in{h}") for h in range(2)]
        staged, go = s("staged"), s("go")
        weighted, carry_out, carry_kept = s("weighted"), s("carry_out"), s("carry_kept")
        summed, sum_kept, own_kept, own_turned, own_t_kept = s("summed"), s("sum_kept"), s("own_kept"), s("own_turned"), s("own_t_kept")
        mapped, posted, steps = s("mapped"), s("posted"), s("steps")
        var_ready, rstd_ready, written = s("var_ready"), s("rstd_ready"), s("written")
        scat_staged = s("scat_staged")
        scattered = [s(f"scattered{h}") for h in range(2)]
        freed, chunk_done = s("freed"), s("chunk_done")

        with nc.Block() as block:
            @block.sync
            def _(sp):
                sp.dma_start(w_in[:], w[0:D, :]).then_inc(const_in, 16)
                if final:
                    sp.dma_start(wa_in[:], wa).then_inc(const_in, 16)
                else:
                    sp.dma_start(bias[:], w[D:D + 1, :].broadcast_to([P, D])).then_inc(const_in, 16)
                sp.wait_ge(const_in, 32)

            @block.vector
            def _(dve):
                nc.vector.memset(pc[1][0:1, :], 0.0)
                nc.vector.memset(own_t[D:D + 1, :, :], 1.0)
                dve.sem_inc(freed, 2)
                dve.sem_inc(chunk_done, 2)

        with nc.Block() as block:
            @block.sync
            def _(sp):
                def load_s(cc, h):
                    sp.dma_start(s_in[:, h, :], sums[:, ds(cc * (CH * P), CH * P)]).then_inc(s_landed[h], 16)

                for h in range(2):
                    load_s(h, h)
                with sp.Fori(0, NB) as b:
                    for h in range(2):
                        t = ds(b * R + CH * h, CH)
                        sp.wait_ge(summed, b * R + CH * (h + 1))
                        load_s(2 * b + 2 + h, h)
                        if not final:
                            sp.wait_ge(chunk_done, 2 * b + (h + 3))
                            sp.dma_start(tab_next[:, t, :], state[:, t, :]).then_inc(written, 16)
                if not final:
                    sp.wait_ge(written, 32 * NB)
                for h in range(2):
                    sp.wait_ge(s_landed[h], 16 * (NB + 1))

            @block.gpsimd
            def _(pool):
                def scatter(b, h):
                    pool.wait_ge(scat_staged, 2 * b + h + 1)
                    pool.wait_ge(chunk_done, 2 * b + (h + 3))
                    pool.sem_inc(go, 1)
                    for j in range(CH):
                        nc.gpsimd.indirect_dma_start(out, bass.IndirectOffsetOnAxis(ap=scat_idx[:, h, j:j + 1], axis=0), res[:, h, j, :], None,
                                                     bounds_check=N - 1, oob_is_err=False).then_inc(scattered[h], 16)

                with pool.Fori(0, NB) as b:
                    for h in range(2):
                        pool.wait_ge(chunk_done, 2 * b + (h + 1))
                        nc.gpsimd.tensor_copy(idx[:, h, :], ptr_a[:, ds(b * R + h * CH, CH)]).then_inc(staged, 1)
                        pool.wait_ge(staged, b * 2 + (h + 1))
                        pool.sem_inc(go, 1)
                        for j in range(CH):
                            nc.gpsimd.indirect_dma_start(g[:, h * CH + j, :], None, tab,
                                                         bass.IndirectOffsetOnAxis(ap=idx[:, h, j:j + 1], axis=0)).then_inc(rows_in[h * CH + j], 16)
                    if final:
                        for h in range(2):
                            pool.wait_ge(scattered[h], b * (16 * CH))
                            nc.gpsimd.tensor_copy(scat_idx[:, h, :], scat[:, ds(b * R + h * CH, CH)]).then_inc(scat_staged, 1)
                            scatter(b, h)
                if final:
                    for h in range(2):
                        pool.wait_ge(scattered[h], 16 * CH * NB)

            @block.tensor
            def _(pe):
                def total(b, i):
                    h, j, n = i // CH, i % CH, b * R + i
                    if j == 0:
                        pe.wait_ge(s_landed[h], b * 16 + 16)
                    if final:
                        pe.wait_ge(own_kept, n + 1)
                        nc.tensor.transpose(ps_o[i % 2][0:D, 0:P], own[:, i % 2, :], ident[:]).then_inc(own_turned, 1)
                    m = s_in[:, h, j * P:(j + 1) * P]
                    pe.wait_ge(carry_kept, n + 1)
                    nc.tensor.matmul(pc[i % 2][0:1, 0:D], m[:, 0:1], gw[:, i, :], start=True, stop=True).then_inc(carry_out, 1)
                    if i > 1:
                        pe.wait_ge(sum_kept, n - 1)
                    nc.tensor.matmul(ps_t[i % 2][0:D, 0:P], gw[:, i, :], m, start=True, stop=True).then_inc(summed, 1)

                def linear(b, i):
                    n = b * R + i
                    pe.wait_ge(freed, n + 1)
                    pe.wait_ge(sum_kept, n + 1)
                    if final:
                        pe.wait_ge(own_t_kept, n + 1)
                        nc.tensor.matmul(ps_w[i % 2][:, 0:D], own_t[:, i % 2, :], wa_in[:], start=True, stop=False)
                    nc.tensor.matmul(ps_w[i % 2][:, 0:D], at[:, i % 2, :], w_in[:], start=not final, stop=True).then_inc(mapped, 1)

                with pe.Fori(0, NB) as b:
                    for i in range(R):
                        total(b, i)
                        if i:
                            linear(b, i - 1)
                    linear(b, R - 1)

            @block.scalar
            def _(act):
                def keep(b, i):
                    n = b * R + i
                    if i > 1:
                        act.wait_ge(mapped, n - 1)
                    act.wait_ge(summed, n + 1)
                    nc.scalar.copy(at[:, i % 2, :], ps_t[i % 2][0:D, 0:P]).then_inc(sum_kept, 1)
                    if final:
                        act.wait_ge(own_turned, n + 1)
                        nc.scalar.copy(own_t[0:D, i % 2, :], ps_o[i % 2][0:D, 0:P]).then_inc(own_t_kept, 1)

                def root(b, h):
                    act.wait_ge(var_ready, 2 * b + h + 1)
                    nc.scalar.activation(rstd[:], var[:], ACT.Sqrt).then_inc(rstd_ready, 1)

                with act.Fori(0, NB) as b:
                    for i in range(R):
                        n = b * R + i
                        if final:
                            if i > 1:
                                act.wait_ge(own_turned, n - 1)
                            nc.scalar.copy(own[:, i % 2, :], cols(state[:, ds(n, 1), :])).then_inc(own_kept, 1)
                        act.wait_ge(weighted, n + 1)
                        act.wait_ge(carry_out, n)
                        nc.scalar.copy(gw[0:1, i, :], pc[(i - 1) % 2][0:1, 0:D]).then_inc(carry_kept, 1)
                        keep(b, i)
                        if not inner and i == CH:
                            root(b, 0)
                    if not inner:
                        root(b, 1)

            @block.vector
            def _(dve):
                def weigh(b, i):
                    n = b * R + i
                    dve.wait_ge(rows_in[i], b * 16 + 16)
                    if final:
                        k = nc.vector.tensor_scalar(gw[:, i:i + 1, :], g[:, i:i + 1, :], w_s[:, ds(n, 1)], None, ALU.mult)
                    else:
                        k = nc.vector.scalar_tensor_tensor(out=gw[:, i:i + 1, :], in0=g[:, i:i + 1, :], scalar=w_s[:, ds(n, 1)],
                                                           in1=state[:, ds(n, 1), :], op0=ALU.mult, op1=ALU.add)
                    k.then_inc(weighted, 1)

                def take(b, i, done):
                    h, j, n = i // CH, i % CH, b * R + i
                    t = ds(n, 1)
                    got = ps_w[i % 2][:, 0:D].rearrange("p (a d) -> p a d", a=1)
                    dve.wait_ge(mapped, n + 1)
                    if final:
                        nc.vector.tensor_tensor(y[:, j:j + 1, :], got, state[:, t, :], ALU.add).then_inc(freed, 1)
                        return
                    nc.vector.scalar_tensor_tensor(out=tmp[:, i % 2:i % 2 + 1, :], in0=got, scalar=dis_w[:, t],
                                                   in1=bias[:].rearrange("p (a d) -> p a d", a=1), op0=ALU.mult, op1=ALU.add).then_inc(freed, 1)
                    dve.wait_ge(freed, n + 3)
                    if inner:
                        k = nc.vector.tensor_scalar(state[:, t, :], tmp[:, i % 2:i % 2 + 1, :], 0.0, dis_c[:, t], ALU.max, ALU.mult)
                        if j == CH - 1:
                            k.then_inc(chunk_done, 1)
                    else:
                        done.up(nc.vector.tensor_tensor(y[:, j:j + 1, :], tmp[:, i % 2:i % 2 + 1, :], fixed[:, t, :], ALU.add))

                def moments(b, h, done):
                    if final:
                        dve.wait_ge(freed, b * R + (h + 1) * CH + 2)
                    else:
                        dve.wait_ge(steps, done.now())
                    row_moments(dve, done, [y[:, j, :] for j in range(CH)], stats, mv)
                    done.up(nc.vector.tensor_scalar(var[:], mv[:, :, 1], EPS, None, ALU.add))
                    dve.wait_ge(steps, done.now())
                    nc.vector.reciprocal(var[:], var[:]).then_inc(var_ready, 1)

                def normed(b, h):
                    if final:
                        dve.wait_ge(scattered[h], b * (16 * CH))
                    dve.wait_ge(rstd_ready, 2 * b + h + 1)
                    for j in range(CH):
                        to = res[:, h, j:j + 1, :] if final else state[:, ds(b * R + h * CH + j, 1), :]
                        k = nc.vector.tensor_scalar(to, y[:, j:j + 1, :], mv[:, j, 0:1], rstd[:, j:j + 1], ALU.subtract, ALU.mult)
                    k.then_inc(chunk_done, 1)

                per_turn = 0 if inner else 2 * ((0 if final else CH) + 2 * CH + 2)
                with dve.Fori(0, NB) as b:
                    done = Count(steps, b, per_turn)
                    weigh(b, 0)
                    for i in range(R):
                        if i < R - 1:
                            weigh(b, i + 1)
                        take(b, i, done)
                        if not inner and i % CH == CH - 1:
                            moments(b, i // CH, done)
                            normed(b, i // CH)
                    assert done.n == per_turn, (done.n, per_turn)


def lay_out(src, dst, edge_attr, edge_weight, x, Wq, bq, Wk, bk, We, be, Wv, bv, W1, b1, W2, b2, W3, b3, mlp_w, mlp_b):
    import numpy as np

    def grid(a, fill):
        g = np.full((T * RE,), fill, a.dtype)
        g[:E] = a
        return g.reshape(T, RE)

    def with_first(first, rest):
        return np.concatenate([first[:, None], rest], axis=1)

    def again(a):
        return np.concatenate([a, a[:R]], axis=0)

    d = grid(dst, N)
    last = d[:, -1]
    before = np.concatenate([np.full((1,), -1, dst.dtype), last[:-1]])
    following = np.concatenate([d.reshape(-1)[1:], np.full((1,), N, dst.dtype)]).reshape(T, RE)
    zero_i, zero_f = np.zeros((T,), src.dtype), np.zeros((T,), edge_weight.dtype)
    ea = np.zeros((T, P, D), edge_attr.dtype)
    ea.reshape(T, P, D)[:, 1:, :] = np.concatenate([edge_attr, np.zeros((T * RE - E, D), edge_attr.dtype)]).reshape(T, RE, D)

    def t_(a):
        return np.ascontiguousarray(a.T)

    def biased(w, b):
        return np.concatenate([w, b[None, :]], axis=0)

    return {
        "x": np.concatenate([x, np.zeros((NN - N, D), x.dtype)]),
        "src_p": t_(with_first(zero_i, grid(src, 0))),
        "dst_k": t_(again(with_first(before, d))),
        "dst_next": t_(with_first(before, following)),
        "dst_i": again(with_first(last, d)).reshape(-1),
        "w_p": t_(with_first(zero_f, grid(edge_weight, 0))),
        "ea_t": t_(ea.reshape(T * P, D)),
        "wkv": np.concatenate([biased(Wk, bk), biased(Wv, bv)], axis=1),
        "wq": biased(Wq, bq),
        "we": biased(We, be),
        "w1": biased(W1, b1),
        "w2": biased(W2, b2),
        "w3": biased(W3, b3),
        "wa": biased(np.ascontiguousarray(mlp_w[:, :D].T), mlp_b),
        "wb": np.ascontiguousarray(mlp_w[:, D:].T),
    }


def kernel(x, src, dst, edge_attr_96, edge_weight, L0_gnn_Wq, L0_gnn_bq, L0_gnn_Wk, L0_gnn_bk, L0_gnn_We, L0_gnn_be,
           L0_gnn_Wv, L0_gnn_bv, L2_gnn_W1, L2_gnn_b1, L2_gnn_W2, L2_gnn_b2, L2_gnn_W3, L2_gnn_b3, L3_gnn_mlp_w, L3_gnn_mlp_b):
    import numpy as np
    import concourse.bacc as bacc
    from concourse.bass_utils import run_bass_kernel_spmd

    given = [np.asarray(a) for a in (src, dst, edge_attr_96, edge_weight, x, L0_gnn_Wq, L0_gnn_bq, L0_gnn_Wk, L0_gnn_bk, L0_gnn_We,
                                     L0_gnn_be, L0_gnn_Wv, L0_gnn_bv, L2_gnn_W1, L2_gnn_b1, L2_gnn_W2, L2_gnn_b2, L2_gnn_W3,
                                     L2_gnn_b3, L3_gnn_mlp_w, L3_gnn_mlp_b)]
    nc = bacc.Bacc("TRN2", target_bir_lowering=False, num_devices=1)
    arrays, args = {}, {}
    for name, a in lay_out(*given).items():
        a = np.ascontiguousarray(a)
        arrays[f"in_{name}"] = a
        args[name] = nc.dram_tensor(f"in_{name}", a.shape, mybir.dt.from_np(a.dtype), kind="ExternalInput").ap()
    args["out"] = nc.dram_tensor("out_nodes", [NN, D], F32, kind="ExternalOutput").ap()

    def scratch(name, shape, dt):
        return nc.dram_tensor(name, shape, dt, kind="Internal").ap()

    build_graph_kernel(nc, scratch, **args)
    r = run_bass_kernel_spmd(nc, [arrays], core_ids=[0])
    return r.results[0]["out_nodes"][:N]
```

```python
from contextlib import ExitStack, contextmanager

import concourse.bass as bass
from concourse import mybir

F32 = mybir.dt.float32
I32 = mybir.dt.int32
ALU = mybir.AluOpType
ACT = mybir.ActivationFunctionType
AX_X = mybir.AxisListType.X

P = 128
D = 96
N = 50000
E = 25000
HEADS = 8
DH = D // HEADS
STEPS = 16
ALPHA = 0.1
EPS = 1e-5

RE = P - 1
CH = 5
R = 2 * CH
T = -(-E // (RE * R)) * R
NB = T // R
NS = T * P
NQ = 392
NN = P * NQ
LNW = 7
JW = 4
JOB_STEPS = 10
LAG = 2
assert JOB_STEPS * (NB // 2) >= NQ // JW + LAG
SKIP = 1 << 20
MSG = D + HEADS + 2


class Count:

    def __init__(self, sem, turn, per):
        self.sem, self.turn, self.per, self.n = sem, turn, per, 0

    def up(self, instruction):
        if hasattr(instruction, "then_inc"):
            instruction.then_inc(self.sem, 1)
        else:
            instruction.sem_inc(self.sem, 1)
        self.n += 1
        return instruction

    def now(self):
        return self.turn * self.per + self.n


@contextmanager
def semaphores(nc):
    taken = []

    def sem(name):
        taken.append(nc.alloc_semaphore(name))
        return taken[-1]

    yield sem
    nc.clear_and_free_semaphores(taken)
    nc.all_engine_barrier()


def ds(start, size):
    return bass.ds(start, size)


def per_head(ap):
    return ap.rearrange("p c (h d) -> p c h d", h=HEADS)


def every(ap):
    return ap.rearrange("p c (h o) -> p c h o", o=1).broadcast_to([P, CH, HEADS, DH])


def cols(ap):
    return ap.rearrange("p a d -> p (a d)")


def row_moments(dve, done, tiles, stats, mv):
    for j, tile in enumerate(tiles):
        done.up(dve.bn_stats(stats[:, j, :], tile))
    dve.wait_ge(done.sem, done.now())
    done.up(dve)
    for j in range(len(tiles)):
        done.up(dve.bn_aggr(mv[:, j, :], stats[:, j, :]))
    dve.wait_ge(done.sem, done.now())


def build_graph_kernel(nc, scratch, x, src_p, dst_k, dst_next, dst_i, w_p, ea_t, wkv, wq, we, w1, w2, w3, wa, wb, out):
    tab1 = scratch("tab1", [2 * NS + NN, D], F32)
    tab2, tab3, tab4, tab5 = (scratch(f"tab{k}", [NS + NN, D], F32) for k in (2, 3, 4, 5))
    slotmap = scratch("slotmap", [NN, 1], I32)
    sums = scratch("sums", [P, (T + R) * P], F32)

    def slot_rows(tab, base=0):
        return tab[base:base + NS, :].rearrange("(p t) d -> p t d", p=P)

    def node_rows(tab):
        return tab[NS:NS + NN, :].rearrange("(p q) d -> p q d", p=P)

    x_rows = x.rearrange("(p q) d -> p q d", p=P)
    out_rows = out.rearrange("(p q) d -> p q d", p=P)

    with ExitStack() as whole:
        def keep(name, shape, dt=F32):
            return whole.enter_context(nc.sbuf_tensor(name, shape, dt))

        state = keep("state", [P, T, D])
        fixed = keep("fixed", [P, T, D])
        ident = keep("ident", [P, P])
        ptr_a = keep("ptr_a", [P, T], I32)
        ptr_b = keep("ptr_b", [P, T], I32)
        src_s = keep("src_s", [P, T], I32)
        dst_s = keep("dst_s", [P, T], I32)
        scat = keep("scat", [P, T], I32)
        w_s = keep("w_s", [P, T])
        cnt = keep("cnt", [P, T])
        wsum = keep("wsum", [P, T])
        canon = keep("canon", [P, T])
        step_a = keep("step_a", [P, T])
        dis_w = keep("dis_w", [P, T])
        dis_c = keep("dis_c", [P, T])

        with ExitStack() as c:
            sem = c.enter_context(semaphores(nc))
            key_k = c.enter_context(nc.sbuf_tensor("key_k", [P, T + R], I32))
            key_f = c.enter_context(nc.sbuf_tensor("key_f", [P, T + R], F32))
            nxt = c.enter_context(nc.sbuf_tensor("nxt", [P, T], I32))
            nxt_f = c.enter_context(nc.sbuf_tensor("nxt_f", [P, T], F32))
            same = c.enter_context(nc.sbuf_tensor("same", [P, T], F32))
            slot_id = c.enter_context(nc.sbuf_tensor("slot_id", [P, T], I32))
            node_id = c.enter_context(nc.sbuf_tensor("node_id", [P, NQ], I32))
            loaded, made, map_set = sem("loaded"), sem("made"), sem("map_set")
            id_set = sem("id_set")
            vec = sem("index_steps")
            with nc.Block() as block:
                @block.sync
                def _(sp):
                    for to, frm in ((key_k, dst_k), (nxt, dst_next), (src_s, src_p), (w_s, w_p)):
                        sp.dma_start(to[:], frm).then_inc(loaded, 16)
                    sp.wait_ge(made, 2)
                    sp.dma_start(slotmap.rearrange("(p q) o -> p (q o)", p=P), node_id[:]).then_inc(map_set, 16)
                    sp.wait_ge(map_set, 16)

                @block.gpsimd
                def _(pool):
                    pool.iota(slot_id[:], [[1, T]], base=0, channel_multiplier=T).then_inc(made, 1)
                    pool.iota(node_id[:], [[1, NQ]], base=NS, channel_multiplier=NQ).then_inc(made, 1)
                    pool.memset(ident[:], 0.0).then_inc(id_set, 1)
                    pool.wait_ge(id_set, 1)
                    pool.affine_select(out=ident[:], in_=ident[:], compare_op=ALU.not_equal, fill=1.0, base=0,
                                       pattern=[[-1, P]], channel_multiplier=1).then_inc(id_set, 1)

                @block.vector
                def _(dve):
                    done = Count(vec, 0, 0)
                    dve.wait_ge(loaded, 64)
                    done.up(nc.vector.tensor_copy(key_f[:], key_k[:]))
                    done.up(nc.vector.tensor_copy(nxt_f[:], nxt[:]))
                    dve.wait_ge(vec, done.now())
                    done.up(nc.vector.tensor_tensor(same[:], key_f[:, 0:T], nxt_f[:], ALU.is_equal))
                    done.up(nc.vector.tensor_scalar(dst_s[:], key_f[:, 0:T], float(N - 1), 0.0, ALU.min, ALU.max))
                    dve.wait_ge(vec, done.now())
                    done.up(nc.vector.tensor_scalar(canon[:], same[:], -1.0, 1.0, ALU.mult, ALU.add))
                    done.up(nc.vector.scalar_tensor_tensor(out=scat[:], in0=same[:], scalar=float(SKIP),
                                                           in1=key_f[:, 0:T], op0=ALU.mult, op1=ALU.add))

            keys = c.enter_context(nc.sbuf_tensor("keys", [P, 2, CH * P], I32))
            s_new = c.enter_context(nc.sbuf_tensor("s_new", [P, 2, CH * P], F32))
            xin = c.enter_context(nc.sbuf_tensor("xin", [P, 2, LNW, D], F32))
            xout = c.enter_context(nc.sbuf_tensor("xout", [P, 2, LNW, D], F32))
            stats = c.enter_context(nc.sbuf_tensor("stats", [P, LNW, 6], F32))
            mv = c.enter_context(nc.sbuf_tensor("mv", [P, 2, LNW, 2], F32))
            var = c.enter_context(nc.sbuf_tensor("var", [P, 2, LNW], F32))
            rstd = c.enter_context(nc.sbuf_tensor("rstd", [P, 2, LNW], F32))
            idx = c.enter_context(nc.sbuf_tensor("idx", [P, 2, CH], I32))
            val = c.enter_context(nc.sbuf_tensor("val", [P, 2, CH], I32))
            keys_in = [sem(f"keys_in{h}") for h in range(2)]
            s_out = [sem(f"s_out{h}") for h in range(2)]
            s_made = sem("s_made")
            x_in = [sem(f"x_in{h}") for h in range(2)]
            x_out = [sem(f"x_out{h}") for h in range(2)]
            ln_done, ln_steps, var_ready, rstd_ready = sem("ln_done"), sem("ln_steps"), sem("var_ready"), sem("rstd_ready")
            staged, go = sem("staged"), sem("go")
            map_done = [sem(f"map_done{h}") for h in range(2)]
            ptr_in = [sem(f"ptr_in{h}") for h in range(2)]
            ptr_kept, ptr_ready = sem("ptr_kept"), sem("ptr_ready")
            NCH = (T + R) // CH
            NJ = NQ // LNW
            with nc.Block() as block:
                @block.sync
                def _(sp):
                    def load_keys(c_, h):
                        part = dst_i[ds(c_ * (CH * P), CH * P)].rearrange("(o n) -> o n", o=1)
                        sp.dma_start(keys[:, h, :], part.broadcast_to([P, CH * P])).then_inc(keys_in[h], 16)

                    for h in range(2):
                        load_keys(h, h)
                        sp.dma_start(xin[:, h], x_rows[:, h * LNW:(h + 1) * LNW, :]).then_inc(x_in[h], 16)
                    with sp.Fori(0, NCH // 2 - 1) as b:
                        for h in range(2):
                            sp.wait_ge(s_made, 2 * b + h + 1)
                            load_keys(2 * b + 2 + h, h)
                            sp.dma_start(sums[:, ds((2 * b + h) * (CH * P), CH * P)], s_new[:, h, :]).then_inc(s_out[h], 16)
                    for h in range(2):
                        sp.wait_ge(s_made, NCH - 1 + h)
                        sp.dma_start(sums[:, (NCH - 2 + h) * CH * P:(NCH - 1 + h) * CH * P], s_new[:, h, :]).then_inc(s_out[h], 16)
                    with sp.Fori(0, NJ // 2 - 1) as b:
                        for h in range(2):
                            sp.wait_ge(ln_done, 2 * b + h + 1)
                            sp.dma_start(xin[:, h], x_rows[:, ds((2 * b + 2 + h) * LNW, LNW), :]).then_inc(x_in[h], 16)
                            sp.dma_start(node_rows(tab1)[:, ds((2 * b + h) * LNW, LNW), :], xout[:, h]).then_inc(x_out[h], 16)
                    for h in range(2):
                        sp.wait_ge(ln_done, NJ - 1 + h)
                        sp.dma_start(node_rows(tab1)[:, (NJ - 2 + h) * LNW:(NJ - 1 + h) * LNW, :], xout[:, h]).then_inc(x_out[h], 16)
                    for h in range(2):
                        sp.wait_ge(s_out[h], 16 * (NCH // 2))
                        sp.wait_ge(x_out[h], 16 * (NJ // 2))

                @block.scalar
                def _(act):
                    with act.Fori(0, NJ // 2) as b:
                        for h in range(2):
                            act.wait_ge(var_ready, 2 * b + h + 1)
                            nc.scalar.activation(rstd[:, h, :], var[:, h, :], ACT.Sqrt).then_inc(rstd_ready, 1)

                @block.vector
                def _(dve):
                    with dve.Fori(0, NCH // 2) as b:
                        for h in range(2):
                            dve.wait_ge(keys_in[h], b * 16 + 16)
                            dve.wait_ge(s_out[h], b * 16)
                            for j in range(CH):
                                k = nc.vector.tensor_scalar(s_new[:, h, j * P:(j + 1) * P], keys[:, h, j * P:(j + 1) * P],
                                                            key_f[:, ds(b * R + h * CH + j, 1)], None, ALU.is_equal)
                            k.then_inc(s_made, 1)
                    with dve.Fori(0, NJ // 2) as b:
                        done = Count(ln_steps, b, 2 * (2 * LNW + 2))
                        for h in range(2):
                            dve.wait_ge(x_in[h], b * 16 + 16)
                            row_moments(dve, done, [xin[:, h, j, :] for j in range(LNW)], stats, mv[:, h])
                            done.up(nc.vector.tensor_scalar(var[:, h, :], mv[:, h, :, 1], EPS, None, ALU.add))
                            dve.wait_ge(ln_steps, done.now())
                            nc.vector.reciprocal(var[:, h, :], var[:, h, :]).then_inc(var_ready, 1)
                        for h in range(2):
                            dve.wait_ge(x_out[h], b * 16)
                            dve.wait_ge(rstd_ready, 2 * b + h + 1)
                            for j in range(LNW):
                                k = nc.vector.tensor_scalar(xout[:, h, j, :], xin[:, h, j, :], mv[:, h, j, 0:1], rstd[:, h, j:j + 1],
                                                            ALU.subtract, ALU.mult)
                            k.then_inc(ln_done, 1)
                    dve.wait_ge(ptr_kept, 2 * NB)
                    nc.vector.tensor_copy(nxt_f[:], ptr_a[:]).then_inc(ptr_ready, 1)
                    dve.wait_ge(ptr_ready, 1)
                    nc.vector.tensor_scalar(same[:], nxt_f[:], float(NS), float(NS + NN), ALU.is_lt, ALU.mult).then_inc(ptr_ready, 1)
                    dve.wait_ge(ptr_ready, 2)
                    nc.vector.tensor_tensor(ptr_b[:], nxt_f[:], same[:], ALU.add).then_inc(ptr_ready, 1)

                @block.gpsimd
                def _(pool):
                    with pool.Fori(0, NB) as b:
                        for h in range(2):
                            pool.wait_ge(map_done[h], b * (16 * CH))
                            nc.gpsimd.tensor_copy(idx[:, h, :], scat[:, ds(b * R + h * CH, CH)]).then_inc(staged, 1)
                            nc.gpsimd.tensor_copy(val[:, h, :], slot_id[:, ds(b * R + h * CH, CH)]).then_inc(staged, 1)
                            pool.wait_ge(staged, b * 4 + 2 * h + 2)
                            pool.sem_inc(go, 1)
                            for j in range(CH):
                                nc.gpsimd.indirect_dma_start(slotmap, bass.IndirectOffsetOnAxis(ap=idx[:, h, j:j + 1], axis=0),
                                                             val[:, h, j:j + 1], None, bounds_check=N - 1,
                                                             oob_is_err=False).then_inc(map_done[h], 16)
                    for h in range(2):
                        pool.wait_ge(map_done[h], 16 * CH * NB)
                    with pool.Fori(0, NB) as b:
                        for h in range(2):
                            nc.gpsimd.tensor_copy(idx[:, h, :], src_s[:, ds(b * R + h * CH, CH)]).then_inc(staged, 1)
                            pool.wait_ge(staged, b * 2 + (4 * NB + h + 1))
                            pool.sem_inc(go, 1)
                            for j in range(CH):
                                nc.gpsimd.indirect_dma_start(val[:, h, j:j + 1], None, slotmap,
                                                             bass.IndirectOffsetOnAxis(ap=idx[:, h, j:j + 1], axis=0)).then_inc(ptr_in[h], 16)
                        for h in range(2):
                            pool.wait_ge(ptr_in[h], b * (16 * CH) + 16 * CH)
                            nc.gpsimd.tensor_copy(ptr_a[:, ds(b * R + h * CH, CH)], val[:, h, :]).then_inc(ptr_kept, 1)
                        pool.wait_ge(ptr_kept, b * 2 + 2)

        edge_attention(nc, state, fixed, ident, src_s, dst_s, w_s, cnt, wsum, x, ea_t, wkv, wq, we, sums, slot_rows(tab1))
        degrees(nc, cnt, wsum, step_a, dis_w)
        appnp(nc, state, fixed, ident, ptr_a, ptr_b, step_a, sums, slot_rows, w1, w2, w3, wa,
              (tab1, tab2, tab3, tab4, tab5), node_rows, out_rows)
        second_norm(nc, state, fixed, cnt, dis_w, dis_c, canon, slot_rows(tab2))
        layers = ((w1, tab2, tab3), (w2, tab3, tab4), (w3, tab4, tab5))
        for n, (w, tab, nxt_tab) in enumerate(layers):
            convolution(nc, n + 2, state, fixed, ident, ptr_a, w_s, dis_w, dis_c, scat, w, None, tab, sums,
                        slot_rows(nxt_tab), out)
        convolution(nc, 5, state, fixed, ident, ptr_a, w_s, dis_w, dis_c, scat, wb, wa, tab5, sums, None, out)


def edge_attention(nc, state, fixed, ident, src_s, dst_s, w_s, cnt, wsum, x, ea_t, wkv, wq, we, sums, tab_slots):
    with ExitStack() as c:
        sem = c.enter_context(semaphores(nc))
        def sb(name, shape, dt=F32):
            return c.enter_context(nc.sbuf_tensor(name, shape, dt))

        wkv_s, wq_s, we_s = sb("wkv_s", [D + 1, 2 * D]), sb("wq_s", [D + 1, D]), sb("we_s", [D + 1, D])
        idx = sb("idx_l0", [P, 2, 2, CH], I32)
        xs = sb("xs", [P, R, D])
        xd = sb("xd", [P, R, D])
        ea = sb("ea", [D + 1, 2, CH * P])
        s_in = sb("s_l0", [P, 2, CH * P])
        xt = sb("xt", [D + 1, 2, 2 * P])
        kvqe = sb("kvqe", [P, CH, 4 * D])
        prod = sb("prod", [P, CH, D])
        score = sb("score", [P, CH, HEADS])
        msg = sb("msg", [P, 2, CH, MSG])
        agg = sb("agg", [P, CH, MSG])
        zinv = sb("zinv", [P, CH, HEADS])
        deg = sb("deg", [P, CH])
        var = sb("var_l0", [P, CH])
        stats = sb("stats_l0", [P, CH, 6])
        mv = sb("mv_l0", [P, CH, 2])
        rstd = sb("rstd_l0", [P, CH])
        ps_t = [c.enter_context(nc.psum_tensor(f"ps_t{k}", [P, 512], F32)) for k in range(2)]
        ps_p = [c.enter_context(nc.psum_tensor(f"ps_p{k}", [P, 512], F32)) for k in range(2)]
        ps_s = [c.enter_context(nc.psum_tensor(f"ps_s{k}", [P, 512], F32)) for k in range(2)]

        const_in = sem("const_in")
        rows_in = [sem(f"l0_rows_in{i}") for i in range(R)]
        ea_in = [sem(f"l0_ea_in{h}") for h in range(2)]
        sm_in = [sem(f"l0_s_in{h}") for h in range(2)]
        staged, go = sem("l0_staged"), sem("l0_go")
        turned, turned_kept = sem("l0_turned"), sem("l0_turned_kept")
        projected, projected_kept = sem("l0_projected"), sem("l0_projected_kept")
        scored, exped, msg_ready = sem("l0_scored"), sem("l0_exped"), sem("l0_msg_ready")
        carry_kept = sem("l0_carry_kept")
        summed, sum_kept = sem("l0_summed"), sem("l0_sum_kept")
        posted, written = sem("l0_posted"), sem("l0_written")
        steps, var_ready, rstd_ready = sem("l0_steps"), sem("l0_var_ready"), sem("l0_rstd_ready")
        NCH = 2 * NB

        with nc.Block() as block:
            @block.sync
            def _(sp):
                for to, frm in ((wkv_s, wkv), (wq_s, wq), (we_s, we)):
                    sp.dma_start(to[:], frm).then_inc(const_in, 16)
                sp.wait_ge(const_in, 48)

            @block.vector
            def _(dve):
                nc.vector.memset(xt[D:D + 1, :, :], 1.0)
                nc.vector.memset(ea[D:D + 1, :, :], 1.0)
                nc.vector.memset(ps_s[1][0:1, :], 0.0)

        with nc.Block() as block:
            @block.sync
            def _(sp):
                def load_ea(cc, h):
                    sp.dma_start(ea[0:D, h, :], ea_t[:, ds(cc * (CH * P), CH * P)]).then_inc(ea_in[h], 16)

                def load_s(cc, h):
                    sp.dma_start(s_in[:, h, :], sums[:, ds(cc * (CH * P), CH * P)]).then_inc(sm_in[h], 16)

                for h in range(2):
                    load_ea(h, h)
                    load_s(h, h)
                sp.wait_ge(projected, CH)
                load_ea(2, 0)

                def turn(b, last):
                    for h in range(2):
                        if not last:
                            sp.wait_ge(projected, b * R + (h + 2) * CH)
                            load_ea(2 * b + 3 + h, 1 - h)
                            sp.wait_ge(summed, b * R + (h + 1) * CH)
                            load_s(2 * b + 2 + h, h)
                        sp.wait_ge(posted, 2 * b + h + 1)
                        sp.dma_start(tab_slots[:, ds(b * R + h * CH, CH), :], state[:, ds(b * R + h * CH, CH), :]).then_inc(written, 16)

                with sp.Fori(0, NB - 1) as b:
                    turn(b, False)
                turn(NB - 1, True)
                sp.wait_ge(written, 16 * NCH)
                sp.wait_ge(ea_in[0], 16 * (NB + 1))

            @block.gpsimd
            def _(pool):
                def turn(b, first):
                    for h in range(2):
                        if not first:
                            pool.wait_ge(turned_kept, b * R + (h - 1) * CH)
                        for k, of in enumerate((src_s, dst_s)):
                            nc.gpsimd.tensor_copy(idx[:, h, k, :], of[:, ds(b * R + h * CH, CH)]).then_inc(staged, 1)
                        pool.wait_ge(staged, b * 4 + 2 * h + 2)
                        pool.sem_inc(go, 1)
                        for j in range(CH):
                            for k, to in enumerate((xs, xd)):
                                nc.gpsimd.indirect_dma_start(to[:, h * CH + j, :], None, x,
                                                             bass.IndirectOffsetOnAxis(ap=idx[:, h, k, j:j + 1], axis=0)).then_inc(rows_in[h * CH + j], 16)

                turn(0, True)
                with pool.Fori(1, NB) as b:
                    turn(b, False)

            def turn_rows(pe, b, i):
                pe.wait_ge(rows_in[i], b * 32 + 32)
                nc.tensor.transpose(ps_t[i % 2][0:D, 0:P], xs[:, i, :], ident[:])
                nc.tensor.transpose(ps_t[i % 2][0:D, P:2 * P], xd[:, i, :], ident[:]).then_inc(turned, 1)

            def project(pe, b, i):
                h, j, n = i // CH, i % CH, b * R + i
                pe.wait_ge(turned_kept, n + 1)
                if j == 0:
                    pe.wait_ge(ea_in[h], b * 16 + 16)
                if not isinstance(n, int) or n > 1:
                    pe.wait_ge(projected_kept, n - 1)
                to = ps_p[i % 2]
                nc.tensor.matmul(to[:, 0:2 * D], xt[:, i % 2, 0:P], wkv_s[:], start=True, stop=True)
                nc.tensor.matmul(to[:, 2 * D:3 * D], xt[:, i % 2, P:2 * P], wq_s[:], start=True, stop=True)
                nc.tensor.matmul(to[:, 3 * D:4 * D], ea[:, h, j * P:(j + 1) * P], we_s[:], start=True, stop=True).then_inc(projected, 1)

            def sum_up(pe, b, i):
                h, j, n = i // CH, i % CH, b * R + i
                if j == 0:
                    pe.wait_ge(sm_in[h], b * 16 + 16)
                pe.wait_ge(carry_kept, n + 1)
                s = s_in[:, h, j * P:(j + 1) * P]
                pe.wait_ge(sum_kept, n - 1 if i else n)
                nc.tensor.matmul(ps_s[i % 2][:, 0:MSG], s, msg[:, h, j, :], start=True, stop=True).then_inc(summed, 1)

            @block.tensor
            def _(pe):
                def turn(b, last):
                    for h in range(2):
                        for j in range(CH):
                            ahead = (b, CH + j) if h == 0 else None if last else (b + 1, j)
                            if ahead:
                                turn_rows(pe, *ahead)
                            sum_up(pe, b, h * CH + j)
                            if ahead:
                                project(pe, *ahead)

                for j in range(CH):
                    turn_rows(pe, 0, j)
                    project(pe, 0, j)
                with pe.Fori(0, NB - 1) as b:
                    turn(b, False)
                turn(NB - 1, True)

            @block.scalar
            def _(act):
                def keep_turned(b, i):
                    n = b * R + i
                    act.wait_ge(turned, n + 1)
                    nc.scalar.copy(state[:, ds(n, 1), :], xd[:, i:i + 1, :])
                    nc.scalar.copy(xt[0:D, i % 2, :], ps_t[i % 2][0:D, 0:2 * P]).then_inc(turned_kept, 1)

                def keep_projection(b, i):
                    n = b * R + i
                    act.wait_ge(projected, n + 1)
                    if i % CH == 0:
                        act.wait_ge(msg_ready, b * 2 + i // CH)
                    nc.scalar.copy(kvqe[:, i % CH, :], ps_p[i % 2][:, 0:4 * D]).then_inc(projected_kept, 1)

                def exponent(b, h):
                    act.wait_ge(scored, b * 2 + h + 1)
                    nc.scalar.activation(score[:], score[:], ACT.Exp, scale=float(DH) ** -0.5).then_inc(exped, 1)

                def keep_sums(b, i):
                    h, j, n = i // CH, i % CH, b * R + i
                    if j == 0:
                        act.wait_ge(msg_ready, b * 2 + h + 1)
                    nc.scalar.copy(msg[0:1, h, j, :], ps_s[(i - 1) % 2][0:1, 0:MSG]).then_inc(carry_kept, 1)
                    if j == 0:
                        act.wait_ge(posted, b * 2 + h)
                    act.wait_ge(summed, n + 1)
                    nc.scalar.copy(agg[:, j, :], ps_s[i % 2][:, 0:MSG]).then_inc(sum_kept, 1)

                def root(b, h):
                    act.wait_ge(var_ready, b * 2 + h + 1)
                    nc.scalar.activation(rstd[:], var[:], ACT.Sqrt).then_inc(rstd_ready, 1)

                def turn(b, last):
                    for h in range(2):
                        for j in range(CH):
                            ahead = (b, CH + j) if h == 0 else None if last else (b + 1, j)
                            if ahead:
                                keep_turned(*ahead)
                            keep_sums(b, h * CH + j)
                            if ahead:
                                keep_projection(*ahead)
                        if ahead:
                            exponent(*((b, 1) if h == 0 else (b + 1, 0)))
                        root(b, h)

                for j in range(CH):
                    keep_turned(0, j)
                    keep_projection(0, j)
                exponent(0, 0)
                with act.Fori(0, NB - 1) as b:
                    turn(b, False)
                turn(NB - 1, True)

            @block.vector
            def _(dve):
                def scores(b, h, done):
                    dve.wait_ge(projected_kept, b * R + (h + 1) * CH)
                    done.up(nc.vector.tensor_tensor(prod[:], kvqe[:, :, 0:D], kvqe[:, :, 2 * D:3 * D], ALU.mult))
                    dve.wait_ge(steps, done.now())
                    done.up(nc.vector.tensor_tensor(prod[:], prod[:], kvqe[:, :, 3 * D:4 * D], ALU.mult))
                    dve.wait_ge(steps, done.now())
                    nc.vector.tensor_reduce(out=cols(score[:]), in_=prod[:].rearrange("p c (h d) -> p (c h) d", h=HEADS),
                                            axis=AX_X, op=ALU.add).then_inc(scored, 1)

                def messages(b, h, done):
                    dve.wait_ge(exped, b * 2 + h + 1)
                    done.up(nc.vector.tensor_scalar(msg[:, h, :, D:D + HEADS], score[:], E_LOW, E_HIGH, ALU.max, ALU.min))
                    done.up(nc.vector.memset(msg[:, h, :, D + HEADS:D + HEADS + 1], 1.0))
                    done.up(nc.vector.tensor_copy(msg[:, h, :, D + HEADS + 1], w_s[:, ds(b * R + h * CH, CH)]))
                    dve.wait_ge(steps, done.now())
                    nc.vector.tensor_tensor(per_head(msg[:, h, :, 0:D]), per_head(kvqe[:, :, D:2 * D]),
                                            every(msg[:, h, :, D:D + HEADS]), ALU.mult).then_inc(msg_ready, 1)

                def attend(b, h, done):
                    t = ds(b * R + h * CH, CH)
                    y = state[:, t, :]
                    dve.wait_ge(sum_kept, b * R + (h + 1) * CH)
                    done.up(nc.vector.tensor_scalar(zinv[:], agg[:, :, D:D + HEADS], 1e-6, None, ALU.add))
                    done.up(nc.vector.tensor_copy(cnt[:, t], agg[:, :, D + HEADS]))
                    done.up(nc.vector.tensor_copy(wsum[:, t], agg[:, :, D + HEADS + 1]))
                    done.up(nc.vector.tensor_scalar(deg[:], agg[:, :, D + HEADS], 1.0, None, ALU.add))
                    dve.wait_ge(steps, done.now())
                    done.up(nc.vector.reciprocal(zinv[:], zinv[:]))
                    dve.wait_ge(steps, done.now())
                    done.up(nc.vector.tensor_tensor(per_head(prod[:]), per_head(agg[:, :, 0:D]), every(zinv[:]), ALU.mult))
                    dve.wait_ge(steps, done.now())
                    done.up(nc.vector.tensor_tensor(y, y, prod[:], ALU.add))
                    dve.wait_ge(steps, done.now())
                    done.up(dve)
                    row_moments(dve, done, [cols(state[:, ds(b * R + h * CH + j, 1), :]) for j in range(CH)], stats, mv)
                    done.up(nc.vector.scalar_tensor_tensor(out=var[:], in0=mv[:, :, 1], scalar=EPS, in1=deg[:], op0=ALU.add, op1=ALU.mult))
                    dve.wait_ge(steps, done.now())
                    nc.vector.reciprocal(var[:], var[:]).then_inc(var_ready, 1)

                def new_state(b, h):
                    t = ds(b * R + h * CH, CH)
                    dve.wait_ge(rstd_ready, 2 * b + h + 1)
                    for j in range(CH):
                        one = state[:, ds(b * R + h * CH + j, 1), :]
                        k = nc.vector.tensor_scalar(one, one, mv[:, j, 0:1], rstd[:, j:j + 1], ALU.subtract, ALU.mult)
                    k.then_inc(posted, 1)
                    dve.wait_ge(posted, 2 * b + h + 1)
                    nc.vector.tensor_scalar(fixed[:, t, :], state[:, t, :], ALPHA, None, ALU.mult)

                per_turn = 2 * (5 + 10 + 2 * CH)
                before = Count(steps, 0, 0)

                def turn(b, last):
                    done = Count(steps, b, per_turn)
                    done.n = before.n
                    for h in range(2):
                        ahead = (b, 1) if h == 0 else None if last else (b + 1, 0)
                        if ahead:
                            scores(*ahead, done)
                        attend(b, h, done)
                        if ahead:
                            messages(*ahead, done)
                        new_state(b, h)
                    return done

                scores(0, 0, before)
                messages(0, 0, before)
                with dve.Fori(0, NB - 1) as b:
                    assert turn(b, False).n == before.n + per_turn
                turn(NB - 1, True)


E_LOW, E_HIGH = 0.006737946999085467, 148.4131591025766


def degrees(nc, cnt, wsum, step_a, dis_w):
    with semaphores(nc) as sem, nc.Block() as block:
        steps, inverse = sem("deg_steps"), sem("deg_inverse")

        @block.scalar
        def _(act):
            act.wait_ge(inverse, 1)
            nc.scalar.activation(dis_w[:], wsum[:], ACT.Sqrt)

        @block.vector
        def _(dve):
            nc.vector.tensor_scalar(cnt[:], cnt[:], 1.0, None, ALU.add).then_inc(steps, 1)
            nc.vector.tensor_scalar(wsum[:], wsum[:], 1.0, None, ALU.add).then_inc(steps, 1)
            dve.wait_ge(steps, 2)
            nc.vector.reciprocal(step_a[:], cnt[:]).then_inc(steps, 1)
            nc.vector.reciprocal(wsum[:], wsum[:]).then_inc(inverse, 1)
            dve.wait_ge(steps, 3)
            nc.vector.tensor_scalar(step_a[:], step_a[:], 1.0 - ALPHA, None, ALU.mult).then_inc(steps, 1)


def appnp(nc, state, fixed, ident, ptr_a, ptr_b, step_a, sums, slot_rows, w1, w2, w3, wa, tabs, node_rows, out_rows):
    BANKS = 5
    RB = 2 * R
    NBB = T // RB
    CARRIES = RB + 1
    NJ = NQ // JW
    JOBS = JOB_STEPS * NBB
    W = JW * P
    tab1, tab2, tab3, tab4, tab5 = tabs
    with ExitStack() as c:
        sem = c.enter_context(semaphores(nc))

        def sb(name, shape, dt=F32):
            return c.enter_context(nc.sbuf_tensor("n_" + name, shape, dt))

        g = sb("g", [P, R, D])
        s_in = sb("s", [P, 2, CH * P])
        idx = sb("idx", [P, 2, CH], I32)
        hold = sb("hold", [1, D])
        own = sb("own", [P, P])
        w1_s, w2_s, w3_s, wa_s = (sb(k, [D + 1, D]) for k in ("w1", "w2", "w3", "wa"))
        x1, x2, h1, h2, y3, x3, y4, res = (sb(k, [P, JW, D]) for k in ("x1", "x2", "h1", "h2", "y3", "x3", "y4", "res"))
        x2t, h1t, h2t, x3t = (sb(k, [D + 1, W]) for k in ("x2t", "h1t", "h2t", "x3t"))
        stats, mv, var, rstd = sb("stats", [P, JW, 6]), sb("mv", [P, 3, JW, 2]), sb("var", [P, 3, JW]), sb("rstd", [P, 3, JW])
        ps = [c.enter_context(nc.psum_tensor(f"l1_ps{k}", [P, 512], F32)) for k in range(BANKS)]
        ps_a, ps_b, ps_c = (c.enter_context(nc.psum_tensor(f"n_ps_{k}", [P, 512], F32)) for k in "abc")

        rows_in = [sem(f"l1_rows_in{i}") for i in range(R)]
        s_landed = [sem(f"l1_s_in{h}") for h in range(2)]
        staged, go, turns = sem("l1_staged"), sem("l1_go"), sem("l1_turns")
        carried, summed = sem("l1_carried"), sem("l1_summed")
        freed = sem("l1_freed")
        written = sem("l1_written")
        const_in, x1_in, own_set = sem("n_const_in"), sem("n_x1_in"), sem("own_set")
        outs = {k: sem(f"n_{k}_out") for k in ("x2", "h1", "h2", "x3", "res")}
        ready = {k: sem(f"n_{k}_ready") for k in ("x2", "h1", "h2", "x3", "res")}
        steps = sem("n_steps")
        var_ready, rstd_ready = ([sem(f"n_{k}{m}") for m in range(3)] for k in ("var_ready", "rstd_ready"))
        turned, turned_kept = ({x_: sem(f"n_{x_}_{k}") for x_ in ("x2", "x3")} for k in ("turned", "turned_kept"))
        wide, wide_kept = ({x_: sem(f"n_{x_}_{k}") for x_ in ("h1", "h2")} for k in ("wide", "wide_kept"))
        narrow = {k: sem(f"n_{k}_narrow") for k in ("h1", "h2", "y3", "y4")}
        added = sem("n_added")
        prime = sb("prime", [1, 6, 8])

        with nc.Block() as block:
            @block.sync
            def _(sp):
                for to, frm in ((w1_s, w1), (w2_s, w2), (w3_s, w3), (wa_s, wa)):
                    sp.dma_start(to[:], frm).then_inc(const_in, 16)
                sp.wait_ge(const_in, 64)
                for k, out in enumerate((*outs.values(), written)):
                    sp.dma_start(prime[:, k], w1[0:1, 0:8]).then_inc(out, 16)
                    sp.wait_ge(out, 16)

            @block.vector
            def _(dve):
                nc.vector.memset(hold[:], 0.0)
                nc.vector.tensor_copy(own[:], ident[:]).then_inc(own_set, 1)
                dve.wait_ge(own_set, 1)
                nc.vector.memset(own[0:1, 0:1], 0.0)
                for a in (x2t, h1t):
                    nc.vector.memset(a[D:D + 1, :], 1.0)
                for a in (h2t, x3t, x2, x3):
                    nc.vector.memset(a[:], 1.0)
                dve.sem_inc(freed, R)
                for k in (ready["h2"], wide_kept["h2"], turned_kept["x3"]):
                    dve.sem_inc(k, 1)

        def passes(eng, one):
            for first, last, job in ((0, JOB_STEPS // 2, True), (JOB_STEPS // 2, STEPS // 2, False)):
                with eng.Fori(first, last) as pair:
                    for odd in range(2):
                        one(pair, odd, job)

        with nc.Block() as block:
            @block.sync
            def _(sp):
                def load_s(cc, h):
                    sp.dma_start(s_in[:, h, :], sums[:, ds(cc * (CH * P), CH * P)]).then_inc(s_landed[h], 16)

                def store(J, lag, name, frm, to):
                    sp.wait_ge(ready[name], J + (2 if name == "h2" else 1))
                    sp.sem_inc(turns, 1)
                    sp.dma_start(to[:, ds((J + (NJ - lag)) % NJ * JW, JW), :], frm[:]).then_inc(outs[name], 16)

                def one(pair, odd, job):
                    to = slot_rows(tab1, 0 if odd else NS + NN)

                    def slots(b, q):
                        n0, h = pair * (2 * T) + b * RB + odd * T, q % 2
                        sp.wait_ge(summed, n0 + CH * (q + 1))
                        load_s(4 * b + 2 + q, h)
                        sp.wait_ge(freed, n0 + (R + CH * (q + 1)))
                        t = ds(b * RB + CH * q, CH)
                        sp.dma_start(to[:, t, :], state[:, t, :]).then_inc(written, 16)

                    with sp.Fori(0, NBB) as b:
                        J = pair * (2 * NBB) + b + odd * NBB
                        slots(b, 0)
                        if job:
                            store(J, 0, "x2", x2, node_rows(tab2))
                            sp.dma_start(x1[:], x1_rows[:, ds((J + 1) % NJ * JW, JW), :]).then_inc(x1_in, 16)
                        slots(b, 1)
                        if job:
                            store(J, 1, "x3", x3, node_rows(tab5))
                        slots(b, 2)
                        if job:
                            store(J, 2, "res", res, out_rows)
                            store(J, 0, "h1", h1, node_rows(tab3))
                        slots(b, 3)
                        if job:
                            store(J, 0, "h2", h2, node_rows(tab4))

                x1_rows = node_rows(tab1)
                for h in range(2):
                    load_s(h, h)
                sp.dma_start(x1[:], x1_rows[:, 0:JW, :]).then_inc(x1_in, 16)
                passes(sp, one)
                sp.wait_ge(written, 16 * 2 * NB * STEPS + 16)
                for h in range(2):
                    sp.wait_ge(s_landed[h], 16 * (NB * STEPS + 1))
                sp.wait_ge(x1_in, 16 * (JOBS + 1))
                for out in outs.values():
                    sp.wait_ge(out, 16 * (JOBS + 1))

            @block.gpsimd
            def _(pool):
                with pool.Fori(0, STEPS // 2) as pair:
                    for odd in range(2):
                        pool.wait_ge(written, pair * (64 * NB) + (odd * 32 * NB + 16))
                        pool.sem_inc(go, 1)
                        with pool.Fori(0, NB) as b:
                            n0 = pair * (2 * T) + b * R + odd * T
                            for h in range(2):
                                pool.wait_ge(freed, n0 + CH * (h + 1))
                                nc.gpsimd.tensor_copy(idx[:, h, :], (ptr_b if odd else ptr_a)[:, ds(b * R + h * CH, CH)]).then_inc(staged, 1)
                                pool.wait_ge(staged, pair * (4 * NB) + b * 2 + (odd * 2 * NB + h + 1))
                                pool.sem_inc(go, 1)
                                for j in range(CH):
                                    nc.gpsimd.indirect_dma_start(g[:, h * CH + j, :], None, tab1 if odd else tab1[0:NS + NN, :],
                                                                 bass.IndirectOffsetOnAxis(ap=idx[:, h, j:j + 1], axis=0)).then_inc(rows_in[h * CH + j], 16)

            @block.tensor
            def _(pe):
                def slots(pair, odd, b, i, job):
                    h, j, turn = i // CH % 2, i % CH, pair * (2 * NBB) + b + odd * NBB
                    if j == 0:
                        pe.wait_ge(s_landed[h], turn * 32 + (i // R * 16 + 16))
                    pe.wait_ge(freed, turn * RB + (i + 1 + R - BANKS))
                    to = ps[i % BANKS][:, 0:D]
                    nc.tensor.matmul(to, own[:], cols(state[:, ds(b * RB + i, 1), :]), start=True, stop=False)
                    if job:
                        nodes(turn, i)
                    pe.wait_ge(carried, turn * CARRIES + (i + 1))
                    nc.tensor.matmul(to, s_in[:, h, j * P:(j + 1) * P], g[:, i % R, :], start=False, stop=True).then_inc(summed, 1)

                def turn_rows(name, frm, half):
                    for j in range(half * JW // 2, (half + 1) * JW // 2):
                        m = nc.tensor.transpose(ps_a[0:D, j * P:(j + 1) * P], frm[:, j, :], ident[:])
                    if half:
                        m.then_inc(turned[name], 1)

                def across(name, frm, w, half):
                    at = slice(half * W // 2, (half + 1) * W // 2)
                    m = nc.tensor.matmul(ps_b[0:D, at], w[:], frm[:, at], start=True, stop=True)
                    if half:
                        m.then_inc(wide[name], 1)

                def rows(name, frm, w, half):
                    for j in range(half * JW // 2, (half + 1) * JW // 2):
                        m = nc.tensor.matmul(ps_c[:, j * D:(j + 1) * D], frm[:, j * P:(j + 1) * P], w[:], start=True, stop=True)
                    if half:
                        m.then_inc(narrow[name], 1)

                def nodes(J, i):
                    if i == 3:
                        pe.wait_ge(wide_kept["h2"], J + 1)
                        pe.wait_ge(ready["h2"], J + 1)
                    if i in (3, 4):
                        rows("y3", h2t, w3_s, i - 3)
                    if i == 8:
                        pe.wait_ge(turned_kept["x3"], J + 1)
                        pe.wait_ge(added, J * 2 + 1)
                    if i in (8, 9):
                        rows("y4", x3t, wa_s, i - 8)
                    if i == 10:
                        pe.wait_ge(ready["x2"], J + 1)
                    if i in (10, 11):
                        turn_rows("x2", x2, i - 10)
                    if i == 13:
                        pe.wait_ge(turned_kept["x2"], J + 1)
                        pe.wait_ge(added, J * 2 + 2)
                    if i in (13, 14):
                        across("h1", x2t, w1_s, i - 13)
                        rows("h1", x2t, w1_s, i - 13)
                    if i == 15:
                        pe.wait_ge(ready["x3"], J + 1)
                    if i in (15, 16):
                        turn_rows("x3", x3, i - 15)
                    if i == 16:
                        pe.wait_ge(wide_kept["h1"], J + 1)
                    if i in (16, 17):
                        across("h2", h1t, w2_s, i - 16)
                    if i == 18:
                        pe.wait_ge(ready["h1"], J + 1)
                    if i in (18, 19):
                        rows("h2", h1t, w2_s, i - 18)

                def one(pair, odd, job):
                    with pe.Fori(0, NBB) as b:
                        for i in range(RB):
                            slots(pair, odd, b, i, job)

                passes(pe, one)

            @block.scalar
            def _(act):
                def slots(pair, odd, b, i):
                    turn = pair * (2 * NBB) + b + odd * NBB
                    act.wait_ge(rows_in[i % R], turn * 32 + (i // R * 16 + 16))
                    if i:
                        act.wait_ge(summed, turn * RB + i)
                    nc.scalar.copy(g[0:1, i % R, :], ps[(i - 1) % BANKS][0:1, 0:D] if i else hold[:]).then_inc(carried, 1)

                def nodes(J, i):
                    if i in (4, 8, 13):
                        k = (4, 8, 13).index(i)
                        act.wait_ge(var_ready[k], J + 1)
                        nc.scalar.activation(rstd[:, k, :], var[:, k, :], ACT.Sqrt).then_inc(rstd_ready[k], 1)
                    elif i in (12, 17):
                        name, to = ("x2", x2t) if i == 12 else ("x3", x3t)
                        act.wait_ge(turned[name], J + 1)
                        nc.scalar.copy(to[0:D, :], ps_a[0:D, 0:W]).then_inc(turned_kept[name], 1)
                    elif i in (15, 18):
                        name, to = ("h1", h1t) if i == 15 else ("h2", h2t)
                        act.wait_ge(wide[name], J + 1)
                        nc.scalar.activation(to[0:D, :], ps_b[0:D, 0:W], ACT.Relu).then_inc(wide_kept[name], 1)

                def one(pair, odd, job):
                    with act.Fori(0, NBB) as b:
                        for i in range(RB):
                            slots(pair, odd, b, i)
                            if job:
                                nodes(pair * (2 * NBB) + b + odd * NBB, i)
                        act.wait_ge(summed, pair * (2 * T) + b * RB + (odd * T + RB))
                        nc.scalar.copy(hold[:], ps[(RB - 1) % BANKS][0:1, 0:D]).then_inc(carried, 1)
                        act.wait_ge(carried, (pair * (2 * NBB) + b + (odd * NBB + 1)) * CARRIES)

                passes(act, one)

            @block.vector
            def _(dve):
                def slots(pair, odd, b, i):
                    t, turn = ds(b * RB + i, 1), pair * (2 * NBB) + b + odd * NBB
                    dve.wait_ge(carried, turn * CARRIES + (i + 2))
                    nc.vector.scalar_tensor_tensor(out=state[:, t, :], in0=ps[i % BANKS][:, 0:D].rearrange("p (a d) -> p a d", a=1),
                                                   scalar=step_a[:, t], in1=fixed[:, t, :], op0=ALU.mult, op1=ALU.add).then_inc(freed, 1)

                def moments(k, done, of, eps):
                    row_moments(dve, done, [of[:, j, :] for j in range(JW)], stats, mv[:, k])
                    done.up(nc.vector.tensor_scalar(var[:, k, :], mv[:, k, :, 1], eps, None, ALU.add))
                    dve.wait_ge(steps, done.now())
                    nc.vector.reciprocal(var[:, k, :], var[:, k, :]).then_inc(var_ready[k], 1)

                def normed(J, k, frm, to, name):
                    dve.wait_ge(outs[name], J * 16 + 16)
                    dve.wait_ge(rstd_ready[k], J + 1)
                    for j in range(JW):
                        m = nc.vector.tensor_scalar(to[:, j, :], frm[:, j, :], mv[:, k, j, 0:1], rstd[:, k, j:j + 1], ALU.subtract, ALU.mult)
                    m.then_inc(ready[name], 1)

                def rectified(J, to, name):
                    dve.wait_ge(outs[name], J * 16 + 16)
                    dve.wait_ge(narrow[name], J + 1)
                    nc.vector.tensor_scalar(cols(to[:]), ps_c[:, 0:JW * D], 0.0, None, ALU.max).then_inc(ready[name], 1)

                def residual(J, k, x_, to, name, done):
                    dve.wait_ge(narrow[name], J + 1)
                    nc.vector.tensor_tensor(cols(to[:]), cols(x_[:]), ps_c[:, 0:JW * D], ALU.add).then_inc(added, 1)
                    dve.wait_ge(added, J * 2 + k)
                    done.up(dve)
                    moments(k, done, to, EPS)

                per_job = 3 * (2 * JW + 2) + 2

                def nodes(J, i, done):
                    if i == 0:
                        dve.wait_ge(x1_in, J * 16 + 16)
                        moments(0, done, x1, EPS / 4)
                    elif i == 4:
                        residual(J, 1, x2, y3, "y3", done)
                    elif i == 5:
                        normed(J, 0, x1, x2, "x2")
                    elif i == 9:
                        residual(J, 2, x3, y4, "y4", done)
                    elif i == 10:
                        normed(J, 1, y3, x3, "x3")
                    elif i == 13:
                        normed(J, 2, y4, res, "res")
                    elif i == 14:
                        rectified(J, h1, "h1")
                    elif i == 19:
                        rectified(J, h2, "h2")

                def one(pair, odd, job):
                    with dve.Fori(0, NBB) as b:
                        J = pair * (2 * NBB) + b + odd * NBB
                        done = Count(steps, J, per_job)
                        for i in range(RB):
                            slots(pair, odd, b, i)
                            if job:
                                nodes(J, i, done)
                        assert not job or done.n == per_job, done.n

                passes(dve, one)


def second_norm(nc, state, fixed, cnt, dis_w, dis_c, canon, tab_slots):
    with ExitStack() as c:
        sem = c.enter_context(semaphores(nc))
        y = c.enter_context(nc.sbuf_tensor("m_y", [P, 2, CH, D], F32))
        stats = c.enter_context(nc.sbuf_tensor("m_stats", [P, 2, CH, 6], F32))
        mv = c.enter_context(nc.sbuf_tensor("m_mv", [P, 2, CH, 2], F32))
        var = c.enter_context(nc.sbuf_tensor("m_var", [P, 2, CH], F32))
        rstd = c.enter_context(nc.sbuf_tensor("m_rstd", [P, 2, CH], F32))
        steps, var_ready, rstd_ready, normed = sem("m_steps"), sem("m_var_ready"), sem("m_rstd_ready"), sem("m_normed")
        masked, scaled, written = sem("m_masked"), sem("m_scaled"), sem("m_written")
        with nc.Block() as block:
            @block.sync
            def _(sp):
                with sp.Fori(0, NB) as b:
                    for h in range(2):
                        t = ds(b * R + h * CH, CH)
                        sp.wait_ge(scaled, 2 * b + h + 1)
                        sp.dma_start(tab_slots[:, t, :], state[:, t, :]).then_inc(written, 16)
                sp.wait_ge(written, 32 * NB)

            @block.scalar
            def _(act):
                act.wait_ge(masked, 1)
                with act.Fori(0, NB) as b:
                    for h in range(2):
                        act.wait_ge(var_ready, 2 * b + h + 1)
                        nc.scalar.activation(rstd[:, h, :], var[:, h, :], ACT.Sqrt).then_inc(rstd_ready, 1)
                    for h in range(2):
                        act.wait_ge(normed, 2 * b + h + 1)
                        for j in range(CH):
                            t = ds(b * R + h * CH + j, 1)
                            k = nc.scalar.activation(state[:, t, :], fixed[:, t, :], ACT.Copy, scale=dis_c[:, t])
                        k.then_inc(scaled, 1)

            @block.vector
            def _(dve):
                nc.vector.tensor_tensor(dis_c[:], dis_w[:], canon[:], ALU.mult).then_inc(masked, 1)
                per_turn = 2 * (1 + 2 * CH + 1 + 3)
                with dve.Fori(0, NB) as b:
                    done = Count(steps, b, per_turn)
                    for h in range(2):
                        t = ds(b * R + h * CH, CH)
                        dve.wait_ge(normed, 2 * b)
                        done.up(nc.vector.scalar_tensor_tensor(out=cols(y[:, h]), in0=cols(fixed[:, t, :]), scalar=1.0 / ALPHA, in1=cols(state[:, t, :]),
                                                               op0=ALU.mult, op1=ALU.add))
                        dve.wait_ge(steps, done.now())
                        row_moments(dve, done, [y[:, h, j, :] for j in range(CH)], stats[:, h], mv[:, h])
                        done.up(nc.vector.tensor_tensor(var[:, h, :], mv[:, h, :, 1], cnt[:, t], ALU.mult))
                        dve.wait_ge(steps, done.now())
                        done.up(nc.vector.tensor_scalar(var[:, h, :], var[:, h, :], EPS, None, ALU.add))
                        dve.wait_ge(steps, done.now())
                        done.up(nc.vector.reciprocal(var[:, h, :], var[:, h, :]))
                        dve.wait_ge(steps, done.now())
                        nc.vector.tensor_tensor(var[:, h, :], var[:, h, :], cnt[:, t], ALU.mult).then_inc(var_ready, 1)
                    for h in range(2):
                        dve.wait_ge(rstd_ready, 2 * b + h + 1)
                        for j in range(CH):
                            k = nc.vector.tensor_scalar(fixed[:, ds(b * R + h * CH + j, 1), :], y[:, h, j:j + 1, :], mv[:, h, j, 0:1],
                                                        rstd[:, h, j:j + 1], ALU.subtract, ALU.mult)
                        k.then_inc(normed, 1)
                    assert done.n == per_turn, done.n


def convolution(nc, layer, state, fixed, ident, ptr_a, w_s, dis_w, dis_c, scat, w, wa, tab, sums, tab_next, out):
    inner, final = layer < 4, layer == 5
    with ExitStack() as c:
        sem = c.enter_context(semaphores(nc))
        def sb(name, shape, dt=F32):
            return c.enter_context(nc.sbuf_tensor(f"c{layer}_{name}", shape, dt))

        def s(name):
            return sem(f"c{layer}_{name}")

        w_in = sb("w", [D, D])
        bias = sb("bias", [P, D])
        wa_in = sb("wa", [D + 1, D])
        g = sb("g", [P, R, D])
        gw = sb("gw", [P, R, D])
        s_in = sb("s", [P, 2, CH * P])
        idx = sb("idx", [P, 2, CH], I32)
        scat_idx = sb("scat_idx", [P, 2, CH], I32)
        at = sb("at", [D, 2, P])
        own = sb("own", [P, 2, D])
        own_t = sb("own_t", [D + 1, 2, P])
        y = sb("y", [P, CH, D])
        tmp = sb("tmp", [P, 2, D])
        prime = sb("prime", [1, 2, 8])
        res = sb("res", [P, 2, CH, D])
        stats, mv = sb("stats", [P, CH, 6]), sb("mv", [P, CH, 2])
        var, rstd = sb("var", [P, CH]), sb("rstd", [P, CH])
        ps_t = [c.enter_context(nc.psum_tensor(f"c{layer}_ps_t{k}", [P, 512], F32)) for k in range(2)]
        ps_w = [c.enter_context(nc.psum_tensor(f"c{layer}_ps_w{k}", [P, 512], F32)) for k in range(2)]
        pc = [c.enter_context(nc.psum_tensor(f"c{layer}_pc{k}", [P, 512], F32)) for k in range(2)]
        ps_o = [c.enter_context(nc.psum_tensor(f"c{layer}_ps_o{k}", [P, 512], F32)) for k in range(2)]
        const_in = s("const_in")
        rows_in = [s(f"rows_in{i}") for i in range(R)]
        s_landed = [s(f"s_in{h}") for h in range(2)]
        staged, go = s("staged"), s("go")
        weighted, carry_out, carry_kept = s("weighted"), s("carry_out"), s("carry_kept")
        summed, sum_kept, own_kept, own_turned, own_t_kept = s("summed"), s("sum_kept"), s("own_kept"), s("own_turned"), s("own_t_kept")
        mapped, posted, steps = s("mapped"), s("posted"), s("steps")
        var_ready, rstd_ready, written = s("var_ready"), s("rstd_ready"), s("written")
        scat_staged = s("scat_staged")
        scattered = [s(f"scattered{h}") for h in range(2)]
        freed, chunk_done = s("freed"), s("chunk_done")

        with nc.Block() as block:
            @block.sync
            def _(sp):
                sp.dma_start(w_in[:], w[0:D, :]).then_inc(const_in, 16)
                if final:
                    sp.dma_start(wa_in[:], wa).then_inc(const_in, 16)
                else:
                    sp.dma_start(bias[:], w[D:D + 1, :].broadcast_to([P, D])).then_inc(const_in, 16)
                sp.wait_ge(const_in, 32)

            if final:
                @block.gpsimd
                def _(pool):
                    for h in range(2):
                        pool.dma_start(prime[:, h], w[0:1, 0:8]).then_inc(scattered[h], 16)
                        pool.wait_ge(scattered[h], 16)

            @block.vector
            def _(dve):
                nc.vector.memset(pc[1][0:1, :], 0.0)
                nc.vector.memset(own_t[D:D + 1, :, :], 1.0)
                dve.sem_inc(freed, 2)

        with nc.Block() as block:
            @block.sync
            def _(sp):
                def load_s(cc, h):
                    sp.dma_start(s_in[:, h, :], sums[:, ds(cc * (CH * P), CH * P)]).then_inc(s_landed[h], 16)

                for h in range(2):
                    load_s(h, h)
                with sp.Fori(0, NB) as b:
                    for h in range(2):
                        t = ds(b * R + CH * h, CH)
                        sp.wait_ge(summed, b * R + CH * (h + 1))
                        load_s(2 * b + 2 + h, h)
                        if not final:
                            sp.wait_ge(chunk_done, 2 * b + (h + 1))
                            sp.dma_start(tab_next[:, t, :], state[:, t, :]).then_inc(written, 16)
                if not final:
                    sp.wait_ge(written, 32 * NB)
                for h in range(2):
                    sp.wait_ge(s_landed[h], 16 * (NB + 1))

            @block.gpsimd
            def _(pool):
                def scatter(b, h):
                    pool.wait_ge(scattered[h], b * (16 * CH) + 16)
                    nc.gpsimd.tensor_copy(scat_idx[:, h, :], scat[:, ds(b * R + h * CH, CH)]).then_inc(scat_staged, 1)
                    pool.wait_ge(scat_staged, 2 * b + h + 1)
                    pool.wait_ge(chunk_done, 2 * b + (h + 1))
                    pool.sem_inc(go, 1)
                    for j in range(CH):
                        nc.gpsimd.indirect_dma_start(out, bass.IndirectOffsetOnAxis(ap=scat_idx[:, h, j:j + 1], axis=0), res[:, h, j, :], None,
                                                     bounds_check=N - 1, oob_is_err=False).then_inc(scattered[h], 16)

                def gather(b, h, first):
                    if not first:
                        pool.wait_ge(weighted, b * R + (h - 1) * CH)
                    nc.gpsimd.tensor_copy(idx[:, h, :], ptr_a[:, ds(b * R + h * CH, CH)]).then_inc(staged, 1)
                    pool.wait_ge(staged, b * 2 + (h + 1))
                    pool.sem_inc(go, 1)
                    for j in range(CH):
                        nc.gpsimd.indirect_dma_start(g[:, h * CH + j, :], None, tab,
                                                     bass.IndirectOffsetOnAxis(ap=idx[:, h, j:j + 1], axis=0)).then_inc(rows_in[h * CH + j], 16)

                for h in range(2):
                    gather(0, h, True)
                with pool.Fori(1, NB) as b:
                    for h in range(2):
                        gather(b, h, False)
                        if final:
                            scatter(b - 1, h)
                if final:
                    for h in range(2):
                        scatter(NB - 1, h)
                    for h in range(2):
                        pool.wait_ge(scattered[h], 16 * CH * NB + 16)

            @block.tensor
            def _(pe):
                def total(b, i):
                    h, j, n = i // CH, i % CH, b * R + i
                    if j == 0:
                        pe.wait_ge(s_landed[h], b * 16 + 16)
                    if final:
                        pe.wait_ge(own_kept, n + 1)
                        nc.tensor.transpose(ps_o[i % 2][0:D, 0:P], own[:, i % 2, :], ident[:]).then_inc(own_turned, 1)
                    m = s_in[:, h, j * P:(j + 1) * P]
                    pe.wait_ge(carry_kept, n + 1)
                    nc.tensor.matmul(pc[i % 2][0:1, 0:D], m[:, 0:1], gw[:, i, :], start=True, stop=True).then_inc(carry_out, 1)
                    if i > 1:
                        pe.wait_ge(sum_kept, n - 1)
                    nc.tensor.matmul(ps_t[i % 2][0:D, 0:P], gw[:, i, :], m, start=True, stop=True).then_inc(summed, 1)

                def linear(b, i):
                    n = b * R + i
                    pe.wait_ge(freed, n + 1)
                    pe.wait_ge(sum_kept, n + 1)
                    if final:
                        pe.wait_ge(own_t_kept, n + 1)
                        nc.tensor.matmul(ps_w[i % 2][:, 0:D], own_t[:, i % 2, :], wa_in[:], start=True, stop=False)
                    nc.tensor.matmul(ps_w[i % 2][:, 0:D], at[:, i % 2, :], w_in[:], start=not final, stop=True).then_inc(mapped, 1)

                with pe.Fori(0, NB) as b:
                    for i in range(R):
                        total(b, i)
                        if i:
                            linear(b, i - 1)
                    linear(b, R - 1)

            @block.scalar
            def _(act):
                def keep(b, i):
                    n = b * R + i
                    if i > 1:
                        act.wait_ge(mapped, n - 1)
                    act.wait_ge(summed, n + 1)
                    nc.scalar.copy(at[:, i % 2, :], ps_t[i % 2][0:D, 0:P]).then_inc(sum_kept, 1)
                    if final:
                        act.wait_ge(own_turned, n + 1)
                        nc.scalar.copy(own_t[0:D, i % 2, :], ps_o[i % 2][0:D, 0:P]).then_inc(own_t_kept, 1)

                def root(b, h):
                    act.wait_ge(var_ready, 2 * b + h + 1)
                    nc.scalar.activation(rstd[:], var[:], ACT.Sqrt).then_inc(rstd_ready, 1)

                with act.Fori(0, NB) as b:
                    for i in range(R):
                        n = b * R + i
                        if final:
                            if i > 1:
                                act.wait_ge(own_turned, n - 1)
                            nc.scalar.copy(own[:, i % 2, :], cols(state[:, ds(n, 1), :])).then_inc(own_kept, 1)
                        act.wait_ge(weighted, n + 1)
                        act.wait_ge(carry_out, n)
                        nc.scalar.copy(gw[0:1, i, :], pc[(i - 1) % 2][0:1, 0:D]).then_inc(carry_kept, 1)
                        if i:
                            keep(b, i - 1)
                        if not inner and i == CH:
                            root(b, 0)
                    keep(b, R - 1)
                    if not inner:
                        root(b, 1)

            @block.vector
            def _(dve):
                def weigh(b, i):
                    n = b * R + i
                    dve.wait_ge(rows_in[i], b * 16 + 16)
                    if final:
                        k = nc.vector.tensor_scalar(gw[:, i:i + 1, :], g[:, i:i + 1, :], w_s[:, ds(n, 1)], None, ALU.mult)
                    else:
                        k = nc.vector.scalar_tensor_tensor(out=gw[:, i:i + 1, :], in0=g[:, i:i + 1, :], scalar=w_s[:, ds(n, 1)],
                                                           in1=state[:, ds(n, 1), :], op0=ALU.mult, op1=ALU.add)
                    k.then_inc(weighted, 1)

                def take(b, i, done):
                    h, j, n = i // CH, i % CH, b * R + i
                    t = ds(n, 1)
                    got = ps_w[i % 2][:, 0:D].rearrange("p (a d) -> p a d", a=1)
                    dve.wait_ge(mapped, n + 1)
                    if final:
                        nc.vector.tensor_tensor(y[:, j:j + 1, :], got, state[:, t, :], ALU.add).then_inc(freed, 1)
                        return
                    nc.vector.scalar_tensor_tensor(out=tmp[:, i % 2:i % 2 + 1, :], in0=got, scalar=dis_w[:, t],
                                                   in1=bias[:].rearrange("p (a d) -> p a d", a=1), op0=ALU.mult, op1=ALU.add).then_inc(freed, 1)
                    dve.wait_ge(freed, n + 3)
                    if inner:
                        k = nc.vector.tensor_scalar(state[:, t, :], tmp[:, i % 2:i % 2 + 1, :], 0.0, dis_c[:, t], ALU.max, ALU.mult)
                        if j == CH - 1:
                            k.then_inc(chunk_done, 1)
                    else:
                        done.up(nc.vector.tensor_tensor(y[:, j:j + 1, :], tmp[:, i % 2:i % 2 + 1, :], fixed[:, t, :], ALU.add))

                def moments(b, h, done):
                    if final:
                        dve.wait_ge(freed, b * R + (h + 1) * CH + 2)
                    else:
                        dve.wait_ge(steps, done.now())
                    row_moments(dve, done, [y[:, j, :] for j in range(CH)], stats, mv)
                    done.up(nc.vector.tensor_scalar(var[:], mv[:, :, 1], EPS, None, ALU.add))
                    dve.wait_ge(steps, done.now())
                    nc.vector.reciprocal(var[:], var[:]).then_inc(var_ready, 1)

                def normed(b, h):
                    if final:
                        dve.wait_ge(scattered[h], b * (16 * CH) + 16)
                    dve.wait_ge(rstd_ready, 2 * b + h + 1)
                    for j in range(CH):
                        to = res[:, h, j:j + 1, :] if final else state[:, ds(b * R + h * CH + j, 1), :]
                        k = nc.vector.tensor_scalar(to, y[:, j:j + 1, :], mv[:, j, 0:1], rstd[:, j:j + 1], ALU.subtract, ALU.mult)
                    k.then_inc(chunk_done, 1)

                per_turn = 0 if inner else 2 * ((0 if final else CH) + 2 * CH + 2)

                def turn(b, last):
                    done = Count(steps, b, per_turn)
                    for h in range(2):
                        for j in range(CH):
                            if h == 0:
                                weigh(b, CH + j)
                            elif not last:
                                weigh(b + 1, j)
                            take(b, h * CH + j, done)
                        if not inner:
                            moments(b, h, done)
                            normed(b, h)
                            dve.wait_ge(chunk_done, 2 * b + h + 1)
                    assert done.n == per_turn, (done.n, per_turn)

                for j in range(CH):
                    weigh(0, j)
                with dve.Fori(0, NB - 1) as b:
                    turn(b, False)
                turn(NB - 1, True)


def lay_out(src, dst, edge_attr, edge_weight, x, Wq, bq, Wk, bk, We, be, Wv, bv, W1, b1, W2, b2, W3, b3, mlp_w, mlp_b):
    import numpy as np

    def grid(a, fill):
        g = np.full((T * RE,), fill, a.dtype)
        g[:E] = a
        return g.reshape(T, RE)

    def with_first(first, rest):
        return np.concatenate([first[:, None], rest], axis=1)

    def again(a):
        return np.concatenate([a, a[:R]], axis=0)

    d = grid(dst, N)
    last = d[:, -1]
    before = np.concatenate([np.full((1,), -1, dst.dtype), last[:-1]])
    following = np.concatenate([d.reshape(-1)[1:], np.full((1,), N, dst.dtype)]).reshape(T, RE)
    zero_i, zero_f = np.zeros((T,), src.dtype), np.zeros((T,), edge_weight.dtype)
    ea = np.zeros((T, P, D), edge_attr.dtype)
    ea.reshape(T, P, D)[:, 1:, :] = np.concatenate([edge_attr, np.zeros((T * RE - E, D), edge_attr.dtype)]).reshape(T, RE, D)

    def t_(a):
        return np.ascontiguousarray(a.T)

    def biased(w, b):
        return np.concatenate([w, b[None, :]], axis=0)

    return {
        "x": np.concatenate([x, np.zeros((NN - N, D), x.dtype)]),
        "src_p": t_(with_first(zero_i, grid(src, 0))),
        "dst_k": t_(again(with_first(before, d))),
        "dst_next": t_(with_first(before, following)),
        "dst_i": again(with_first(last, d)).reshape(-1),
        "w_p": t_(with_first(zero_f, grid(edge_weight, 0))),
        "ea_t": t_(np.concatenate([ea.reshape(T * P, D), np.zeros((CH * P, D), ea.dtype)])),
        "wkv": np.concatenate([biased(Wk, bk), biased(Wv, bv)], axis=1),
        "wq": biased(Wq, bq),
        "we": biased(We, be),
        "w1": biased(W1, b1),
        "w2": biased(W2, b2),
        "w3": biased(W3, b3),
        "wa": biased(np.ascontiguousarray(mlp_w[:, :D].T), mlp_b),
        "wb": np.ascontiguousarray(mlp_w[:, D:].T),
    }


def kernel(x, src, dst, edge_attr_96, edge_weight, L0_gnn_Wq, L0_gnn_bq, L0_gnn_Wk, L0_gnn_bk, L0_gnn_We, L0_gnn_be,
           L0_gnn_Wv, L0_gnn_bv, L2_gnn_W1, L2_gnn_b1, L2_gnn_W2, L2_gnn_b2, L2_gnn_W3, L2_gnn_b3, L3_gnn_mlp_w, L3_gnn_mlp_b):
    import numpy as np
    import concourse.bacc as bacc
    from concourse.bass_utils import run_bass_kernel_spmd

    given = [np.asarray(a) for a in (src, dst, edge_attr_96, edge_weight, x, L0_gnn_Wq, L0_gnn_bq, L0_gnn_Wk, L0_gnn_bk, L0_gnn_We,
                                     L0_gnn_be, L0_gnn_Wv, L0_gnn_bv, L2_gnn_W1, L2_gnn_b1, L2_gnn_W2, L2_gnn_b2, L2_gnn_W3,
                                     L2_gnn_b3, L3_gnn_mlp_w, L3_gnn_mlp_b)]
    nc = bacc.Bacc("TRN2", target_bir_lowering=False, num_devices=1)
    arrays, args = {}, {}
    for name, a in lay_out(*given).items():
        a = np.ascontiguousarray(a)
        arrays[f"in_{name}"] = a
        args[name] = nc.dram_tensor(f"in_{name}", a.shape, mybir.dt.from_np(a.dtype), kind="ExternalInput").ap()
    args["out"] = nc.dram_tensor("out_nodes", [NN, D], F32, kind="ExternalOutput").ap()

    def scratch(name, shape, dt):
        return nc.dram_tensor(name, shape, dt, kind="Internal").ap()

    build_graph_kernel(nc, scratch, **args)
    r = run_bass_kernel_spmd(nc, [arrays], core_ids=[0])
    return r.results[0]["out_nodes"][:N]
```

```python
from contextlib import ExitStack, contextmanager

import concourse.bass as bass
from concourse import mybir

F32 = mybir.dt.float32
I32 = mybir.dt.int32
ALU = mybir.AluOpType
ACT = mybir.ActivationFunctionType
AX_X = mybir.AxisListType.X

P = 128
D = 96
N = 50000
E = 25000
HEADS = 8
DH = D // HEADS
STEPS = 16
ALPHA = 0.1
EPS = 1e-5

RE = P - 1
CH = 5
R = 2 * CH
T = -(-E // (RE * R)) * R
NB = T // R
NS = T * P
NQ = 396
NN = P * NQ
LNW = 6
JW = 3
JOB_STEPS = 14
LAG = 2
assert JOB_STEPS == STEPS - 2 and JOB_STEPS * (NB // 2) >= NQ // JW + LAG
SKIP = 1 << 20
MSG = D + HEADS + 2


class Count:

    def __init__(self, sem, turn, per):
        self.sem, self.turn, self.per, self.n = sem, turn, per, 0

    def up(self, instruction):
        if hasattr(instruction, "then_inc"):
            instruction.then_inc(self.sem, 1)
        else:
            instruction.sem_inc(self.sem, 1)
        self.n += 1
        return instruction

    def now(self):
        return self.turn * self.per + self.n


@contextmanager
def semaphores(nc):
    taken = []

    def sem(name):
        taken.append(nc.alloc_semaphore(name))
        return taken[-1]

    yield sem
    nc.clear_and_free_semaphores(taken)
    nc.all_engine_barrier()


def ds(start, size):
    return bass.ds(start, size)


def per_head(ap):
    return ap.rearrange("p c (h d) -> p c h d", h=HEADS)


def every(ap):
    return ap.rearrange("p c (h o) -> p c h o", o=1).broadcast_to([P, CH, HEADS, DH])


def cols(ap):
    return ap.rearrange("p a d -> p (a d)")


def row_moments(dve, done, tiles, stats, mv):
    for j, tile in enumerate(tiles):
        done.up(dve.bn_stats(stats[:, j, :], tile))
    dve.wait_ge(done.sem, done.now())
    done.up(dve)
    for j in range(len(tiles)):
        done.up(dve.bn_aggr(mv[:, j, :], stats[:, j, :]))
    dve.wait_ge(done.sem, done.now())


def build_graph_kernel(nc, scratch, x, src_p, dst_k, dst_next, dst_i, w_p, ea_t, wkv, wq, we, w1, w2, w3, wa, wb, out):
    tab1 = scratch("tab1", [2 * NS + NN, D], F32)
    tab2, tab3, tab4, tab5 = (scratch(f"tab{k}", [NS + NN, D], F32) for k in (2, 3, 4, 5))
    slotmap = scratch("slotmap", [NN, 1], I32)
    sums = scratch("sums", [P, (T + R) * P], F32)

    def slot_rows(tab, base=0):
        return tab[base:base + NS, :].rearrange("(p t) d -> p t d", p=P)

    def node_rows(tab):
        return tab[NS:NS + NN, :].rearrange("(p q) d -> p q d", p=P)

    x_rows = x.rearrange("(p q) d -> p q d", p=P)
    out_rows = out.rearrange("(p q) d -> p q d", p=P)

    with ExitStack() as whole:
        def keep(name, shape, dt=F32):
            return whole.enter_context(nc.sbuf_tensor(name, shape, dt))

        state = keep("state", [P, T, D])
        fixed = keep("fixed", [P, T, D])
        ident = keep("ident", [P, P])
        ptr = keep("ptr", [P, 2 * T + 2 * R], I32)
        src_s = keep("src_s", [P, T], I32)
        dst_s = keep("dst_s", [P, T], I32)
        scat = keep("scat", [P, T], I32)
        w_s = keep("w_s", [P, T])
        cnt = keep("cnt", [P, T])
        wsum = keep("wsum", [P, T])
        canon = keep("canon", [P, T])
        step_a = keep("step_a", [P, T])
        dis_w = keep("dis_w", [P, T])
        dis_c = keep("dis_c", [P, T])

        with ExitStack() as c:
            sem = c.enter_context(semaphores(nc))
            key_k = c.enter_context(nc.sbuf_tensor("key_k", [P, T + R], I32))
            key_f = c.enter_context(nc.sbuf_tensor("key_f", [P, T + R], F32))
            nxt = c.enter_context(nc.sbuf_tensor("nxt", [P, T], I32))
            nxt_f = c.enter_context(nc.sbuf_tensor("nxt_f", [P, T], F32))
            same = c.enter_context(nc.sbuf_tensor("same", [P, T], F32))
            slot_id = c.enter_context(nc.sbuf_tensor("slot_id", [P, T], I32))
            node_id = c.enter_context(nc.sbuf_tensor("node_id", [P, NQ], I32))
            loaded, made, map_set = sem("loaded"), sem("made"), sem("map_set")
            id_set = sem("id_set")
            vec = sem("index_steps")
            s_out = [sem(f"s_out{h}") for h in range(2)]
            x_out = [sem(f"x_out{h}") for h in range(2)]
            map_done = [sem(f"map_done{h}") for h in range(2)]
            prime = c.enter_context(nc.sbuf_tensor("prime_0", [1, 6, 8], F32))
            with nc.Block() as block:
                @block.sync
                def _(sp):
                    for k, moved in enumerate((*s_out, *x_out)):
                        sp.dma_start(prime[:, k], x[0:1, 0:8]).then_inc(moved, 16)
                        sp.wait_ge(moved, 16)
                    for to, frm in ((key_k, dst_k), (nxt, dst_next), (src_s, src_p), (w_s, w_p)):
                        sp.dma_start(to[:], frm).then_inc(loaded, 16)
                    sp.wait_ge(made, 2)
                    sp.dma_start(slotmap.rearrange("(p q) o -> p (q o)", p=P), node_id[:]).then_inc(map_set, 16)
                    sp.wait_ge(map_set, 16)

                @block.gpsimd
                def _(pool):
                    pool.iota(slot_id[:], [[1, T]], base=0, channel_multiplier=T).then_inc(made, 1)
                    pool.iota(node_id[:], [[1, NQ]], base=NS, channel_multiplier=NQ).then_inc(made, 1)
                    pool.memset(ident[:], 0.0).then_inc(id_set, 1)
                    pool.wait_ge(id_set, 1)
                    for h in range(2):
                        pool.dma_start(prime[:, 4 + h], x[0:1, 0:8]).then_inc(map_done[h], 16)
                        pool.wait_ge(map_done[h], 16)
                    pool.affine_select(out=ident[:], in_=ident[:], compare_op=ALU.not_equal, fill=1.0, base=0,
                                       pattern=[[-1, P]], channel_multiplier=1).then_inc(id_set, 1)

                @block.vector
                def _(dve):
                    done = Count(vec, 0, 0)
                    dve.wait_ge(loaded, 64)
                    done.up(nc.vector.tensor_copy(key_f[:], key_k[:]))
                    done.up(nc.vector.tensor_copy(nxt_f[:], nxt[:]))
                    dve.wait_ge(vec, done.now())
                    done.up(nc.vector.tensor_tensor(same[:], key_f[:, 0:T], nxt_f[:], ALU.is_equal))
                    done.up(nc.vector.tensor_scalar(dst_s[:], key_f[:, 0:T], float(N - 1), 0.0, ALU.min, ALU.max))
                    dve.wait_ge(vec, done.now())
                    done.up(nc.vector.tensor_scalar(canon[:], same[:], -1.0, 1.0, ALU.mult, ALU.add))
                    done.up(nc.vector.scalar_tensor_tensor(out=scat[:], in0=same[:], scalar=float(SKIP),
                                                           in1=key_f[:, 0:T], op0=ALU.mult, op1=ALU.add))

            keys = c.enter_context(nc.sbuf_tensor("keys", [P, 2, CH * P], I32))
            s_new = c.enter_context(nc.sbuf_tensor("s_new", [P, 2, CH * P], F32))
            xin = c.enter_context(nc.sbuf_tensor("xin", [P, 2, LNW, D], F32))
            xout = c.enter_context(nc.sbuf_tensor("xout", [P, 2, LNW, D], F32))
            stats = c.enter_context(nc.sbuf_tensor("stats", [P, LNW, 6], F32))
            mv = c.enter_context(nc.sbuf_tensor("mv", [P, 2, LNW, 2], F32))
            var = c.enter_context(nc.sbuf_tensor("var", [P, 2, LNW], F32))
            rstd = c.enter_context(nc.sbuf_tensor("rstd", [P, 2, LNW], F32))
            idx = c.enter_context(nc.sbuf_tensor("idx", [P, 2, CH], I32))
            val = c.enter_context(nc.sbuf_tensor("val", [P, 2, CH], I32))
            keys_in = [sem(f"keys_in{h}") for h in range(2)]
            s_made = sem("s_made")
            x_in = [sem(f"x_in{h}") for h in range(2)]
            ln_done, ln_steps, var_ready, rstd_ready = sem("ln_done"), sem("ln_steps"), sem("var_ready"), sem("rstd_ready")
            staged, go = sem("staged"), sem("go")
            ptr_in = [sem(f"ptr_in{h}") for h in range(2)]
            ptr_kept, ptr_ready = sem("ptr_kept"), sem("ptr_ready")
            NCH = (T + R) // CH
            NJ = NQ // LNW
            with nc.Block() as block:
                @block.sync
                def _(sp):
                    def load_keys(c_, h):
                        part = dst_i[ds(c_ * (CH * P), CH * P)].rearrange("(o n) -> o n", o=1)
                        sp.dma_start(keys[:, h, :], part.broadcast_to([P, CH * P])).then_inc(keys_in[h], 16)

                    for h in range(2):
                        load_keys(h, h)
                        sp.dma_start(xin[:, h], x_rows[:, h * LNW:(h + 1) * LNW, :]).then_inc(x_in[h], 16)
                    with sp.Fori(0, NCH // 2 - 1) as b:
                        for h in range(2):
                            sp.wait_ge(s_made, 2 * b + h + 1)
                            load_keys(2 * b + 2 + h, h)
                            sp.dma_start(sums[:, ds((2 * b + h) * (CH * P), CH * P)], s_new[:, h, :]).then_inc(s_out[h], 16)
                    for h in range(2):
                        sp.wait_ge(s_made, NCH - 1 + h)
                        sp.dma_start(sums[:, (NCH - 2 + h) * CH * P:(NCH - 1 + h) * CH * P], s_new[:, h, :]).then_inc(s_out[h], 16)
                    with sp.Fori(0, NJ // 2 - 1) as b:
                        for h in range(2):
                            sp.wait_ge(ln_done, 2 * b + h + 1)
                            sp.dma_start(xin[:, h], x_rows[:, ds((2 * b + 2 + h) * LNW, LNW), :]).then_inc(x_in[h], 16)
                            sp.dma_start(node_rows(tab1)[:, ds((2 * b + h) * LNW, LNW), :], xout[:, h]).then_inc(x_out[h], 16)
                    for h in range(2):
                        sp.wait_ge(ln_done, NJ - 1 + h)
                        sp.dma_start(node_rows(tab1)[:, (NJ - 2 + h) * LNW:(NJ - 1 + h) * LNW, :], xout[:, h]).then_inc(x_out[h], 16)
                    for h in range(2):
                        sp.wait_ge(s_out[h], 16 * (NCH // 2 + 1))
                        sp.wait_ge(x_out[h], 16 * (NJ // 2 + 1))

                @block.scalar
                def _(act):
                    with act.Fori(0, NJ // 2) as b:
                        for h in range(2):
                            act.wait_ge(var_ready, 2 * b + h + 1)
                            nc.scalar.activation(rstd[:, h, :], var[:, h, :], ACT.Sqrt).then_inc(rstd_ready, 1)

                @block.vector
                def _(dve):
                    with dve.Fori(0, NCH // 2) as b:
                        for h in range(2):
                            dve.wait_ge(keys_in[h], b * 16 + 16)
                            dve.wait_ge(s_out[h], b * 16 + 16)
                            for j in range(CH):
                                k = nc.vector.tensor_scalar(s_new[:, h, j * P:(j + 1) * P], keys[:, h, j * P:(j + 1) * P],
                                                            key_f[:, ds(b * R + h * CH + j, 1)], None, ALU.is_equal)
                            k.then_inc(s_made, 1)
                    with dve.Fori(0, NJ // 2) as b:
                        done = Count(ln_steps, b, 2 * (2 * LNW + 2))
                        for h in range(2):
                            dve.wait_ge(x_in[h], b * 16 + 16)
                            row_moments(dve, done, [xin[:, h, j, :] for j in range(LNW)], stats, mv[:, h])
                            done.up(nc.vector.tensor_scalar(var[:, h, :], mv[:, h, :, 1], EPS, None, ALU.add))
                            dve.wait_ge(ln_steps, done.now())
                            nc.vector.reciprocal(var[:, h, :], var[:, h, :]).then_inc(var_ready, 1)
                        for h in range(2):
                            dve.wait_ge(x_out[h], b * 16 + 16)
                            dve.wait_ge(rstd_ready, 2 * b + h + 1)
                            for j in range(LNW):
                                k = nc.vector.tensor_scalar(xout[:, h, j, :], xin[:, h, j, :], mv[:, h, j, 0:1], rstd[:, h, j:j + 1],
                                                            ALU.subtract, ALU.mult)
                            k.then_inc(ln_done, 1)
                    dve.wait_ge(ptr_kept, 2 * NB)
                    nc.vector.tensor_copy(nxt_f[:], ptr[:, 0:T]).then_inc(ptr_ready, 1)
                    dve.wait_ge(ptr_ready, 1)
                    nc.vector.tensor_scalar(same[:], nxt_f[:], float(NS), float(NS + NN), ALU.is_lt, ALU.mult).then_inc(ptr_ready, 1)
                    dve.wait_ge(ptr_ready, 2)
                    nc.vector.tensor_tensor(ptr[:, T:2 * T], nxt_f[:], same[:], ALU.add)
                    nc.vector.tensor_copy(ptr[:, 2 * T:], ptr[:, 0:2 * R])

                @block.gpsimd
                def _(pool):
                    with pool.Fori(0, NB) as b:
                        for h in range(2):
                            pool.wait_ge(map_done[h], b * (16 * CH) + 16)
                            nc.gpsimd.tensor_copy(idx[:, h, :], scat[:, ds(b * R + h * CH, CH)]).then_inc(staged, 1)
                            nc.gpsimd.tensor_copy(val[:, h, :], slot_id[:, ds(b * R + h * CH, CH)]).then_inc(staged, 1)
                            pool.wait_ge(staged, b * 4 + 2 * h + 2)
                            pool.sem_inc(go, 1)
                            for j in range(CH):
                                nc.gpsimd.indirect_dma_start(slotmap, bass.IndirectOffsetOnAxis(ap=idx[:, h, j:j + 1], axis=0),
                                                             val[:, h, j:j + 1], None, bounds_check=N - 1,
                                                             oob_is_err=False).then_inc(map_done[h], 16)
                    for h in range(2):
                        pool.wait_ge(map_done[h], 16 * CH * NB + 16)

                    def look_up(b, h, first):
                        nc.gpsimd.tensor_copy(idx[:, h, :], src_s[:, ds(b * R + h * CH, CH)]).then_inc(staged, 1)
                        pool.wait_ge(staged, b * 2 + (4 * NB + h + 1))
                        if not first:
                            pool.wait_ge(ptr_kept, b * 2 + (h - 1))
                        pool.sem_inc(go, 1)
                        for j in range(CH):
                            nc.gpsimd.indirect_dma_start(val[:, h, j:j + 1], None, slotmap,
                                                         bass.IndirectOffsetOnAxis(ap=idx[:, h, j:j + 1], axis=0)).then_inc(ptr_in[h], 16)

                    def keep_pointers(b, h):
                        pool.wait_ge(ptr_in[h], b * (16 * CH) + 16 * CH)
                        nc.gpsimd.tensor_copy(ptr[:, ds(b * R + h * CH, CH)], val[:, h, :]).then_inc(ptr_kept, 1)

                    look_up(0, 0, True)
                    look_up(0, 1, True)
                    keep_pointers(0, 0)
                    with pool.Fori(1, NB) as b:
                        look_up(b, 0, False)
                        keep_pointers(b - 1, 1)
                        look_up(b, 1, False)
                        keep_pointers(b, 0)
                    keep_pointers(NB - 1, 1)

        edge_attention(nc, state, fixed, ident, src_s, dst_s, w_s, cnt, wsum, x, ea_t, wkv, wq, we, sums, slot_rows(tab1))
        appnp(nc, state, fixed, ident, ptr, step_a, cnt, wsum, dis_w, dis_c, canon, sums, slot_rows, w1, w2, w3, wa,
              (tab1, tab2, tab3, tab4, tab5), node_rows, out_rows)
        layers = ((w1, tab2, tab3), (w2, tab3, tab4), (w3, tab4, tab5))
        for n, (w, tab, nxt_tab) in enumerate(layers):
            convolution(nc, n + 2, state, fixed, ident, ptr, w_s, dis_w, dis_c, scat, w, None, tab, sums,
                        slot_rows(nxt_tab), out)
        convolution(nc, 5, state, fixed, ident, ptr, w_s, dis_w, dis_c, scat, wb, wa, tab5, sums, None, out)


def edge_attention(nc, state, fixed, ident, src_s, dst_s, w_s, cnt, wsum, x, ea_t, wkv, wq, we, sums, tab_slots):
    with ExitStack() as c:
        sem = c.enter_context(semaphores(nc))
        def sb(name, shape, dt=F32):
            return c.enter_context(nc.sbuf_tensor(name, shape, dt))

        wkv_s, wq_s, we_s = sb("wkv_s", [D + 1, 2 * D]), sb("wq_s", [D + 1, D]), sb("we_s", [D + 1, D])
        idx = sb("idx_l0", [P, 2, 2, CH], I32)
        xs = sb("xs", [P, R, D])
        xd = sb("xd", [P, R, D])
        ea = sb("ea", [D + 1, 2, CH * P])
        s_in = sb("s_l0", [P, 2, CH * P])
        xt = sb("xt", [D + 1, 2, 2 * P])
        kvqe = sb("kvqe", [P, 2, CH, 4 * D])
        prod = sb("prod", [P, CH, D])
        score = sb("score", [P, CH, HEADS])
        msg = sb("msg", [P, 2, CH, MSG])
        agg = sb("agg", [P, 2, CH, MSG])
        zinv = sb("zinv", [P, CH, HEADS])
        deg = sb("deg", [P, CH])
        var = sb("var_l0", [P, CH])
        stats = sb("stats_l0", [P, CH, 6])
        mv = sb("mv_l0", [P, CH, 2])
        rstd = sb("rstd_l0", [P, CH])
        ps_t = [c.enter_context(nc.psum_tensor(f"ps_t{k}", [P, 512], F32)) for k in range(2)]
        ps_p = [c.enter_context(nc.psum_tensor(f"ps_p{k}", [P, 512], F32)) for k in range(2)]
        ps_s = [c.enter_context(nc.psum_tensor(f"ps_s{k}", [P, 512], F32)) for k in range(2)]

        const_in = sem("const_in")
        rows_in = [sem(f"l0_rows_in{i}") for i in range(R)]
        ea_in = [sem(f"l0_ea_in{h}") for h in range(2)]
        sm_in = [sem(f"l0_s_in{h}") for h in range(2)]
        staged, go = sem("l0_staged"), sem("l0_go")
        turned, turned_kept = sem("l0_turned"), sem("l0_turned_kept")
        projected, projected_kept = sem("l0_projected"), sem("l0_projected_kept")
        scored, exped, msg_ready = sem("l0_scored"), sem("l0_exped"), sem("l0_msg_ready")
        carry_kept = sem("l0_carry_kept")
        summed, sum_kept = sem("l0_summed"), sem("l0_sum_kept")
        posted, written = sem("l0_posted"), sem("l0_written")
        steps, var_ready, rstd_ready = sem("l0_steps"), sem("l0_var_ready"), sem("l0_rstd_ready")
        NCH = 2 * NB

        with nc.Block() as block:
            @block.sync
            def _(sp):
                for to, frm in ((wkv_s, wkv), (wq_s, wq), (we_s, we)):
                    sp.dma_start(to[:], frm).then_inc(const_in, 16)
                sp.wait_ge(const_in, 48)

            @block.vector
            def _(dve):
                nc.vector.memset(xt[D:D + 1, :, :], 1.0)
                nc.vector.memset(ea[D:D + 1, :, :], 1.0)
                nc.vector.memset(ps_s[1][0:1, :], 0.0)

        with nc.Block() as block:
            @block.sync
            def _(sp):
                def load_ea(cc, h):
                    sp.dma_start(ea[0:D, h, :], ea_t[:, ds(cc * (CH * P), CH * P)]).then_inc(ea_in[h], 16)

                def load_s(cc, h):
                    sp.dma_start(s_in[:, h, :], sums[:, ds(cc * (CH * P), CH * P)]).then_inc(sm_in[h], 16)

                for h in range(2):
                    load_ea(h, h)
                    load_s(h, h)
                for h in range(2):
                    sp.wait_ge(projected, (h + 1) * CH)
                    load_ea(2 + h, h)

                def turn(b, more_ea, more_s):
                    for h in range(2):
                        if more_ea:
                            sp.wait_ge(projected, b * R + (h + 3) * CH)
                            load_ea(2 * b + 4 + h, h)
                        if more_s:
                            sp.wait_ge(summed, b * R + (h + 1) * CH)
                            load_s(2 * b + 2 + h, h)
                        sp.wait_ge(posted, 2 * b + h + 1)
                        sp.dma_start(tab_slots[:, ds(b * R + h * CH, CH), :], state[:, ds(b * R + h * CH, CH), :]).then_inc(written, 16)

                with sp.Fori(0, NB - 2) as b:
                    turn(b, True, True)
                turn(NB - 2, False, True)
                turn(NB - 1, False, False)
                sp.wait_ge(written, 16 * NCH)

            @block.gpsimd
            def _(pool):
                def turn(b, first):
                    for h in range(2):
                        if not first:
                            pool.wait_ge(turned_kept, b * R + (h - 1) * CH)
                        for k, of in enumerate((src_s, dst_s)):
                            nc.gpsimd.tensor_copy(idx[:, h, k, :], of[:, ds(b * R + h * CH, CH)]).then_inc(staged, 1)
                        pool.wait_ge(staged, b * 4 + 2 * h + 2)
                        pool.sem_inc(go, 1)
                        for j in range(CH):
                            for k, to in enumerate((xs, xd)):
                                nc.gpsimd.indirect_dma_start(to[:, h * CH + j, :], None, x,
                                                             bass.IndirectOffsetOnAxis(ap=idx[:, h, k, j:j + 1], axis=0)).then_inc(rows_in[h * CH + j], 16)

                turn(0, True)
                with pool.Fori(1, NB) as b:
                    turn(b, False)

            def turn_rows(pe, b, i):
                pe.wait_ge(rows_in[i], b * 32 + 32)
                nc.tensor.transpose(ps_t[i % 2][0:D, 0:P], xs[:, i, :], ident[:])
                nc.tensor.transpose(ps_t[i % 2][0:D, P:2 * P], xd[:, i, :], ident[:]).then_inc(turned, 1)

            def project(pe, b, i):
                h, j, n = i // CH, i % CH, b * R + i
                pe.wait_ge(turned_kept, n + 1)
                if j == 0:
                    pe.wait_ge(ea_in[h], b * 16 + 16)
                if not isinstance(n, int) or n > 1:
                    pe.wait_ge(projected_kept, n - 1)
                to = ps_p[i % 2]
                nc.tensor.matmul(to[:, 0:2 * D], xt[:, i % 2, 0:P], wkv_s[:], start=True, stop=True)
                nc.tensor.matmul(to[:, 2 * D:3 * D], xt[:, i % 2, P:2 * P], wq_s[:], start=True, stop=True)
                nc.tensor.matmul(to[:, 3 * D:4 * D], ea[:, h, j * P:(j + 1) * P], we_s[:], start=True, stop=True).then_inc(projected, 1)

            def sum_up(pe, b, i):
                h, j, n = i // CH, i % CH, b * R + i
                if j == 0:
                    pe.wait_ge(sm_in[h], b * 16 + 16)
                pe.wait_ge(carry_kept, n + 1)
                s = s_in[:, h, j * P:(j + 1) * P]
                if not isinstance(n, int) or n > 1:
                    pe.wait_ge(sum_kept, n - 1)
                nc.tensor.matmul(ps_s[i % 2][:, 0:MSG], s, msg[:, h, j, :], start=True, stop=True).then_inc(summed, 1)

            @block.tensor
            def _(pe):
                def turn(b, left):
                    for i in range(R):
                        if i + 1 < R and left:
                            turn_rows(pe, b + 1, i + 1)
                        elif i + 1 == R and left > 1:
                            turn_rows(pe, b + 2, 0)
                        sum_up(pe, b, i)
                        if left:
                            project(pe, b + 1, i)

                turn_rows(pe, 0, 0)
                for i in range(R):
                    turn_rows(pe, *((0, i + 1) if i + 1 < R else (1, 0)))
                    project(pe, 0, i)
                turn(0, 2)
                with pe.Fori(1, NB - 2) as b:
                    turn(b, 2)
                turn(NB - 2, 1)
                turn(NB - 1, 0)

            @block.scalar
            def _(act):
                def keep_turned(b, i):
                    n = b * R + i
                    act.wait_ge(turned, n + 1)
                    nc.scalar.copy(state[:, ds(n, 1), :], xd[:, i:i + 1, :])
                    nc.scalar.copy(xt[0:D, i % 2, :], ps_t[i % 2][0:D, 0:2 * P]).then_inc(turned_kept, 1)

                def keep_projection(b, i):
                    n = b * R + i
                    act.wait_ge(projected, n + 1)
                    if i % CH == 0 and (not isinstance(n, int) or n >= R):
                        act.wait_ge(msg_ready, b * 2 + (i // CH - 1))
                    nc.scalar.copy(kvqe[:, i // CH, i % CH, :], ps_p[i % 2][:, 0:4 * D]).then_inc(projected_kept, 1)

                def exponent(b, h):
                    act.wait_ge(scored, b * 2 + h + 1)
                    nc.scalar.activation(score[:], score[:], ACT.Exp, scale=float(DH) ** -0.5).then_inc(exped, 1)

                def carry(b, i):
                    h, j, n = i // CH, i % CH, b * R + i
                    if j == 0:
                        act.wait_ge(msg_ready, b * 2 + h + 1)
                    if not isinstance(n, int) or n:
                        act.wait_ge(summed, n)
                    nc.scalar.copy(msg[0:1, h, j, :], ps_s[(i - 1) % 2][0:1, 0:MSG]).then_inc(carry_kept, 1)

                def keep_sums(b, i):
                    h, j, n = i // CH, i % CH, b * R + i
                    if j == 0 and (not isinstance(n, int) or n >= R):
                        act.wait_ge(posted, b * 2 + h - 1)
                    act.wait_ge(summed, n + 1)
                    nc.scalar.copy(agg[:, h, j, :], ps_s[i % 2][:, 0:MSG]).then_inc(sum_kept, 1)

                def root(b, h):
                    act.wait_ge(var_ready, b * 2 + h + 1)
                    nc.scalar.activation(rstd[:], var[:], ACT.Sqrt).then_inc(rstd_ready, 1)

                def turn(b, first, left):
                    last = not left
                    for i in range(R):
                        h, j = i // CH, i % CH
                        if i + 1 < R or left:
                            carry(*((b, i + 1) if i + 1 < R else (b + 1, 0)))
                        if i + 1 < R and left:
                            keep_turned(b + 1, i + 1)
                        elif i + 1 == R and left > 1:
                            keep_turned(b + 2, 0)
                        keep_sums(b, i)
                        if left:
                            keep_projection(b + 1, i)
                        if j == 1 and not (last and h):
                            exponent(*((b, 1) if h == 0 else (b + 1, 0)))
                        if j == 3 and not (first and h == 0):
                            root(*((b - 1, 1) if h == 0 else (b, 0)))

                keep_turned(0, 0)
                for i in range(R):
                    keep_turned(*((0, i + 1) if i + 1 < R else (1, 0)))
                    keep_projection(0, i)
                    if i == CH:
                        exponent(0, 0)
                carry(0, 0)
                turn(0, True, 2)
                with act.Fori(1, NB - 2) as b:
                    turn(b, False, 2)
                turn(NB - 2, False, 1)
                turn(NB - 1, False, 0)
                root(NB - 1, 1)

            @block.vector
            def _(dve):
                def scores(b, h, done):
                    dve.wait_ge(projected_kept, b * R + (h + 1) * CH)
                    done.up(nc.vector.tensor_tensor(prod[:], kvqe[:, h, :, 0:D], kvqe[:, h, :, 2 * D:3 * D], ALU.mult))
                    dve.wait_ge(steps, done.now())
                    done.up(nc.vector.tensor_tensor(prod[:], prod[:], kvqe[:, h, :, 3 * D:4 * D], ALU.mult))
                    dve.wait_ge(steps, done.now())
                    if not isinstance(b, int) or b or h:
                        dve.wait_ge(msg_ready, b * 2 + h)
                    nc.vector.tensor_reduce(out=cols(score[:]), in_=prod[:].rearrange("p c (h d) -> p (c h) d", h=HEADS),
                                            axis=AX_X, op=ALU.add).then_inc(scored, 1)

                def messages(b, h, done):
                    dve.wait_ge(exped, b * 2 + h + 1)
                    done.up(nc.vector.tensor_scalar(msg[:, h, :, D:D + HEADS], score[:], E_LOW, E_HIGH, ALU.max, ALU.min))
                    done.up(nc.vector.memset(msg[:, h, :, D + HEADS:D + HEADS + 1], 1.0))
                    done.up(nc.vector.tensor_copy(msg[:, h, :, D + HEADS + 1], w_s[:, ds(b * R + h * CH, CH)]))
                    dve.wait_ge(steps, done.now())
                    nc.vector.tensor_tensor(per_head(msg[:, h, :, 0:D]), per_head(kvqe[:, h, :, D:2 * D]),
                                            every(msg[:, h, :, D:D + HEADS]), ALU.mult).then_inc(msg_ready, 1)

                def attend(b, h, later, done):
                    t = ds(b * R + h * CH, CH)
                    y = state[:, t, :]
                    dve.wait_ge(sum_kept, b * R + (h + 1) * CH)
                    done.up(nc.vector.tensor_scalar(zinv[:], agg[:, h, :, D:D + HEADS], 1e-6, None, ALU.add))
                    done.up(nc.vector.tensor_copy(cnt[:, t], agg[:, h, :, D + HEADS]))
                    done.up(nc.vector.tensor_copy(wsum[:, t], agg[:, h, :, D + HEADS + 1]))
                    done.up(nc.vector.tensor_scalar(deg[:], agg[:, h, :, D + HEADS], 1.0, None, ALU.add))
                    dve.wait_ge(steps, done.now())
                    done.up(nc.vector.reciprocal(zinv[:], zinv[:]))
                    dve.wait_ge(steps, done.now())
                    dve.wait_ge(scored, later)
                    done.up(nc.vector.tensor_tensor(per_head(prod[:]), per_head(agg[:, h, :, 0:D]), every(zinv[:]), ALU.mult))
                    dve.wait_ge(steps, done.now())
                    done.up(nc.vector.tensor_tensor(y, y, prod[:], ALU.add))
                    dve.wait_ge(steps, done.now())
                    done.up(dve)
                    row_moments(dve, done, [cols(state[:, ds(b * R + h * CH + j, 1), :]) for j in range(CH)], stats, mv)
                    done.up(nc.vector.scalar_tensor_tensor(out=var[:], in0=mv[:, :, 1], scalar=EPS, in1=deg[:], op0=ALU.add, op1=ALU.mult))
                    dve.wait_ge(steps, done.now())
                    nc.vector.reciprocal(var[:], var[:]).then_inc(var_ready, 1)

                def new_state(b, h):
                    t = ds(b * R + h * CH, CH)
                    dve.wait_ge(rstd_ready, 2 * b + h + 1)
                    for j in range(CH):
                        one = state[:, ds(b * R + h * CH + j, 1), :]
                        k = nc.vector.tensor_scalar(one, one, mv[:, j, 0:1], rstd[:, j:j + 1], ALU.subtract, ALU.mult)
                    k.then_inc(posted, 1)
                    dve.wait_ge(posted, 2 * b + h + 1)
                    nc.vector.tensor_scalar(fixed[:, t, :], state[:, t, :], ALPHA, None, ALU.mult)

                per_turn = 2 * (5 + 10 + 2 * CH)
                start = Count(steps, 0, 0)

                def turn(b, done, first, last):
                    for h in range(2):
                        ahead = (b, 1) if h == 0 else None if last else (b + 1, 0)
                        behind = (b, 0) if h else None if first else (b - 1, 1)
                        if ahead:
                            scores(*ahead, done)
                        if behind:
                            attend(*behind, 2 * b + h + (2 if ahead else 1), done)
                        if ahead:
                            messages(*ahead, done)
                        if behind:
                            new_state(*behind)

                def counted(b):
                    done = Count(steps, b, per_turn)
                    done.n = start.n - per_turn
                    return done

                scores(0, 0, start)
                messages(0, 0, start)
                turn(0, start, True, False)
                with dve.Fori(1, NB - 1) as b:
                    done = counted(b)
                    turn(b, done, False, False)
                    assert done.n == start.n
                done = counted(NB - 1)
                turn(NB - 1, done, False, True)
                attend(NB - 1, 1, NCH, done)
                new_state(NB - 1, 1)


E_LOW, E_HIGH = 0.006737946999085467, 148.4131591025766


def appnp(nc, state, fixed, ident, ptr, step_a, cnt, wsum, dis_w, dis_c, canon, sums, slot_rows, w1, w2, w3, wa, tabs, node_rows, out_rows):
    BANKS = 5
    RB = 2 * R
    NBB = T // RB
    CARRIES = RB + 1
    NJ = NQ // JW
    JOBS = JOB_STEPS * NBB
    W = JW * P
    tab1, tab2, tab3, tab4, tab5 = tabs
    with ExitStack() as c:
        sem = c.enter_context(semaphores(nc))

        def sb(name, shape, dt=F32):
            return c.enter_context(nc.sbuf_tensor("n_" + name, shape, dt))

        g = sb("g", [P, RB, D])
        s_in = sb("s", [P, 2, CH * P])
        idx = sb("idx", [P, 4, CH], I32)
        hold = sb("hold", [1, D])
        own = sb("own", [P, P])
        w1_s, w2_s, w3_s, wa_s = (sb(k, [D + 1, D]) for k in ("w1", "w2", "w3", "wa"))
        x1, x2, h1, h2, y3, x3, y4, res = (sb(k, [P, JW, D]) for k in ("x1", "x2", "h1", "h2", "y3", "x3", "y4", "res"))
        x2t, h1t, h2t, x3t = (sb(k, [D + 1, W]) for k in ("x2t", "h1t", "h2t", "x3t"))
        stats, mv, var, rstd = sb("stats", [P, JW, 6]), sb("mv", [P, 3, JW, 2]), sb("var", [P, 3, JW]), sb("rstd", [P, 3, JW])
        ps = [c.enter_context(nc.psum_tensor(f"l1_ps{k}", [P, 512], F32)) for k in range(BANKS)]
        ps_a, ps_b, ps_c = (c.enter_context(nc.psum_tensor(f"n_ps_{k}", [P, 512], F32)) for k in "abc")

        rows_in = [sem(f"l1_rows_in{i}") for i in range(RB)]
        s_landed = [sem(f"l1_s_in{h}") for h in range(2)]
        staged, go, turns = sem("l1_staged"), sem("l1_go"), sem("l1_turns")
        carried, summed = sem("l1_carried"), sem("l1_summed")
        freed = sem("l1_freed")
        written = sem("l1_written")
        const_in, x1_in, own_set = sem("n_const_in"), sem("n_x1_in"), sem("own_set")
        outs = {k: sem(f"n_{k}_out") for k in ("x2", "h1", "h2", "x3", "res")}
        ready = {k: sem(f"n_{k}_ready") for k in ("x2", "h1", "h2", "x3", "res")}
        steps = sem("n_steps")
        var_ready, rstd_ready = ([sem(f"n_{k}{m}") for m in range(3)] for k in ("var_ready", "rstd_ready"))
        turned, turned_kept = ({x_: sem(f"n_{x_}_{k}") for x_ in ("x2", "x3")} for k in ("turned", "turned_kept"))
        wide, wide_kept = ({x_: sem(f"n_{x_}_{k}") for x_ in ("h1", "h2")} for k in ("wide", "wide_kept"))
        narrow = {k: sem(f"n_{k}_narrow") for k in ("h1", "h2", "y3", "y4")}
        added = sem("n_added")
        deg_steps, inverse, rooted = sem("deg_steps"), sem("deg_inverse"), sem("deg_rooted")
        prime = sb("prime", [1, 6, 8])
        f_y, f_stats, f_mv = sb("f_y", [P, 2, CH, D]), sb("f_stats", [P, 2, CH, 6]), sb("f_mv", [P, 2, CH, 2])
        f_var, f_rstd = sb("f_var", [P, 2, CH]), sb("f_rstd", [P, 2, CH])
        f_steps, f_var_ready, f_rstd_ready = sem("f_steps"), sem("f_var_ready"), sem("f_rstd_ready")
        f_normed, f_scaled, f_written = sem("f_normed"), sem("f_scaled"), sem("f_written")

        with nc.Block() as block:
            @block.sync
            def _(sp):
                for to, frm in ((w1_s, w1), (w2_s, w2), (w3_s, w3), (wa_s, wa)):
                    sp.dma_start(to[:], frm).then_inc(const_in, 16)
                for k, out in enumerate((*outs.values(), written)):
                    sp.dma_start(prime[:, k], w1[0:1, 0:8]).then_inc(out, 16)
                sp.wait_ge(const_in, 64)
                for out in (*outs.values(), written):
                    sp.wait_ge(out, 16)

            @block.scalar
            def _(act):
                act.wait_ge(inverse, 1)
                nc.scalar.activation(dis_w[:], wsum[:], ACT.Sqrt).then_inc(rooted, 1)

            @block.vector
            def _(dve):
                nc.vector.memset(hold[:], 0.0)
                nc.vector.tensor_scalar(wsum[:], wsum[:], 1.0, None, ALU.add).then_inc(deg_steps, 1)
                nc.vector.tensor_scalar(cnt[:], cnt[:], 1.0, None, ALU.add).then_inc(deg_steps, 1)
                dve.wait_ge(deg_steps, 2)
                nc.vector.reciprocal(wsum[:], wsum[:]).then_inc(inverse, 1)
                nc.vector.reciprocal(step_a[:], cnt[:]).then_inc(deg_steps, 1)
                dve.wait_ge(deg_steps, 3)
                nc.vector.tensor_scalar(step_a[:], step_a[:], 1.0 - ALPHA, None, ALU.mult)
                dve.wait_ge(rooted, 1)
                nc.vector.tensor_tensor(dis_c[:], dis_w[:], canon[:], ALU.mult)
                nc.vector.tensor_copy(idx[:].rearrange("p h c -> p (h c)"), ptr[:, 0:RB]).then_inc(staged, 4)
                nc.vector.tensor_copy(own[:], ident[:]).then_inc(own_set, 1)
                dve.wait_ge(own_set, 1)
                nc.vector.memset(own[0:1, 0:1], 0.0)
                for a in (x2t, h2t):
                    nc.vector.memset(a[D:D + 1, :], 1.0)
                for a in (h1t, x3t, x2, x3):
                    nc.vector.memset(a[:], 1.0)
                dve.sem_inc(freed, RB)
                for k in (ready["h2"], wide_kept["h1"], turned_kept["x3"]):
                    dve.sem_inc(k, 1)

        def passes(eng, one):
            last_pair = STEPS // 2 - 1
            with eng.Fori(0, last_pair) as pair:
                for odd in range(2):
                    one(pair, odd, True, False)
            one(last_pair, 0, False, False)
            one(last_pair, 1, False, True)

        def bodies(eng, norm, body):
            if norm:
                body(0)
            with eng.Fori(1 if norm else 0, NBB) as b:
                body(b)

        def before(b, q, lag):
            if isinstance(b, int) and 4 * b + q < lag:
                return None
            return b * RB + (q - lag) * CH, b * 4 + (q - lag), (q - lag) % 2

        with nc.Block() as block:
            @block.sync
            def _(sp):
                def load_s(cc, h):
                    sp.dma_start(s_in[:, h, :], sums[:, ds(cc * (CH * P), CH * P)]).then_inc(s_landed[h], 16)

                def store(J, lag, name, frm, to):
                    sp.wait_ge(ready[name], J + (2 if name == "h2" else 1))
                    sp.sem_inc(turns, 1)
                    sp.dma_start(to[:, ds((J + (NJ - lag)) % NJ * JW, JW), :], frm[:]).then_inc(outs[name], 16)

                def store_x2(chunk):
                    if chunk:
                        t0, c_, _ = chunk
                        sp.wait_ge(f_scaled, c_ + 1)
                        sp.dma_start(slot_rows(tab2)[:, ds(t0, CH), :], state[:, ds(t0, CH), :]).then_inc(f_written, 16)

                def one(pair, odd, job, norm):
                    to = slot_rows(tab1, 0 if odd else NS + NN)

                    def slots(b, q):
                        n0, h = pair * (2 * T) + b * RB + odd * T, q % 2
                        sp.wait_ge(summed, n0 + CH * (q + 1))
                        load_s(4 * b + 2 + q, h)
                        if norm:
                            store_x2(before(b, q, 4))
                            return
                        sp.wait_ge(freed, n0 + (RB + CH * (q + 1)))
                        t = ds(b * RB + CH * q, CH)
                        sp.dma_start(to[:, t, :], state[:, t, :]).then_inc(written, 16)

                    def body(b):
                        J = pair * (2 * NBB) + b + odd * NBB
                        slots(b, 0)
                        if job:
                            store(J, 0, "x2", x2, node_rows(tab2))
                            sp.dma_start(x1[:], x1_rows[:, ds((J + 1) % NJ * JW, JW), :]).then_inc(x1_in, 16)
                        slots(b, 1)
                        if job:
                            store(J, 1, "x3", x3, node_rows(tab5))
                        slots(b, 2)
                        if job:
                            store(J, 2, "res", res, out_rows)
                            store(J, 0, "h1", h1, node_rows(tab3))
                        slots(b, 3)
                        if job:
                            store(J, 0, "h2", h2, node_rows(tab4))

                    bodies(sp, norm, body)

                x1_rows = node_rows(tab1)
                for h in range(2):
                    load_s(h, h)
                sp.dma_start(x1[:], x1_rows[:, 0:JW, :]).then_inc(x1_in, 16)
                passes(sp, one)
                for q in range(4):
                    store_x2(before(NBB, q, 4))
                sp.wait_ge(written, 16 * 2 * NB * (STEPS - 1) + 16)
                sp.wait_ge(f_written, 16 * 2 * NB)
                for h in range(2):
                    sp.wait_ge(s_landed[h], 16 * (NB * STEPS + 1))
                sp.wait_ge(x1_in, 16 * (JOBS + 1))
                for out in outs.values():
                    sp.wait_ge(out, 16 * (JOBS + 1))

            @block.gpsimd
            def _(pool):
                with pool.Fori(0, STEPS // 2) as pair:
                    for odd in range(2):
                        pool.wait_ge(written, pair * (64 * NB) + (odd * 32 * NB + 16))
                        pool.sem_inc(go, 1)
                        with pool.Fori(0, NBB) as b:
                            n0 = pair * (2 * T) + b * RB + odd * T
                            for q in range(4):
                                pool.wait_ge(freed, n0 + CH * (q + 1))
                                pool.wait_ge(staged, pair * (8 * NBB) + b * 4 + (odd * 4 * NBB + q + 1))
                                pool.sem_inc(go, 1)
                                for j in range(CH):
                                    i = q * CH + j
                                    nc.gpsimd.indirect_dma_start(g[:, i, :], None, tab1 if odd else tab1[0:NS + NN, :],
                                                                 bass.IndirectOffsetOnAxis(ap=idx[:, q, j:j + 1], axis=0)).then_inc(rows_in[i], 16)

            @block.tensor
            def _(pe):
                def slots(pair, odd, b, i, job):
                    h, j, turn = i // CH % 2, i % CH, pair * (2 * NBB) + b + odd * NBB
                    if j == 0:
                        pe.wait_ge(s_landed[h], turn * 32 + (i // R * 16 + 16))
                    pe.wait_ge(freed, turn * RB + (i + 1 + RB - BANKS))
                    to = ps[i % BANKS][:, 0:D]
                    nc.tensor.matmul(to, own[:], cols(state[:, ds(b * RB + i, 1), :]), start=True, stop=False)
                    if job:
                        nodes(turn, i)
                    pe.wait_ge(carried, turn * CARRIES + (i + 1))
                    nc.tensor.matmul(to, s_in[:, h, j * P:(j + 1) * P], g[:, i, :], start=False, stop=True).then_inc(summed, 1)

                def turn_rows(name, frm, half):
                    for j in range(half * JW // 2, (half + 1) * JW // 2):
                        m = nc.tensor.transpose(ps_a[0:D, j * P:(j + 1) * P], frm[:, j, :], ident[:])
                    if half:
                        m.then_inc(turned[name], 1)

                def across(name, frm, w, part, parts):
                    at = slice(part * W // parts, (part + 1) * W // parts)
                    m = nc.tensor.matmul(ps_b[0:D, at], w[:], frm[:, at], start=True, stop=True)
                    if part == parts - 1:
                        m.then_inc(wide[name], 1)

                def rows(name, frm, w, half):
                    for j in range(half * JW // 2, (half + 1) * JW // 2):
                        m = nc.tensor.matmul(ps_c[:, j * D:(j + 1) * D], frm[:, j * P:(j + 1) * P], w[:], start=True, stop=True)
                    if half:
                        m.then_inc(narrow[name], 1)

                def nodes(J, i):
                    if i == 0:
                        pe.wait_ge(wide_kept["h1"], J + 1)
                    if i in (0, 1):
                        across("h2", h1t, w2_s, i, 2)
                    if i == 3:
                        pe.wait_ge(wide_kept["h2"], J + 1)
                        pe.wait_ge(ready["h2"], J + 1)
                    if i in (3, 4):
                        rows("y3", h2t, w3_s, i - 3)
                    if i == 8:
                        pe.wait_ge(turned_kept["x3"], J + 1)
                        pe.wait_ge(added, J * 2 + 1)
                    if i in (8, 9):
                        rows("y4", x3t, wa_s, i - 8)
                    if i == 10:
                        pe.wait_ge(ready["x2"], J + 1)
                    if i in (10, 11):
                        turn_rows("x2", x2, i - 10)
                    if i == 13:
                        pe.wait_ge(turned_kept["x2"], J + 1)
                        pe.wait_ge(added, J * 2 + 2)
                    if i in (13, 14):
                        rows("h1", x2t, w1_s, i - 13)
                    if i in (13, 14, 15):
                        across("h1", x2t, w1_s, i - 13, 4)
                    if i == 15:
                        across("h1", x2t, w1_s, 3, 4)
                    if i == 16:
                        pe.wait_ge(ready["x3"], J + 1)
                    if i in (16, 17):
                        turn_rows("x3", x3, i - 16)
                    if i == 18:
                        pe.wait_ge(wide_kept["h1"], J + 2)
                        pe.wait_ge(ready["h1"], J + 1)
                    if i in (18, 19):
                        rows("h2", h1t, w2_s, i - 18)

                def one(pair, odd, job, norm):
                    with pe.Fori(0, NBB) as b:
                        for i in range(RB):
                            slots(pair, odd, b, i, job)

                passes(pe, one)

            @block.scalar
            def _(act):
                def slots(pair, odd, b, i):
                    turn = pair * (2 * NBB) + b + odd * NBB
                    act.wait_ge(rows_in[i], turn * 16 + 16)
                    if i:
                        act.wait_ge(summed, turn * RB + i)
                    nc.scalar.copy(g[0:1, i, :], ps[(i - 1) % BANKS][0:1, 0:D] if i else hold[:]).then_inc(carried, 1)

                def nodes(J, i):
                    if i in (4, 8, 13):
                        k = (4, 8, 13).index(i)
                        act.wait_ge(var_ready[k], J + 1)
                        nc.scalar.activation(rstd[:, k, :], var[:, k, :], ACT.Sqrt).then_inc(rstd_ready[k], 1)
                    elif i in (12, 18):
                        name, to = ("x2", x2t) if i == 12 else ("x3", x3t)
                        act.wait_ge(turned[name], J + 1)
                        nc.scalar.copy(to[0:D, :], ps_a[0:D, 0:W]).then_inc(turned_kept[name], 1)
                    elif i in (2, 16):
                        name, to = ("h1", h1t) if i == 16 else ("h2", h2t)
                        act.wait_ge(wide[name], J + 1)
                        nc.scalar.activation(to[0:D, :], ps_b[0:D, 0:W], ACT.Relu).then_inc(wide_kept[name], 1)

                def root(chunk):
                    if chunk:
                        act.wait_ge(f_var_ready, chunk[1] + 1)
                        nc.scalar.activation(f_rstd[:, chunk[2], :], f_var[:, chunk[2], :], ACT.Sqrt).then_inc(f_rstd_ready, 1)

                def scale(chunk, tiles):
                    if chunk:
                        act.wait_ge(f_normed, chunk[1] + 1)
                        for j in tiles:
                            t = ds(chunk[0] + j, 1)
                            k = nc.scalar.activation(state[:, t, :], fixed[:, t, :], ACT.Copy, scale=dis_c[:, t])
                        if j == CH - 1:
                            k.then_inc(f_scaled, 1)

                def one(pair, odd, job, norm):
                    def body(b):
                        for i in range(RB):
                            slots(pair, odd, b, i)
                            if job:
                                nodes(pair * (2 * NBB) + b + odd * NBB, i)
                            if norm and i % CH == 0:
                                root(before(b, i // CH, 2))
                            if norm:
                                scale(before(b, i // CH, 4), (i % CH,))
                        act.wait_ge(summed, pair * (2 * T) + b * RB + (odd * T + RB))
                        nc.scalar.copy(hold[:], ps[(RB - 1) % BANKS][0:1, 0:D]).then_inc(carried, 1)
                        act.wait_ge(carried, (pair * (2 * NBB) + b + (odd * NBB + 1)) * CARRIES)

                    bodies(act, norm, body)

                passes(act, one)
                for q in range(2):
                    root(before(NBB, q, 2))
                for q in range(4):
                    scale(before(NBB, q, 4), range(CH))

            @block.vector
            def _(dve):
                def slots(pair, odd, b, i):
                    t, turn = ds(b * RB + i, 1), pair * (2 * NBB) + b + odd * NBB
                    dve.wait_ge(carried, turn * CARRIES + (i + 2))
                    nc.vector.scalar_tensor_tensor(out=state[:, t, :], in0=ps[i % BANKS][:, 0:D].rearrange("p (a d) -> p a d", a=1),
                                                   scalar=step_a[:, t], in1=fixed[:, t, :], op0=ALU.mult, op1=ALU.add).then_inc(freed, 1)

                def moments(k, done, of, eps):
                    row_moments(dve, done, [of[:, j, :] for j in range(JW)], stats, mv[:, k])
                    done.up(nc.vector.tensor_scalar(var[:, k, :], mv[:, k, :, 1], eps, None, ALU.add))
                    dve.wait_ge(steps, done.now())
                    nc.vector.reciprocal(var[:, k, :], var[:, k, :]).then_inc(var_ready[k], 1)

                def normed(J, k, frm, to, name):
                    dve.wait_ge(outs[name], J * 16 + 16)
                    dve.wait_ge(rstd_ready[k], J + 1)
                    for j in range(JW):
                        m = nc.vector.tensor_scalar(to[:, j, :], frm[:, j, :], mv[:, k, j, 0:1], rstd[:, k, j:j + 1], ALU.subtract, ALU.mult)
                    m.then_inc(ready[name], 1)

                def rectified(J, to, name):
                    dve.wait_ge(outs[name], J * 16 + 16)
                    dve.wait_ge(narrow[name], J + 1)
                    nc.vector.tensor_scalar(cols(to[:]), ps_c[:, 0:JW * D], 0.0, None, ALU.max).then_inc(ready[name], 1)

                def residual(J, k, x_, to, name, done):
                    dve.wait_ge(narrow[name], J + 1)
                    nc.vector.tensor_tensor(cols(to[:]), cols(x_[:]), ps_c[:, 0:JW * D], ALU.add).then_inc(added, 1)
                    dve.wait_ge(added, J * 2 + k)
                    done.up(dve)
                    moments(k, done, to, EPS)

                per_job = 3 * (2 * JW + 2) + 2

                def nodes(J, i, done):
                    if i == 0:
                        dve.wait_ge(x1_in, J * 16 + 16)
                        moments(0, done, x1, EPS / 4)
                    elif i == 4:
                        residual(J, 1, x2, y3, "y3", done)
                    elif i == 5:
                        normed(J, 0, x1, x2, "x2")
                    elif i == 9:
                        residual(J, 2, x3, y4, "y4", done)
                    elif i == 10:
                        normed(J, 1, y3, x3, "x3")
                    elif i == 13:
                        normed(J, 2, y4, res, "res")
                    elif i == 14:
                        rectified(J, h1, "h1")
                    elif i == 19:
                        rectified(J, h2, "h2")

                per_chunk = 1 + 2 * CH + 1 + 3

                def chunk_moments(chunk, part):
                    if not chunk:
                        return
                    t, h = ds(chunk[0], CH), chunk[2]
                    done = Count(f_steps, chunk[1], per_chunk)
                    done.n = (0, 1, 1 + CH, 2 + 2 * CH, 4 + 2 * CH)[part]
                    if part:
                        dve.wait_ge(f_steps, done.now())
                    if part == 0:
                        dve.wait_ge(freed, chunk[0] + (CH + (STEPS - 1) * T + RB))
                        done.up(nc.vector.scalar_tensor_tensor(out=cols(f_y[:, h]), in0=cols(fixed[:, t, :]), scalar=1.0 / ALPHA,
                                                               in1=cols(state[:, t, :]), op0=ALU.mult, op1=ALU.add))
                    elif part == 1:
                        for j in range(CH):
                            done.up(dve.bn_stats(f_stats[:, h, j, :], f_y[:, h, j, :]))
                    elif part == 2:
                        done.up(dve)
                        for j in range(CH):
                            done.up(dve.bn_aggr(f_mv[:, h, j, :], f_stats[:, h, j, :]))
                    elif part == 3:
                        done.up(nc.vector.tensor_tensor(f_var[:, h, :], f_mv[:, h, :, 1], cnt[:, t], ALU.mult))
                        dve.wait_ge(f_steps, done.now())
                        done.up(nc.vector.tensor_scalar(f_var[:, h, :], f_var[:, h, :], EPS, None, ALU.add))
                    else:
                        done.up(nc.vector.reciprocal(f_var[:, h, :], f_var[:, h, :]))
                        dve.wait_ge(f_steps, done.now())
                        assert done.n == per_chunk, done.n
                        nc.vector.tensor_tensor(f_var[:, h, :], f_var[:, h, :], cnt[:, t], ALU.mult).then_inc(f_var_ready, 1)

                def chunk_normed(chunk):
                    if chunk:
                        h = chunk[2]
                        dve.wait_ge(f_rstd_ready, chunk[1] + 1)
                        for j in range(CH):
                            k = nc.vector.tensor_scalar(fixed[:, ds(chunk[0] + j, 1), :], f_y[:, h, j:j + 1, :], f_mv[:, h, j, 0:1],
                                                        f_rstd[:, h, j:j + 1], ALU.subtract, ALU.mult)
                        k.then_inc(f_normed, 1)
                        dve.wait_ge(f_normed, chunk[1] + 1)

                def one(pair, odd, job, norm):
                    def body(b):
                        J = pair * (2 * NBB) + b + odd * NBB
                        done = Count(steps, J, per_job)
                        for i in range(RB):
                            slots(pair, odd, b, i)
                            if i % CH == CH - 1:
                                nc.vector.tensor_copy(idx[:, i // CH, :], ptr[:, ds((b + 1) * RB + (odd * T + i + 1 - CH), CH)]).then_inc(staged, 1)
                            if job:
                                nodes(J, i, done)
                            if norm and i % CH == CH - 1:
                                chunk_normed(before(b, i // CH, 2))
                                chunk_moments(before(b, i // CH, 0), 0)
                            elif norm:
                                chunk_moments(before(b, i // CH, 1), i % CH + 1)
                        assert not job or done.n == per_job, done.n

                    bodies(dve, norm, body)

                passes(dve, one)
                for part in range(1, 5):
                    chunk_moments(before(NBB, 0, 1), part)
                for q in range(2):
                    chunk_normed(before(NBB, q, 2))


def convolution(nc, layer, state, fixed, ident, ptr, w_s, dis_w, dis_c, scat, w, wa, tab, sums, tab_next, out):
    inner, final = layer < 4, layer == 5
    later = layer == 4
    with ExitStack() as c:
        sem = c.enter_context(semaphores(nc))
        def sb(name, shape, dt=F32):
            return c.enter_context(nc.sbuf_tensor(f"c{layer}_{name}", shape, dt))

        def s(name):
            return sem(f"c{layer}_{name}")

        w_in = sb("w", [D, D])
        bias = sb("bias", [P, D])
        wa_in = sb("wa", [D + 1, D])
        g = sb("g", [P, R, D])
        gw = sb("gw", [P, R, D])
        s_in = sb("s", [P, 2, CH * P])
        idx = sb("idx", [P, 2, CH], I32)
        scat_idx = sb("scat_idx", [P, 2, CH], I32)
        at = sb("at", [D, 2, P])
        own = sb("own", [P, 2, D])
        own_t = sb("own_t", [D + 1, 2, P])
        y = sb("y", [P, 2, CH, D])
        tmp = sb("tmp", [P, 2, D])
        prime = sb("prime", [1, 2, 8])
        res = sb("res", [P, 2, CH, D])
        stats, mv = sb("stats", [P, CH, 6]), sb("mv", [P, 2, CH, 2])
        var, rstd = sb("var", [P, 2, CH]), sb("rstd", [P, 2, CH])
        ps_t = [c.enter_context(nc.psum_tensor(f"c{layer}_ps_t{k}", [P, 512], F32)) for k in range(2)]
        ps_w = [c.enter_context(nc.psum_tensor(f"c{layer}_ps_w{k}", [P, 512], F32)) for k in range(2)]
        pc = [c.enter_context(nc.psum_tensor(f"c{layer}_pc{k}", [P, 512], F32)) for k in range(2)]
        ps_o = [c.enter_context(nc.psum_tensor(f"c{layer}_ps_o{k}", [P, 512], F32)) for k in range(2)]
        const_in = s("const_in")
        rows_in = [s(f"rows_in{i}") for i in range(R)]
        s_landed = [s(f"s_in{h}") for h in range(2)]
        staged, go = s("staged"), s("go")
        weighted, carry_out, carry_kept = s("weighted"), s("carry_out"), s("carry_kept")
        summed, sum_kept, own_kept, own_turned, own_t_kept = s("summed"), s("sum_kept"), s("own_kept"), s("own_turned"), s("own_t_kept")
        mapped, posted, steps = s("mapped"), s("posted"), s("steps")
        var_ready, rstd_ready, written = s("var_ready"), s("rstd_ready"), s("written")
        scat_staged = s("scat_staged")
        scattered = [s(f"scattered{h}") for h in range(2)]
        freed, chunk_done = s("freed"), s("chunk_done")

        with nc.Block() as block:
            @block.sync
            def _(sp):
                sp.dma_start(w_in[:], w[0:D, :]).then_inc(const_in, 16)
                if final:
                    sp.dma_start(wa_in[:], wa).then_inc(const_in, 16)
                else:
                    sp.dma_start(bias[:], w[D:D + 1, :].broadcast_to([P, D])).then_inc(const_in, 16)
                sp.wait_ge(const_in, 32)

            if final:
                @block.gpsimd
                def _(pool):
                    for h in range(2):
                        pool.dma_start(prime[:, h], w[0:1, 0:8]).then_inc(scattered[h], 16)
                        pool.wait_ge(scattered[h], 16)

            @block.vector
            def _(dve):
                nc.vector.tensor_copy(idx[:].rearrange("p h c -> p (h c)"), ptr[:, 0:R]).then_inc(staged, 2)
                nc.vector.memset(pc[1][0:1, :], 0.0)
                nc.vector.memset(own_t[D:D + 1, :, :], 1.0)
                dve.sem_inc(freed, 2)
                dve.sem_inc(carry_out, 1)

        with nc.Block() as block:
            @block.sync
            def _(sp):
                def load_s(cc, h):
                    sp.dma_start(s_in[:, h, :], sums[:, ds(cc * (CH * P), CH * P)]).then_inc(s_landed[h], 16)

                for h in range(2):
                    load_s(h, h)
                with sp.Fori(0, NB) as b:
                    for h in range(2):
                        t = ds(b * R + CH * h, CH)
                        sp.wait_ge(summed, b * R + CH * (h + 1))
                        load_s(2 * b + 2 + h, h)
                        if not final:
                            sp.wait_ge(chunk_done, 2 * b + (h + 1))
                            sp.dma_start(tab_next[:, t, :], state[:, t, :]).then_inc(written, 16)
                if not final:
                    sp.wait_ge(written, 32 * NB)
                for h in range(2):
                    sp.wait_ge(s_landed[h], 16 * (NB + 1))

            @block.gpsimd
            def _(pool):
                def scatter(b, h):
                    pool.wait_ge(scattered[h], b * (16 * CH) + 16)
                    nc.gpsimd.tensor_copy(scat_idx[:, h, :], scat[:, ds(b * R + h * CH, CH)]).then_inc(scat_staged, 1)
                    pool.wait_ge(scat_staged, 2 * b + h + 1)
                    pool.wait_ge(chunk_done, 2 * b + (h + 1))
                    pool.sem_inc(go, 1)
                    for j in range(CH):
                        nc.gpsimd.indirect_dma_start(out, bass.IndirectOffsetOnAxis(ap=scat_idx[:, h, j:j + 1], axis=0), res[:, h, j, :], None,
                                                     bounds_check=N - 1, oob_is_err=False).then_inc(scattered[h], 16)

                def gather(b, h, first):
                    if not first:
                        pool.wait_ge(weighted, b * R + (h - 1) * CH)
                    pool.wait_ge(staged, b * 2 + (h + 1))
                    pool.sem_inc(go, 1)
                    for j in range(CH):
                        nc.gpsimd.indirect_dma_start(g[:, h * CH + j, :], None, tab,
                                                     bass.IndirectOffsetOnAxis(ap=idx[:, h, j:j + 1], axis=0)).then_inc(rows_in[h * CH + j], 16)

                for h in range(2):
                    gather(0, h, True)
                with pool.Fori(1, NB) as b:
                    for h in range(2):
                        gather(b, h, False)
                        if final:
                            scatter(b - 1, h)
                if final:
                    for h in range(2):
                        scatter(NB - 1, h)
                    for h in range(2):
                        pool.wait_ge(scattered[h], 16 * CH * NB + 16)

            @block.tensor
            def _(pe):
                def total(b, i):
                    h, j, n = i // CH, i % CH, b * R + i
                    if j == 0:
                        pe.wait_ge(s_landed[h], b * 16 + 16)
                    if final:
                        pe.wait_ge(own_kept, n + 1)
                        nc.tensor.transpose(ps_o[i % 2][0:D, 0:P], own[:, i % 2, :], ident[:]).then_inc(own_turned, 1)
                    m = s_in[:, h, j * P:(j + 1) * P]
                    pe.wait_ge(carry_kept, n + 1)
                    nc.tensor.matmul(pc[i % 2][0:1, 0:D], m[:, 0:1], gw[:, i, :], start=True, stop=True).then_inc(carry_out, 1)
                    if i > 1:
                        pe.wait_ge(sum_kept, n - 1)
                    nc.tensor.matmul(ps_t[i % 2][0:D, 0:P], gw[:, i, :], m, start=True, stop=True).then_inc(summed, 1)

                def linear(b, i):
                    n = b * R + i
                    pe.wait_ge(freed, n + 1)
                    pe.wait_ge(sum_kept, n + 1)
                    if final:
                        pe.wait_ge(own_t_kept, n + 1)
                        nc.tensor.matmul(ps_w[i % 2][:, 0:D], own_t[:, i % 2, :], wa_in[:], start=True, stop=False)
                    nc.tensor.matmul(ps_w[i % 2][:, 0:D], at[:, i % 2, :], w_in[:], start=not final, stop=True).then_inc(mapped, 1)

                with pe.Fori(0, NB) as b:
                    for i in range(R):
                        total(b, i)
                        if i:
                            linear(b, i - 1)
                    linear(b, R - 1)

            @block.scalar
            def _(act):
                def keep(b, i):
                    n = b * R + i
                    if i > 1:
                        act.wait_ge(mapped, n - 1)
                    act.wait_ge(summed, n + 1)
                    nc.scalar.copy(at[:, i % 2, :], ps_t[i % 2][0:D, 0:P]).then_inc(sum_kept, 1)
                    if final:
                        act.wait_ge(own_turned, n + 1)
                        nc.scalar.copy(own_t[0:D, i % 2, :], ps_o[i % 2][0:D, 0:P]).then_inc(own_t_kept, 1)

                def root(b, h):
                    act.wait_ge(var_ready, 2 * b + h + 1)
                    nc.scalar.activation(rstd[:, h, :], var[:, h, :], ACT.Sqrt).then_inc(rstd_ready, 1)

                def turn(b, first):
                    for i in range(R):
                        n = b * R + i
                        if final:
                            if i > 1:
                                act.wait_ge(own_turned, n - 1)
                            nc.scalar.copy(own[:, i % 2, :], cols(state[:, ds(n, 1), :])).then_inc(own_kept, 1)
                        act.wait_ge(weighted, n + 1)
                        act.wait_ge(carry_out, n + 1)
                        nc.scalar.copy(gw[0:1, i, :], pc[(i - 1) % 2][0:1, 0:D]).then_inc(carry_kept, 1)
                        if i:
                            keep(b, i - 1)
                        if later and i == 2 and not first:
                            root(b - 1, 1)
                        if later and i == CH + 2 or final and i == CH:
                            root(b, 0)
                    keep(b, R - 1)
                    if final:
                        root(b, 1)

                if later:
                    turn(0, True)
                with act.Fori(1 if later else 0, NB) as b:
                    turn(b, False)
                if later:
                    root(NB - 1, 1)

            @block.vector
            def _(dve):
                def weigh(b, i):
                    n = b * R + i
                    dve.wait_ge(rows_in[i], b * 16 + 16)
                    if final:
                        k = nc.vector.tensor_scalar(gw[:, i:i + 1, :], g[:, i:i + 1, :], w_s[:, ds(n, 1)], None, ALU.mult)
                    else:
                        k = nc.vector.scalar_tensor_tensor(out=gw[:, i:i + 1, :], in0=g[:, i:i + 1, :], scalar=w_s[:, ds(n, 1)],
                                                           in1=state[:, ds(n, 1), :], op0=ALU.mult, op1=ALU.add)
                    k.then_inc(weighted, 1)
                    if i % CH == CH - 1:
                        nc.vector.tensor_copy(idx[:, i // CH, :], ptr[:, ds(n + 1 + CH, CH)]).then_inc(staged, 1)

                def take(b, i, done):
                    h, j, n = i // CH, i % CH, b * R + i
                    t = ds(n, 1)
                    got = ps_w[i % 2][:, 0:D].rearrange("p (a d) -> p a d", a=1)
                    dve.wait_ge(mapped, n + 1)
                    if final:
                        nc.vector.tensor_tensor(y[:, h, j:j + 1, :], got, state[:, t, :], ALU.add).then_inc(freed, 1)
                        return
                    nc.vector.scalar_tensor_tensor(out=tmp[:, i % 2:i % 2 + 1, :], in0=got, scalar=dis_w[:, t],
                                                   in1=bias[:].rearrange("p (a d) -> p a d", a=1), op0=ALU.mult, op1=ALU.add).then_inc(freed, 1)
                    dve.wait_ge(freed, n + 3)
                    if inner:
                        k = nc.vector.tensor_scalar(state[:, t, :], tmp[:, i % 2:i % 2 + 1, :], 0.0, dis_c[:, t], ALU.max, ALU.mult)
                        if j == CH - 1:
                            k.then_inc(chunk_done, 1)
                    else:
                        done.up(nc.vector.tensor_tensor(y[:, h, j:j + 1, :], tmp[:, i % 2:i % 2 + 1, :], fixed[:, t, :], ALU.add))

                def moments(b, h, done):
                    if final:
                        dve.wait_ge(freed, b * R + (h + 1) * CH + 2)
                    else:
                        dve.wait_ge(steps, done.now())
                    row_moments(dve, done, [y[:, h, j, :] for j in range(CH)], stats, mv[:, h])
                    done.up(nc.vector.tensor_scalar(var[:, h, :], mv[:, h, :, 1], EPS, None, ALU.add))
                    dve.wait_ge(steps, done.now())
                    nc.vector.reciprocal(var[:, h, :], var[:, h, :]).then_inc(var_ready, 1)

                def normed(b, h):
                    if final:
                        dve.wait_ge(scattered[h], b * (16 * CH) + 16)
                    dve.wait_ge(rstd_ready, 2 * b + h + 1)
                    for j in range(CH):
                        to = res[:, h, j:j + 1, :] if final else state[:, ds(b * R + h * CH + j, 1), :]
                        k = nc.vector.tensor_scalar(to, y[:, h, j:j + 1, :], mv[:, h, j, 0:1], rstd[:, h, j:j + 1], ALU.subtract, ALU.mult)
                    k.then_inc(chunk_done, 1)
                    dve.wait_ge(chunk_done, 2 * b + h + 1)

                per_turn = 0 if inner else 2 * ((0 if final else CH) + 2 * CH + 2)

                def turn(b, first, last):
                    done = Count(steps, b, per_turn)
                    for h in range(2):
                        for j in range(CH):
                            if h == 0:
                                weigh(b, CH + j)
                            elif not last:
                                weigh(b + 1, j)
                            take(b, h * CH + j, done)
                        if later and not (first and h == 0):
                            normed(*((b, 0) if h else (b - 1, 1)))
                        if not inner:
                            moments(b, h, done)
                        if final:
                            normed(b, h)
                    assert done.n == per_turn, (done.n, per_turn)

                for j in range(CH):
                    weigh(0, j)
                if later:
                    turn(0, True, False)
                with dve.Fori(1 if later else 0, NB - 1) as b:
                    turn(b, False, False)
                turn(NB - 1, False, True)
                if later:
                    normed(NB - 1, 1)


def lay_out(src, dst, edge_attr, edge_weight, x, Wq, bq, Wk, bk, We, be, Wv, bv, W1, b1, W2, b2, W3, b3, mlp_w, mlp_b):
    import numpy as np

    def grid(a, fill):
        g = np.full((T * RE,), fill, a.dtype)
        g[:E] = a
        return g.reshape(T, RE)

    def with_first(first, rest):
        return np.concatenate([first[:, None], rest], axis=1)

    def again(a):
        return np.concatenate([a, a[:R]], axis=0)

    d = grid(dst, N)
    last = d[:, -1]
    before = np.concatenate([np.full((1,), -1, dst.dtype), last[:-1]])
    following = np.concatenate([d.reshape(-1)[1:], np.full((1,), N, dst.dtype)]).reshape(T, RE)
    zero_i, zero_f = np.zeros((T,), src.dtype), np.zeros((T,), edge_weight.dtype)
    ea = np.zeros((T, P, D), edge_attr.dtype)
    ea.reshape(T, P, D)[:, 1:, :] = np.concatenate([edge_attr, np.zeros((T * RE - E, D), edge_attr.dtype)]).reshape(T, RE, D)

    def t_(a):
        return np.ascontiguousarray(a.T)

    def biased(w, b):
        return np.concatenate([w, b[None, :]], axis=0)

    return {
        "x": np.concatenate([x, np.zeros((NN - N, D), x.dtype)]),
        "src_p": t_(with_first(zero_i, grid(src, 0))),
        "dst_k": t_(again(with_first(before, d))),
        "dst_next": t_(with_first(before, following)),
        "dst_i": again(with_first(last, d)).reshape(-1),
        "w_p": t_(with_first(zero_f, grid(edge_weight, 0))),
        "ea_t": t_(np.concatenate([ea.reshape(T * P, D), np.zeros((CH * P, D), ea.dtype)])),
        "wkv": np.concatenate([biased(Wk, bk), biased(Wv, bv)], axis=1),
        "wq": biased(Wq, bq),
        "we": biased(We, be),
        "w1": biased(W1, b1),
        "w2": biased(W2, b2),
        "w3": biased(W3, b3),
        "wa": biased(np.ascontiguousarray(mlp_w[:, :D].T), mlp_b),
        "wb": np.ascontiguousarray(mlp_w[:, D:].T),
    }


def kernel(x, src, dst, edge_attr_96, edge_weight, L0_gnn_Wq, L0_gnn_bq, L0_gnn_Wk, L0_gnn_bk, L0_gnn_We, L0_gnn_be,
           L0_gnn_Wv, L0_gnn_bv, L2_gnn_W1, L2_gnn_b1, L2_gnn_W2, L2_gnn_b2, L2_gnn_W3, L2_gnn_b3, L3_gnn_mlp_w, L3_gnn_mlp_b):
    import numpy as np
    import concourse.bacc as bacc
    from concourse.bass_utils import run_bass_kernel_spmd

    given = [np.asarray(a) for a in (src, dst, edge_attr_96, edge_weight, x, L0_gnn_Wq, L0_gnn_bq, L0_gnn_Wk, L0_gnn_bk, L0_gnn_We,
                                     L0_gnn_be, L0_gnn_Wv, L0_gnn_bv, L2_gnn_W1, L2_gnn_b1, L2_gnn_W2, L2_gnn_b2, L2_gnn_W3,
                                     L2_gnn_b3, L3_gnn_mlp_w, L3_gnn_mlp_b)]
    nc = bacc.Bacc("TRN2", target_bir_lowering=False, num_devices=1)
    arrays, args = {}, {}
    for name, a in lay_out(*given).items():
        a = np.ascontiguousarray(a)
        arrays[f"in_{name}"] = a
        args[name] = nc.dram_tensor(f"in_{name}", a.shape, mybir.dt.from_np(a.dtype), kind="ExternalInput").ap()
    args["out"] = nc.dram_tensor("out_nodes", [NN, D], F32, kind="ExternalOutput").ap()

    def scratch(name, shape, dt):
        return nc.dram_tensor(name, shape, dt, kind="Internal").ap()

    build_graph_kernel(nc, scratch, **args)
    r = run_bass_kernel_spmd(nc, [arrays], core_ids=[0])
    return r.results[0]["out_nodes"][:N]
```
